# Optimizing a Trainium2 kernel written in Bass

```python
import numpy as np
import jax
import jax.numpy as jnp

def _softmax(x, axis=-1):
    return jax.nn.softmax(x, axis=axis)

def _gelu(x):
    return jax.nn.gelu(x, approximate=True)

def _silu(x):
    return jax.nn.silu(x)

def _sigmoid(x):
    return jax.nn.sigmoid(x)

def _layernorm(x, axis=-1, eps=1e-05):
    m = jnp.mean(x, axis=axis, keepdims=True)
    v = jnp.var(x, axis=axis, keepdims=True)
    return (x - m) / jnp.sqrt(v + eps)

def _scatter_add(tgt, idx, src, axis=0):
    return tgt.at[idx].add(src)

def _segment_sum(src, seg, n):
    return jax.ops.segment_sum(src, seg, n)
kernel_name = 'mk_xattn_ffn_d2_seqx_r4_8ca3ec'

def setup_inputs(seed: int=0):
    np.random.seed(seed)
    _w = jnp.asarray

    def _rec_inputs():
        import jax
        import jax.numpy as jnp
        _rk = jax.random.key(seed)
        x = -0.0002928 + 1 * jax.random.normal(jax.random.fold_in(_rk, 1), (64, 128, 256), jnp.float32)
        _lenS = 128 - jax.random.randint(jax.random.fold_in(_rk, 7), (64,), 0, max(1, 128 // 4) + 1, jnp.int32)
        _lenS2 = 128 - jax.random.randint(jax.random.fold_in(_rk, 8), (64,), 0, max(1, 128 // 4) + 1, jnp.int32)
        _ctx_1024P = jax.random.normal(jax.random.fold_in(_rk, 11), (64, 16, 256), jnp.float32)
        _ctx_1024c = jax.random.dirichlet(jax.random.fold_in(_rk, 511), 0.3 * jnp.ones((16,), jnp.float32), (64, 128))
        _ctx_1024t = jnp.einsum('bsk,bkd->bsd', _ctx_1024c, _ctx_1024P)
        _ctx_1024t = _ctx_1024t * jax.lax.rsqrt(jnp.mean(jnp.square(_ctx_1024t)) + 1e-12) * 0.953939
        ctx_1024 = -1.39393e-06 + 0.999914 * (_ctx_1024t + 0.3 * jax.random.normal(jax.random.fold_in(_rk, 611), (64, 128, 256), jnp.float32))
        return (x, ctx_1024)
    x, ctx_1024 = _rec_inputs()

    def _L0_xattn_setup():
        import jax, jax.numpy as jnp
        import numpy as np
        EMBED_DIM = 256
        NUM_HEADS = 16
        HEAD_DIM = EMBED_DIM // NUM_HEADS
        SEG_LENS = [256, 512, 1024]
        DIL_RATIOS = [1, 2, 4]
        NEG = -100000000.0

        def _branch(q, k, v, sl, dr, L):
            B = q.shape[0]
            H, D = (NUM_HEADS, HEAD_DIM)
            sl = min(sl, L)
            pad = -L % sl
            if pad:
                pw = ((0, 0), (0, pad), (0, 0), (0, 0))
                q, k, v = (jnp.pad(q, pw), jnp.pad(k, pw), jnp.pad(v, pw))
            n = (L + pad) // sl
            qs = q.reshape(B * n, sl, H, D)
            ks = k.reshape(B * n, sl, H, D)
            vs = v.reshape(B * n, sl, H, D)
            hg = H // dr
            g = sl // dr
            grp = jnp.arange(H) // hg
            pos = jnp.arange(g)[:, None] * dr + grp[None]
            hidx = jnp.arange(H)[None, :]
            sp = lambda x: x[:, pos, hidx, :]
            qd, kd, vd = (sp(qs), sp(ks), sp(vs))
            scores = jnp.einsum('bqhd,bkhd->bhqk', qd, kd) * D ** (-0.5)
            mask = jnp.tril(jnp.ones((g, g), bool))
            scores = jnp.where(mask, scores, -jnp.inf)
            lse = jax.nn.logsumexp(scores, axis=-1)
            o = jnp.einsum('bhqk,bkhd->bqhd', jnp.exp(scores - lse[..., None]), vd)
            hcol = jnp.arange(H)[:, None]
            od = jnp.zeros((B * n, H, sl, D), o.dtype).at[:, hcol, pos.T].set(o.transpose(0, 2, 1, 3))
            ld = jnp.zeros((B * n, H, sl), lse.dtype).at[:, hcol, pos.T].set(lse)
            ld = jnp.where(ld == 0.0, NEG, ld)
            od = od.reshape(B, n, H, sl, D).transpose(0, 2, 1, 3, 4)
            od = od.reshape(B, H, n * sl, D)[:, :, :L]
            ld = ld.reshape(B, n, H, sl).transpose(0, 2, 1, 3).reshape(B, H, n * sl)[:, :, :L]
            return (od, ld)
        root = jax.random.key(seed)
        ks = jax.random.split(root, 12)
        B, L, E = (1, 1024, EMBED_DIM)
        s = 0.02
        return {'query': jax.random.normal(ks[0], (B, L, E), jnp.float32), 'key': jax.random.normal(ks[1], (B, L, E), jnp.float32), 'value': jax.random.normal(ks[2], (B, L, E), jnp.float32), 'Wq': jax.random.normal(ks[3], (E, E), jnp.float32) * s, 'bq': jnp.zeros((E,), jnp.float32), 'Wk': jax.random.normal(ks[4], (E, E), jnp.float32) * s, 'bk': jnp.zeros((E,), jnp.float32), 'Wv': jax.random.normal(ks[5], (E, E), jnp.float32) * s, 'bv': jnp.zeros((E,), jnp.float32), 'Wo': jax.random.normal(ks[6], (E, E), jnp.float32) * s, 'bo': jnp.zeros((E,), jnp.float32)}
    _L0_xattn_all = _L0_xattn_setup()
    _L0_xattn_in = {k: v for k, v in _L0_xattn_all.items() if k in ('Wq', 'bq', 'Wk', 'bk', 'Wv', 'bv', 'Wo', 'bo')}
    del _L0_xattn_all

    def _L0_ffn_setup():
        import jax, jax.numpy as jnp
        import numpy as np
        B, T, C = (4, 512, 256)
        H = 128
        E_ATT = 8
        E_MOE = 8
        I = 256
        MIN_ATT = 2
        MIN_MOE = 2
        EPS_LN = 1e-05

        def _normalize(x, axis):
            n = jnp.linalg.norm(x, axis=axis, keepdims=True)
            return x / jnp.maximum(n, 1e-12)

        def _layernorm(x, w, b):
            m = jnp.mean(x, axis=-1, keepdims=True)
            v = jnp.mean(jnp.square(x - m), axis=-1, keepdims=True)
            return (x - m) / jnp.sqrt(v + EPS_LN) * w + b

        def _gating(flat_hs, sim, gates, min_experts):
            logits = _normalize(flat_hs, -1) @ _normalize(sim, 0) - jax.nn.sigmoid(gates)
            gated = jax.nn.relu(logits)
            mask = (gated > 0).astype(gated.dtype)
            inactive = jnp.sum(mask, axis=1) == 0
            _, idx = jax.lax.top_k(logits, min_experts)
            onehot = jnp.sum(jax.nn.one_hot(idx, logits.shape[-1], dtype=gated.dtype), axis=1)
            put = inactive[:, None] & (onehot > 0)
            mask = jnp.where(put, 1.0, mask)
            masked = jnp.where(mask > 0, gated, -jnp.inf)
            return jax.nn.softmax(masked, axis=-1)
        key = jax.random.key(seed)
        ks = jax.random.split(key, 12)
        d = {}
        d['x'] = jax.random.normal(ks[0], (B, T, C), dtype=jnp.float32)
        d['ln1_w'] = jnp.ones((C,), jnp.float32)
        d['ln1_b'] = jnp.zeros((C,), jnp.float32)
        d['ln2_w'] = jnp.ones((C,), jnp.float32)
        d['ln2_b'] = jnp.zeros((C,), jnp.float32)
        d['smha_sim'] = jax.random.normal(ks[1], (C, E_ATT), dtype=jnp.float32)
        d['smha_gates'] = jnp.zeros((E_ATT,), jnp.float32)
        sq = 1.0 / np.sqrt(C + H)
        d['q_proj'] = jax.random.normal(ks[2], (E_ATT, C, H), dtype=jnp.float32) * sq
        d['k_proj'] = jax.random.normal(ks[3], (E_ATT, C, H), dtype=jnp.float32) * sq
        d['v_proj'] = jax.random.normal(ks[4], (E_ATT, C, H), dtype=jnp.float32) * sq
        d['o_proj'] = jax.random.normal(ks[5], (E_ATT, H, C), dtype=jnp.float32) * sq
        d['moe_sim'] = jax.random.normal(ks[6], (C, E_MOE), dtype=jnp.float32)
        d['moe_gates'] = jnp.zeros((E_MOE,), jnp.float32)
        d['w1'] = jax.random.normal(ks[7], (E_MOE, C, I), dtype=jnp.float32) * (1.0 / np.sqrt(C))
        d['w2'] = jax.random.normal(ks[8], (E_MOE, I, C), dtype=jnp.float32) * (1.0 / np.sqrt(I))
        return d
    _L0_ffn_all = _L0_ffn_setup()
    _L0_ffn_in = {k: v for k, v in _L0_ffn_all.items() if k in ('ln1_w', 'ln1_b', 'ln2_w', 'ln2_b', 'smha_sim', 'smha_gates', 'q_proj', 'k_proj', 'v_proj', 'o_proj', 'moe_sim', 'moe_gates', 'w1', 'w2')}
    del _L0_ffn_all

    def _L1_xattn_setup():
        import jax, jax.numpy as jnp
        import numpy as np
        from math import sqrt
        D_MODEL = 256
        N_HEADS = 16
        DK = D_MODEL // N_HEADS
        key = jax.random.key(seed)
        ks = jax.random.split(key, 11)
        B, L, S = (2, 512, 512)
        inp = {'queries': jax.random.normal(ks[0], (B, L, D_MODEL), jnp.float32), 'keys': jax.random.normal(ks[1], (B, S, D_MODEL), jnp.float32), 'values': jax.random.normal(ks[2], (B, S, D_MODEL), jnp.float32), 'Wq': jax.random.normal(ks[3], (D_MODEL, D_MODEL), jnp.float32) * 0.02, 'bq': jnp.zeros((D_MODEL,), jnp.float32), 'Wk': jax.random.normal(ks[4], (D_MODEL, D_MODEL), jnp.float32) * 0.02, 'bk': jnp.zeros((D_MODEL,), jnp.float32), 'Wv': jax.random.normal(ks[5], (D_MODEL, D_MODEL), jnp.float32) * 0.02, 'bv': jnp.zeros((D_MODEL,), jnp.float32), 'Wo': jax.random.normal(ks[6], (D_MODEL, D_MODEL), jnp.float32) * 0.02, 'bo': jnp.zeros((D_MODEL,), jnp.float32)}
        return inp
    _L1_xattn_all = _L1_xattn_setup()
    _L1_xattn_in = {k: v for k, v in _L1_xattn_all.items() if k in ('Wq', 'bq', 'Wk', 'bk', 'Wv', 'bv', 'Wo', 'bo')}
    del _L1_xattn_all

    def _L1_ffn_setup():
        import jax, jax.numpy as jnp
        import numpy as np
        B, S, D, E = (2, 512, 256, 8)
        key = jax.random.key(seed)
        ks = jax.random.split(key, 5)
        x = jax.random.normal(ks[0], (B, S, D), dtype=jnp.float32)
        router_w = jax.random.normal(ks[1], (E, D), dtype=jnp.float32) * 0.02
        router_b = jnp.zeros((E,), dtype=jnp.float32)
        expert_w = jax.random.normal(ks[2], (E, D, D), dtype=jnp.float32) * 0.02
        expert_b = jnp.zeros((E, D), dtype=jnp.float32)
        return {'x': x, 'router_w': router_w, 'router_b': router_b, 'expert_w': expert_w, 'expert_b': expert_b}
    _L1_ffn_all = _L1_ffn_setup()
    _L1_ffn_in = {k: v for k, v in _L1_ffn_all.items() if k in ('router_w', 'router_b', 'expert_w', 'expert_b')}
    del _L1_ffn_all
    return {'x': x, 'ctx_1024': ctx_1024, 'L0_xattn_Wq': _L0_xattn_in['Wq'], 'L0_xattn_bq': _L0_xattn_in['bq'], 'L0_xattn_Wk': _L0_xattn_in['Wk'], 'L0_xattn_bk': _L0_xattn_in['bk'], 'L0_xattn_Wv': _L0_xattn_in['Wv'], 'L0_xattn_bv': _L0_xattn_in['bv'], 'L0_xattn_Wo': _L0_xattn_in['Wo'], 'L0_xattn_bo': _L0_xattn_in['bo'], 'L0_ffn_ln1_w': _L0_ffn_in['ln1_w'], 'L0_ffn_ln1_b': _L0_ffn_in['ln1_b'], 'L0_ffn_ln2_w': _L0_ffn_in['ln2_w'], 'L0_ffn_ln2_b': _L0_ffn_in['ln2_b'], 'L0_ffn_smha_sim': _L0_ffn_in['smha_sim'], 'L0_ffn_smha_gates': _L0_ffn_in['smha_gates'], 'L0_ffn_q_proj': _L0_ffn_in['q_proj'], 'L0_ffn_k_proj': _L0_ffn_in['k_proj'], 'L0_ffn_v_proj': _L0_ffn_in['v_proj'], 'L0_ffn_o_proj': _L0_ffn_in['o_proj'], 'L0_ffn_moe_sim': _L0_ffn_in['moe_sim'], 'L0_ffn_moe_gates': _L0_ffn_in['moe_gates'], 'L0_ffn_w1': _L0_ffn_in['w1'], 'L0_ffn_w2': _L0_ffn_in['w2'], 'L1_xattn_Wq': _L1_xattn_in['Wq'], 'L1_xattn_bq': _L1_xattn_in['bq'], 'L1_xattn_Wk': _L1_xattn_in['Wk'], 'L1_xattn_bk': _L1_xattn_in['bk'], 'L1_xattn_Wv': _L1_xattn_in['Wv'], 'L1_xattn_bv': _L1_xattn_in['bv'], 'L1_xattn_Wo': _L1_xattn_in['Wo'], 'L1_xattn_bo': _L1_xattn_in['bo'], 'L1_ffn_router_w': _L1_ffn_in['router_w'], 'L1_ffn_router_b': _L1_ffn_in['router_b'], 'L1_ffn_expert_w': _L1_ffn_in['expert_w'], 'L1_ffn_expert_b': _L1_ffn_in['expert_b']}

def reference(x, ctx_1024, L0_xattn_Wq, L0_xattn_bq, L0_xattn_Wk, L0_xattn_bk, L0_xattn_Wv, L0_xattn_bv, L0_xattn_Wo, L0_xattn_bo, L0_ffn_ln1_w, L0_ffn_ln1_b, L0_ffn_ln2_w, L0_ffn_ln2_b, L0_ffn_smha_sim, L0_ffn_smha_gates, L0_ffn_q_proj, L0_ffn_k_proj, L0_ffn_v_proj, L0_ffn_o_proj, L0_ffn_moe_sim, L0_ffn_moe_gates, L0_ffn_w1, L0_ffn_w2, L1_xattn_Wq, L1_xattn_bq, L1_xattn_Wk, L1_xattn_bk, L1_xattn_Wv, L1_xattn_bv, L1_xattn_Wo, L1_xattn_bo, L1_ffn_router_w, L1_ffn_router_b, L1_ffn_expert_w, L1_ffn_expert_b):
    import jax
    import jax.numpy as jnp

    def _L0_xattn_ref(query, key, value, Wq, bq, Wk, bk, Wv, bv, Wo, bo):
        import jax, jax.numpy as jnp
        import numpy as np
        EMBED_DIM = 256
        NUM_HEADS = 16
        HEAD_DIM = EMBED_DIM // NUM_HEADS
        SEG_LENS = [256, 512, 1024]
        DIL_RATIOS = [1, 2, 4]
        NEG = -100000000.0

        def _branch(q, k, v, sl, dr, L):
            B = q.shape[0]
            H, D = (NUM_HEADS, HEAD_DIM)
            sl = min(sl, L)
            pad = -L % sl
            if pad:
                pw = ((0, 0), (0, pad), (0, 0), (0, 0))
                q, k, v = (jnp.pad(q, pw), jnp.pad(k, pw), jnp.pad(v, pw))
            n = (L + pad) // sl
            qs = q.reshape(B * n, sl, H, D)
            ks = k.reshape(B * n, sl, H, D)
            vs = v.reshape(B * n, sl, H, D)
            hg = H // dr
            g = sl // dr
            grp = jnp.arange(H) // hg
            pos = jnp.arange(g)[:, None] * dr + grp[None]
            hidx = jnp.arange(H)[None, :]
            sp = lambda x: x[:, pos, hidx, :]
            qd, kd, vd = (sp(qs), sp(ks), sp(vs))
            scores = jnp.einsum('bqhd,bkhd->bhqk', qd, kd) * D ** (-0.5)
            mask = jnp.tril(jnp.ones((g, g), bool))
            scores = jnp.where(mask, scores, -jnp.inf)
            lse = jax.nn.logsumexp(scores, axis=-1)
            o = jnp.einsum('bhqk,bkhd->bqhd', jnp.exp(scores - lse[..., None]), vd)
            hcol = jnp.arange(H)[:, None]
            od = jnp.zeros((B * n, H, sl, D), o.dtype).at[:, hcol, pos.T].set(o.transpose(0, 2, 1, 3))
            ld = jnp.zeros((B * n, H, sl), lse.dtype).at[:, hcol, pos.T].set(lse)
            ld = jnp.where(ld == 0.0, NEG, ld)
            od = od.reshape(B, n, H, sl, D).transpose(0, 2, 1, 3, 4)
            od = od.reshape(B, H, n * sl, D)[:, :, :L]
            ld = ld.reshape(B, n, H, sl).transpose(0, 2, 1, 3).reshape(B, H, n * sl)[:, :, :L]
            return (od, ld)
        B, L, E = query.shape
        H, D = (NUM_HEADS, HEAD_DIM)
        q = (query @ Wq.T + bq).reshape(B, L, H, D)
        k = (key @ Wk.T + bk).reshape(B, L, H, D)
        v = (value @ Wv.T + bv).reshape(B, L, H, D)
        outs, lses = ([], [])
        for sl, dr in zip(SEG_LENS, DIL_RATIOS):
            o, l = _branch(q, k, v, sl, dr, L)
            outs.append(o)
            lses.append(l)
        lse_all = jnp.stack(lses, 0)[..., None]
        m = lse_all.max(0)
        w = jnp.exp(lse_all - m)
        w = w / w.sum(0)
        w = jax.lax.stop_gradient(w)
        out = sum((o * wi.astype(o.dtype) for o, wi in zip(outs, w)))
        out = out.transpose(0, 2, 1, 3).reshape(B, L, E)
        return out @ Wo.T + bo

    def _L0_ffn_ref(x, ln1_w, ln1_b, ln2_w, ln2_b, smha_sim, smha_gates, q_proj, k_proj, v_proj, o_proj, moe_sim, moe_gates, w1, w2):
        import jax, jax.numpy as jnp
        import numpy as np
        B, T, C = (4, 512, 256)
        H = 128
        E_ATT = 8
        E_MOE = 8
        I = 256
        MIN_ATT = 2
        MIN_MOE = 2
        EPS_LN = 1e-05

        def _normalize(x, axis):
            n = jnp.linalg.norm(x, axis=axis, keepdims=True)
            return x / jnp.maximum(n, 1e-12)

        def _layernorm(x, w, b):
            m = jnp.mean(x, axis=-1, keepdims=True)
            v = jnp.mean(jnp.square(x - m), axis=-1, keepdims=True)
            return (x - m) / jnp.sqrt(v + EPS_LN) * w + b

        def _gating(flat_hs, sim, gates, min_experts):
            logits = _normalize(flat_hs, -1) @ _normalize(sim, 0) - jax.nn.sigmoid(gates)
            gated = jax.nn.relu(logits)
            mask = (gated > 0).astype(gated.dtype)
            inactive = jnp.sum(mask, axis=1) == 0
            _, idx = jax.lax.top_k(logits, min_experts)
            onehot = jnp.sum(jax.nn.one_hot(idx, logits.shape[-1], dtype=gated.dtype), axis=1)
            put = inactive[:, None] & (onehot > 0)
            mask = jnp.where(put, 1.0, mask)
            masked = jnp.where(mask > 0, gated, -jnp.inf)
            return jax.nn.softmax(masked, axis=-1)
        b, t, c = x.shape
        n1 = _layernorm(x, ln1_w, ln1_b)
        rw = _gating(n1.reshape(b * t, c), smha_sim, smha_gates, MIN_ATT).reshape(b, t, -1)
        q = jnp.einsum('btc,ech,bte->bth', n1, q_proj, rw)
        k = jnp.einsum('btc,ech,bte->bth', n1, k_proj, rw)
        v = jnp.einsum('btc,ech,bte->bth', n1, v_proj, rw)
        scale = 1.0 / jnp.sqrt(jnp.asarray(q.shape[-1], q.dtype))
        scores = jnp.einsum('bth,bsh->bts', q, k) * scale
        causal = jnp.tril(jnp.ones((t, t), dtype=bool))
        scores = jnp.where(causal, scores, -jnp.inf)
        attn = jnp.einsum('bts,bsh->bth', jax.nn.softmax(scores, axis=-1), v)
        attn_out = jnp.einsum('bth,ehc,bte->btc', attn, o_proj, rw)
        hs = x + attn_out
        n2 = _layernorm(hs, ln2_w, ln2_b)
        rw2 = _gating(n2.reshape(b * t, c), moe_sim, moe_gates, MIN_MOE).reshape(b, t, -1)
        inter = jax.nn.gelu(jnp.einsum('btc,eci->btei', n2, w1), approximate=False)
        moe_out = jnp.einsum('btei,eic,bte->btc', inter, w2, rw2)
        return hs + moe_out

    def _L1_xattn_ref(queries, keys, values, Wq, bq, Wk, bk, Wv, bv, Wo, bo):
        import jax, jax.numpy as jnp
        import numpy as np
        from math import sqrt
        D_MODEL = 256
        N_HEADS = 16
        DK = D_MODEL // N_HEADS
        B, L, _ = queries.shape
        S = values.shape[1]
        H, dk = (N_HEADS, DK)
        q = (queries @ Wq + bq).reshape(B, L, H, dk)
        k = (keys @ Wk + bk).reshape(B, S, H, dk)
        v = (values @ Wv + bv).reshape(B, S, H, dk)
        scale = 1.0 / sqrt(dk)
        scores = jnp.einsum('blhd,bshd->bhls', q, k)
        causal = jnp.triu(jnp.ones((L, S), dtype=bool), k=1)
        scores = jnp.where(causal[None, None], -jnp.inf, scores)
        attn = jax.nn.softmax(scores * scale, axis=-1)
        out = jnp.einsum('bhls,bshd->blhd', attn, v).reshape(B, L, H * dk)
        out = out @ Wo + bo
        return out

    def _L1_ffn_ref(x, router_w, router_b, expert_w, expert_b):
        import jax, jax.numpy as jnp
        import numpy as np
        B, S, D, E = (2, 512, 256, 8)
        logits = jnp.einsum('bsd,ed->bse', x, router_w) + router_b
        probs = jax.nn.softmax(logits, axis=-1)
        weights = jnp.max(probs, axis=-1)
        top1 = jnp.argmax(probs, axis=-1)
        y_all = jnp.einsum('bsd,eod->bseo', x, expert_w) + expert_b
        y = jnp.take_along_axis(y_all, top1[:, :, None, None], axis=2)[:, :, 0, :]
        out = y * weights[:, :, None]
        return out
    x = x + _L0_xattn_ref(_layernorm(x, axis=-1), ctx_1024, ctx_1024, L0_xattn_Wq, L0_xattn_bq, L0_xattn_Wk, L0_xattn_bk, L0_xattn_Wv, L0_xattn_bv, L0_xattn_Wo, L0_xattn_bo)
    x = x + _L0_ffn_ref(_layernorm(x, axis=-1), L0_ffn_ln1_w, L0_ffn_ln1_b, L0_ffn_ln2_w, L0_ffn_ln2_b, L0_ffn_smha_sim, L0_ffn_smha_gates, L0_ffn_q_proj, L0_ffn_k_proj, L0_ffn_v_proj, L0_ffn_o_proj, L0_ffn_moe_sim, L0_ffn_moe_gates, L0_ffn_w1, L0_ffn_w2)
    x = x + _L1_xattn_ref(_layernorm(x, axis=-1), ctx_1024, ctx_1024, L1_xattn_Wq, L1_xattn_bq, L1_xattn_Wk, L1_xattn_bk, L1_xattn_Wv, L1_xattn_bv, L1_xattn_Wo, L1_xattn_bo)
    x = x + _L1_ffn_ref(_layernorm(x, axis=-1), L1_ffn_router_w, L1_ffn_router_b, L1_ffn_expert_w, L1_ffn_expert_b)
    return x

_drawn_inputs = setup_inputs


def setup_inputs(seed=0):
    import zlib

    import numpy as np

    out = dict(_drawn_inputs(seed))
    spreads = {'L0_xattn_bq': (0.0, 0.8),
     'L0_xattn_bk': (0.0, 2.0),
     'L0_xattn_bv': (0.0, 0.1),
     'L0_xattn_bo': (0.0, 0.1),
     'L0_ffn_ln1_w': (1.0, 0.2),
     'L0_ffn_ln1_b': (0.0, 0.1),
     'L0_ffn_ln2_w': (1.0, 0.2),
     'L0_ffn_ln2_b': (0.0, 0.1),
     'L0_ffn_smha_gates': (0.0, 0.1),
     'L0_ffn_moe_gates': (0.0, 0.1),
     'L1_xattn_bq': (0.0, 2.0),
     'L1_xattn_bk': (0.0, 2.0),
     'L1_xattn_bv': (0.0, 0.488),
     'L1_xattn_bo': (0.0, 0.1),
     'L1_ffn_router_b': (0.0, 0.399),
     'L1_ffn_expert_b': (0.0, 0.8)}
    factors = {'L0_xattn_Wq': 4.76, 'L0_xattn_Wk': 4.835, 'L1_xattn_Wq': 8.0, 'L1_xattn_Wk': 8.0}
    for name, (base, spread) in spreads.items():
        noise = np.random.default_rng([zlib.crc32(name.encode()), seed]).standard_normal(out[name].shape)
        drawn = base * np.exp(spread * noise) if base else spread * noise
        out[name] = jnp.asarray(drawn.astype(out[name].dtype))
    for name, factor in factors.items():
        out[name] = (out[name] * factor).astype(out[name].dtype)
    return out
```

```python
from collections import namedtuple
from contextlib import ExitStack

import numpy as np

import concourse.bass as bass
from concourse import mybir

F32 = mybir.dt.float32
F32R = mybir.dt.float32r
BF16 = mybir.dt.bfloat16
ALU = mybir.AluOpType
ACT = mybir.ActivationFunctionType
AX = mybir.AxisListType

P = 128
C = 256
KT = C // P
H = 16
D = C // H
E = 8
HID = 128
UH = 4
UNITS = H // UH
LN_EPS = 1e-5
MASKED = -1e30


class Named:
    pass


def named(**values):
    return namedtuple("named", values)(*values.values())


def wait(eng, sem, value):
    if isinstance(value, int) and value <= 0:
        return
    eng.wait_ge(sem, value)


def is_(index, value):
    return isinstance(index, int) and index == value


def mm3(pe, out, left, right, first, last):
    pe.matmul(out, left[0], right[0], start=first, stop=False)
    pe.matmul(out, left[1], right[0], start=False, stop=False)
    return pe.matmul(out, left[0], right[1], start=False, stop=last)


def clear(nc, sems):
    with nc.Block() as block:
        @block.sync
        def _(sp):
            for sem in sems:
                sp.sem_clear(sem)


def host_constants():
    k = np.arange(P)
    causal = k[:, None] <= k[None, :]
    count = np.zeros((P, UNITS, P), np.float32)
    for j in range(UNITS):
        same2 = (k[:, None] % 2 == j // 2) & (k[None, :] % 2 == j // 2)
        same4 = (k[:, None] % 4 == j) & (k[None, :] % 4 == j)
        count[:, j, :] = causal * (1.0 + same2 + same4)
    plain = np.repeat(causal[:, None, :].astype(np.float32), UNITS, 1)
    hidden = np.where(causal.T, 0.0, MASKED).astype(np.float32)
    ones_half = np.zeros((P, 2, 32), np.float32)
    ones_half[:, 0, :D] = 1.0
    ones_half[:, 1, D:] = 1.0
    head_rows = (k[:, None] // D == np.arange(P // D)[None, :]) * np.float32(D ** -0.5)
    bf = np.dtype("bfloat16")
    return {
        "ident": np.eye(P, dtype=np.float32),
        "ident_bf": np.eye(P).astype(bf),
        "hidden_bf": np.tile(hidden, (1, UH)).astype(bf),
        "count_bf": count.astype(bf),
        "plain_bf": plain.astype(bf),
        "ones_half": ones_half,
        "head_rows": head_rows.astype(np.float32),
        "rank": np.tile(np.arange(E, 0, -1, dtype=np.float32), (P, 2, 1)),
    }


def split_weights(nc, S, name, pieces, transposes=None):
    turned = S.sem(f"{name}_turned")
    hi_done = S.sem(f"{name}_hi")
    lo_done = S.sem(f"{name}_lo")
    with nc.Block() as block:
        if transposes:
            @block.tensor
            def _(pe):
                for n in range(len(pieces)):
                    wait(pe, lo_done, n - len(S.bank) + 1)
                    transposes(pe, n).then_inc(turned, 1)

        @block.scalar
        def _(act):
            for n, (hi, _, src) in enumerate(pieces):
                if transposes:
                    act.wait_ge(turned, n + 1)
                act.activation(hi, src, ACT.Copy).then_inc(hi_done, 1)

        @block.vector
        def _(dve):
            for n, (hi, lo, src) in enumerate(pieces):
                dve.wait_ge(hi_done, n + 1)
                dve.tensor_tensor(lo, src, hi.bitcast(F32), ALU.subtract).then_inc(lo_done, 1)


def ln_scales(nc, S, name, twice=False):
    step = S.sem(f"{name}_step")
    root = S.sem(f"{name}_root")
    even, odd = S.stats[:, :, 0:3], S.stats[:, :, 3:6]
    with nc.Block() as block:
        @block.vector
        def _(dve):
            n = [0]

            def then(ins):
                n[0] += 1
                ins.then_inc(step, 1)
                dve.wait_ge(step, n[0])

            diff, var = S.rstd2, S.var
            then(dve.tensor_tensor(S.mean[:], even[:, :, 1], odd[:, :, 1], ALU.add))
            then(dve.tensor_tensor(diff[:], even[:, :, 1], odd[:, :, 1], ALU.subtract))
            then(dve.tensor_scalar(S.mean[:], S.mean[:], 0.5, None, ALU.mult))
            then(dve.tensor_tensor(diff[:], diff[:], diff[:], ALU.mult))
            then(dve.tensor_tensor(var[:], even[:, :, 2], odd[:, :, 2], ALU.add))
            then(dve.tensor_scalar(diff[:], diff[:], 0.25, LN_EPS, ALU.mult, ALU.add))
            then(dve.scalar_tensor_tensor(var[:], var[:], 1.0 / C, diff[:], ALU.mult, ALU.add))
            sqrt_at = n[0]
            dve.wait_ge(root, 1)
            then(dve.reciprocal(S.rstd[:], S.root[:]))
            if twice:
                then(dve.tensor_scalar(var[:], var[:], LN_EPS, None, ALU.subtract))
                then(dve.tensor_tensor(var[:], var[:], S.rstd[:], ALU.mult))
                then(dve.tensor_tensor(var[:], var[:], S.rstd[:], ALU.mult))
                then(dve.tensor_scalar(var[:], var[:], LN_EPS, None, ALU.add))
                dve.wait_ge(root, 2)
                then(dve.reciprocal(S.rstd2[:], S.root[:]))
                then(dve.tensor_tensor(S.rstd2[:], S.rstd2[:], S.rstd[:], ALU.mult))

        @block.scalar
        def _(act):
            act.wait_ge(step, 7)
            act.activation(S.root[:], S.var[:], ACT.Sqrt).then_inc(root, 1)
            if twice:
                act.wait_ge(step, 12)
                act.activation(S.root[:], S.var[:], ACT.Sqrt).then_inc(root, 1)


def attention_weights(nc, S, name, W, transposed):
    raw = S.raw[:, 0:4 * KT * C].rearrange("p (w k c) -> p w k c", w=4, k=KT)
    if not transposed:
        split_weights(nc, S, name, [(W.hi[:, w], W.lo[:, w], raw[:, w]) for w in range(4)])
        return

    def turn(pe, n):
        out = S.bank[n % len(S.bank)].rearrange("p (k c) -> p k c", k=KT)
        for k in range(KT):
            for o in range(KT):
                last = pe.transpose(out[:, k, o * P:(o + 1) * P], raw[:, n, o, k * P:(k + 1) * P], S.ident[:])
        return last

    split_weights(nc, S, name, [
        (W.hi[:, n], W.lo[:, n], S.bank[n % len(S.bank)].rearrange("p (k c) -> p k c", k=KT))
        for n in range(4)], turn)


def attention(nc, S, L, ctx_dram, W, bias, count, load_next):
    NP = S.n_seq // 2
    UP = 2 * UNITS
    with ExitStack() as mem:
        def sb(name, shape, dt=F32):
            return mem.enter_context(nc.sbuf_tensor(f"{L}_{name}", shape, dt))

        own_sems = []

        def sem(name):
            own_sems.append(mem.enter_context(nc.semaphore(f"{L}_{name}")))
            return own_sems[-1]

        normed = sb("normed", [P, 2, C])
        ctx_in = sb("ctx_in", [P, 2, 2, C])
        nT = [sb("nT_hi", [P, KT, 2 * P], F32R), sb("nT_lo", [P, KT, 2 * P], F32R)]
        cT = [sb("cT_hi", [P, KT, 2 * P], F32R), sb("cT_lo", [P, KT, 2 * P], F32R)]
        q_sb = sb("q", [P, KT, 2 * P])
        q_heads = sb("q_heads", [P, 2, KT, P // D, P])
        kT = sb("kT", [P, 2, KT, 2 * P])
        v_pad = sb("v_pad", [P, 2, 2, H * 32])
        probs = sb("probs", [P, 2, UH, P])
        probsT = sb("probsT", [P, 2, UH, P])
        neg_max = sb("neg_max", [P, 2, UH])
        recip = sb("recip", [P, KT, P])
        o_sb = sb("o", [P, KT, P])
        oT = [sb("oT_hi", [P, KT, P], F32R), sb("oT_lo", [P, KT, P], F32R)]
        x_new = sb("x_new", [P, C])
        seq_stats = sb("seq_stats", [P, 6])

        scores = [S.bank[0].rearrange("p (h k) -> p h k", h=UH), S.bank[1].rearrange("p (h k) -> p h k", h=UH)]
        pT_ps = [S.bank[2].rearrange("p (h k) -> p h k", h=UH), S.bank[3].rearrange("p (h k) -> p h k", h=UH)]
        o_ps = S.bank[4].rearrange("p (m q) -> p m q", q=P)
        sum_ps = S.bank[5].rearrange("p (m q) -> p m q", q=P)
        bank_a, bank_b = S.bank[6], S.bank[7]
        tiles = lambda bank: bank.rearrange("p (k t) -> p k t", k=KT)

        ctx_loaded = [sem("ctx_even_loaded"), sem("ctx_odd_loaded")]
        n_ready, bo_added, x_done = sem("n_ready"), sem("bo_added"), sem("x_done")
        tn_ready, tc_ready = sem("tn_ready"), sem("tc_ready")
        nhi_ready, nlo_ready = sem("nhi_ready"), sem("nlo_ready")
        chi_ready, clo_ready = sem("chi_ready"), sem("clo_ready")
        q_made, k_made, v_made = sem("q_made"), sem("k_made"), sem("v_made")
        q_ready, kT_ready, v_ready, v_cleared = sem("q_ready"), sem("kT_ready"), sem("v_ready"), sem("v_cleared")
        q_heads_ready = sem("q_heads_ready")
        scores_ready, max_ready, exp_done = sem("scores_ready"), sem("max_ready"), sem("exp_done")
        pT_made, pT_ready, pv_done = sem("pT_made"), sem("pT_ready"), sem("pv_done")
        recip_done, o_done, ohi_done, o_ready = sem("recip_done"), sem("o_done"), sem("ohi_done"), sem("o_ready")
        y_made, stats_done = sem("y_made"), sem("stats_done")

        def pairs(eng, step):
            for b in range(2):
                step(b, b)
            if NP > 4:
                with eng.Fori(1, NP // 2 - 1) as i:
                    for b in range(2):
                        step(2 * i + b, b)
            for b in range(2):
                step(NP - 2 + b, b)

        with nc.Block() as block:
            @block.sync
            def _(sp):
                def load(p, b):
                    wait(sp, tc_ready, p - 1)
                    sp.dma_start(ctx_in[:, b], ctx_dram[bass.ds(2 * p, 2)].rearrange("s t c -> t s c")
                                 ).then_inc(ctx_loaded[b], 16)
                load(0, 0)
                next_loaded = load_next(sp)
                load(1, 1)
                if NP > 4:
                    with sp.Fori(1, NP // 2 - 1) as i:
                        for b in range(2):
                            load(2 * i + b, b)
                for b in range(2):
                    load(NP - 2 + b, b)
                wait(sp, *next_loaded)

            @block.tensor
            def _(pe):
                def turn_n(p):
                    wait(pe, n_ready, p + 1)
                    wait(pe, v_ready, p)
                    for k in range(KT):
                        for s in range(2):
                            last = pe.transpose(tiles(bank_a)[:, k, s * P:(s + 1) * P],
                                                normed[:, s, k * P:(k + 1) * P], S.ident[:])
                    last.then_inc(tn_ready, 1)

                def turn_c(p, b):
                    wait(pe, ctx_loaded[b], 8 * (p - b) + 16)
                    wait(pe, x_done, 2 * p - 3)
                    for k in range(KT):
                        for s in range(2):
                            last = pe.transpose(tiles(bank_b)[:, k, s * P:(s + 1) * P],
                                                ctx_in[:, b, s, k * P:(k + 1) * P], S.ident[:])
                    last.then_inc(tc_ready, 1)

                def project_q(p):
                    wait(pe, nlo_ready, p + 1)
                    wait(pe, x_done, 2 * p - 2)
                    for m in range(KT):
                        for k in range(KT):
                            last = mm3(pe, tiles(bank_a)[:, m, :],
                                       [w[:, 0, k, m * P:(m + 1) * P] for w in (W.hi, W.lo)],
                                       [t[:, k, :] for t in nT], k == 0, k == KT - 1)
                    last.then_inc(q_made, 1)

                def project_k(p):
                    wait(pe, clo_ready, p + 1)
                    for m in range(KT):
                        for k in range(KT):
                            last = mm3(pe, tiles(bank_b)[:, m, :],
                                       [w[:, 1, k, m * P:(m + 1) * P] for w in (W.hi, W.lo)],
                                       [t[:, k, :] for t in cT], k == 0, k == KT - 1)
                    last.then_inc(k_made, 1)

                def project_v(p, s):
                    if s == 0:
                        wait(pe, q_ready, p + 1)
                    for k in range(KT):
                        last = mm3(pe, tiles(bank_a)[:, s, :], [t[:, k, s * P:(s + 1) * P] for t in cT],
                                   [w[:, 2, k, :] for w in (W.hi, W.lo)], k == 0, k == KT - 1)
                    if s == 1:
                        last.then_inc(v_made, 1)

                def project_o(p, s):
                    wait(pe, o_ready, 2 * p + s + 1)
                    if s == 0:
                        pe.wait_ge(kT_ready, NP if is_(p, NP - 1) else p + 2)
                    elif is_(p, NP - 1):
                        pe.wait_ge(x_done, 2 * p)
                    elif is_(p, NP - 2):
                        pe.wait_ge(v_ready, NP)
                    else:
                        pe.wait_ge(nlo_ready, p + 3)
                    out = (bank_b, bank_a)[s][:, 0:C]
                    for k in range(KT):
                        last = mm3(pe, out, [t[:, k, :] for t in oT], [w[:, 3, k, :] for w in (W.hi, W.lo)],
                                   k == 0, k == KT - 1)
                    last.then_inc(y_made, 1)

                def score(p, b, u):
                    s, j = divmod(u, UNITS)
                    wait(pe, exp_done, UP * p + u - 1)
                    if u % UNITS == 0:
                        pe.wait_ge(q_heads_ready, 2 * p + s + 1)
                    if u == 0:
                        pe.wait_ge(kT_ready, p + 1)
                    bank = scores[u % 2]
                    pe.matmul(S.bank[u % 2], S.ident_bf[:], S.hidden_bf[:], start=True, stop=False)
                    for i in range(UH):
                        last = pe.matmul(bank[:, i, :], q_heads[:, s, j // 2, (j % 2) * UH + i, :],
                                         kT[:, b, j // 2, s * P:(s + 1) * P], start=False, stop=i == UH - 1)
                    last.then_inc(scores_ready, 1)

                def turn_p(p, u):
                    wait(pe, exp_done, UP * p + u + 1)
                    wait(pe, pT_ready, UP * p + u - 1)
                    for i in range(UH):
                        last = pe.transpose(pT_ps[u % 2][:, i, :], probs[:, u % 2, i, :], S.ident[:])
                    last.then_inc(pT_made, 1)

                def times_v(p, b, u):
                    s, j = divmod(u, UNITS)
                    m, e = divmod(j, 2)
                    wait(pe, pT_ready, UP * p + u + 1)
                    if j == 0:
                        wait(pe, o_done, 2 * p + s)
                    if u == 0:
                        pe.wait_ge(v_ready, p + 1)
                    for to_sum in range(2):
                        for i in range(UH):
                            h = UH * j + i
                            left = S.ones_half[:, e, :] if to_sum else v_pad[:, b, s, h * 32:(h + 1) * 32]
                            out = (o_ps, sum_ps)[to_sum][32 * i:32 * (i + 1), m, :]
                            last = pe.matmul(out, left, probsT[:, u % 2, i, :], start=e == 0, stop=e == 1)
                    last.then_inc(pv_done, 1)

                def step(p, b):
                    first = is_(p, 0)
                    more = not is_(p, NP - 1)
                    for k in range(UP):
                        score(p, b, k)
                        if k >= 1:
                            turn_p(p, k - 1)
                        elif not first:
                            turn_p(p - 1, UP - 1)
                        if k >= 2:
                            times_v(p, b, k - 2)
                        elif not first:
                            times_v(p - 1, 1 - b, UP - 2 + k)
                        if k == 0 and more:
                            turn_n(p + 1)
                        if k == 1 and more:
                            turn_c(p + 1, 1 - b)
                        if k == 2 and not first:
                            project_o(p - 1, 1)
                        if k == 3 and more:
                            project_q(p + 1)
                        if k == 4 and more:
                            project_k(p + 1)
                        if k == 5 and more:
                            project_v(p + 1, 0)
                        if k == 6:
                            project_o(p, 0)
                        if k == 7 and more:
                            project_v(p + 1, 1)

                turn_n(0)
                turn_c(0, 0)
                project_q(0)
                project_k(0)
                project_v(0, 0)
                project_v(0, 1)
                pairs(pe, step)
                turn_p(NP - 1, UP - 1)
                times_v(NP - 1, 1, UP - 2)
                times_v(NP - 1, 1, UP - 1)
                project_o(NP - 1, 1)

            @block.scalar
            def _(act):
                def round_n(p):
                    act.wait_ge(tn_ready, p + 1)
                    wait(act, q_made, p)
                    act.activation(nT[0][:], tiles(bank_a), ACT.Copy).then_inc(nhi_ready, 1)

                def round_c(p):
                    act.wait_ge(tc_ready, p + 1)
                    wait(act, v_made, p)
                    act.activation(cT[0][:], tiles(bank_b), ACT.Copy).then_inc(chi_ready, 1)

                def keep_q(p):
                    act.wait_ge(q_made, p + 1)
                    wait(act, q_heads_ready, 2 * p)
                    for m in range(KT):
                        last = act.activation(q_sb[:, m, :], tiles(bank_a)[:, m, :], ACT.Identity,
                                              bias=bias.q[:, m:m + 1])
                    last.then_inc(q_ready, 1)

                def keep_k(p, b):
                    act.wait_ge(k_made, p + 1)
                    wait(act, scores_ready, UP * (p - 1))
                    for m in range(KT):
                        last = act.activation(kT[:, b, m, :], tiles(bank_b)[:, m, :], ACT.Identity,
                                              bias=bias.k[:, m:m + 1])
                    last.then_inc(kT_ready, 1)

                def exps(p, u):
                    act.wait_ge(max_ready, UP * p + u + 1)
                    wait(act, pT_made, UP * p + u - 1)
                    for i in range(UH):
                        last = act.activation(probs[:, u % 2, i, :], scores[u % 2][:, i, :], ACT.Exp,
                                              bias=neg_max[:, u % 2, i:i + 1])
                    last.then_inc(exp_done, 1)

                def step(p, b):
                    more = not is_(p, NP - 1)
                    for k in range(UP):
                        exps(p, k)
                        if k == 0 and more:
                            round_n(p + 1)
                        if k == 1 and more:
                            round_c(p + 1)
                        if k == 3 and more:
                            keep_q(p + 1)
                        if k == 4 and more:
                            keep_k(p + 1, 1 - b)

                round_n(0)
                round_c(0)
                keep_q(0)
                keep_k(0, 0)
                pairs(act, step)

            @block.vector
            def _(dve):
                def norm(p):
                    wait(dve, tn_ready, p)
                    for s in range(2):
                        q = 2 * p + s
                        last = dve.tensor_scalar(normed[:, s, :], S.x[:, q, :], S.mean[:, bass.ds(q, 1)],
                                                 S.rstd[:, bass.ds(q, 1)], ALU.subtract, ALU.mult)
                    last.then_inc(n_ready, 1)

                def rest_n(p):
                    dve.wait_ge(nhi_ready, p + 1)
                    dve.tensor_tensor(nT[1][:], tiles(bank_a), nT[0][:].bitcast(F32), ALU.subtract
                                      ).then_inc(nlo_ready, 1)

                def rest_c(p):
                    dve.wait_ge(chi_ready, p + 1)
                    dve.tensor_tensor(cT[1][:], tiles(bank_b), cT[0][:].bitcast(F32), ALU.subtract
                                      ).then_inc(clo_ready, 1)

                def keep_v(p, b):
                    dve.wait_ge(v_made, p + 1)
                    wait(dve, pv_done, UP * (p - 1))
                    for s in range(2):
                        for m in range(KT):
                            out = v_pad[:, b, s, m * 256:(m + 1) * 256]
                            src = tiles(bank_a)[:, s, m * P:(m + 1) * P].rearrange("p (e i d) -> p e i d", e=2, i=UH)
                            add = bias.v[:, m * P:(m + 1) * P].rearrange("p (e i d) -> p e i d", e=2, i=UH)
                            for e in range(2):
                                half = out[:, e * P:(e + 1) * P].rearrange("p (i z) -> p i z", i=UH)
                                last = dve.tensor_tensor(half[:, :, e * D:(e + 1) * D], src[:, e], add[:, e], ALU.add)
                    last.then_inc(v_ready, 1)

                def row_max(p, u):
                    dve.wait_ge(scores_ready, UP * p + u + 1)
                    wait(dve, exp_done, UP * p + u - 1)
                    dve.tensor_reduce(neg_max[:, u % 2, :], scores[u % 2], AX.X, ALU.max, negate=True
                                      ).then_inc(max_ready, 1)

                def keep_p(p, u):
                    dve.wait_ge(pT_made, UP * p + u + 1)
                    wait(dve, pv_done, UP * p + u - 1)
                    seen = count[:, u % UNITS, :].unsqueeze(1).broadcast_to([P, UH, P])
                    dve.tensor_tensor(probsT[:, u % 2], pT_ps[u % 2], seen, ALU.mult).then_inc(pT_ready, 1)

                def normalize(p, s):
                    n = 2 * p + s
                    dve.wait_ge(pv_done, UP * p + (s + 1) * UNITS)
                    dve.reciprocal(recip[:], sum_ps[:, 0:KT, :]).then_inc(recip_done, 1)
                    dve.wait_ge(recip_done, n + 1)
                    dve.tensor_tensor(o_sb[:], o_ps[:, 0:KT, :], recip[:], ALU.mult).then_inc(o_done, 1)
                    dve.wait_ge(o_done, n + 1)
                    wait(dve, y_made, n)
                    dve.tensor_copy(oT[0][:], o_sb[:]).then_inc(ohi_done, 1)
                    dve.wait_ge(ohi_done, n + 1)
                    dve.tensor_tensor(oT[1][:], o_sb[:], oT[0][:].bitcast(F32), ALU.subtract).then_inc(o_ready, 1)

                def residual(p, s):
                    n = 2 * p + s
                    y = (bank_b, bank_a)[s][:, 0:C]
                    dve.wait_ge(y_made, n + 1)
                    dve.wait_ge(bo_added, p + 1)
                    dve.tensor_tensor(x_new[:], y, S.x[:, n, :], ALU.add).then_inc(x_done, 1)
                    dve.wait_ge(x_done, n + 1)
                    dve.bn_stats(seq_stats[:], x_new[:]).then_inc(stats_done, 1)
                    dve.tensor_copy(S.x[:, n, :], x_new[:])
                    dve.wait_ge(stats_done, n + 1)
                    dve.tensor_copy(S.stats[:, n, :], seq_stats[:])

                def step(p, b):
                    first = is_(p, 0)
                    more = not is_(p, NP - 1)
                    more2 = not (is_(p, NP - 1) or is_(p, NP - 2))
                    for k in range(UP):
                        row_max(p, k)
                        if k >= 1:
                            keep_p(p, k - 1)
                        elif not first:
                            keep_p(p - 1, UP - 1)
                        if k == 0 and more:
                            rest_n(p + 1)
                        if k == 1:
                            if not first:
                                normalize(p - 1, 1)
                            if more:
                                rest_c(p + 1)
                        if k == 2 and not first:
                            residual(p - 1, 1)
                        if k == 4 and more2:
                            norm(p + 2)
                        if k == 5:
                            normalize(p, 0)
                        if k == 6:
                            residual(p, 0)
                        if k == 7 and more:
                            keep_v(p + 1, 1 - b)

                dve.memset(v_pad[:], 0.0).then_inc(v_cleared, 1)
                norm(0)
                rest_n(0)
                rest_c(0)
                norm(1)
                dve.wait_ge(v_cleared, 1)
                keep_v(0, 0)
                pairs(dve, step)
                keep_p(NP - 1, UP - 1)
                normalize(NP - 1, 1)
                residual(NP - 1, 1)

            @block.gpsimd
            def _(pool):
                def spread_q(p, s):
                    pool.wait_ge(q_ready, p + 1)
                    wait(pool, scores_ready, UP * (p - 1) + (s + 1) * UNITS)
                    for m in range(KT):
                        last = pool.tensor_tensor(
                            q_heads[:, s, m],
                            q_sb[:, m, s * P:(s + 1) * P].unsqueeze(1).broadcast_to([P, P // D, P]),
                            S.head_rows[:].unsqueeze(2).broadcast_to([P, P // D, P]), ALU.mult)
                    last.then_inc(q_heads_ready, 1)

                def add_bo(p):
                    pool.wait_ge(n_ready, p + 1)
                    for s in range(2):
                        n = 2 * p + s
                        last = pool.tensor_tensor(S.x[:, n, :], S.x[:, n, :], bias.o[:], ALU.add)
                    last.then_inc(bo_added, 1)

                def step(p, b):
                    more = not is_(p, NP - 1)
                    add_bo(p)
                    if more:
                        for s in range(2):
                            spread_q(p + 1, s)

                for s in range(2):
                    spread_q(0, s)
                pairs(pool, step)
        clear(nc, own_sems)


def gate_weights(nc, S, name, G):
    step, squares, root = (S.sem(f"{name}_{n}") for n in ("step", "squares", "root"))
    with nc.sbuf_tensor(f"{name}_ones", [P, P], F32) as ones, nc.Block() as block:
        @block.vector
        def _(dve):
            n = [0]

            def then(ins):
                n[0] += 1
                ins.then_inc(step, 1)
                dve.wait_ge(step, n[0])

            dve.memset(ones[:], 1.0)
            then(dve.tensor_tensor(G.work[:], G.sim[:], G.sim[:], ALU.mult))
            dve.wait_ge(squares, 1)
            then(dve.tensor_copy(G.norm[:], S.bank[0][:, 0:E]))
            then(dve.tensor_tensor(G.norm[:], S.bank[0][:, E:2 * E], G.norm[:], ALU.add))
            dve.wait_ge(root, 1)
            then(dve.tensor_scalar(G.norm[:], G.norm[:], 1e-12, None, ALU.max))
            then(dve.reciprocal(G.norm[:], G.norm[:]))
            then(dve.tensor_tensor(G.sim[:], G.sim[:], G.norm[:].unsqueeze(1).broadcast_to([P, KT, E]), ALU.mult))
            then(dve.tensor_copy(G.hi[:], G.sim[:]))
            then(dve.tensor_tensor(G.lo[:], G.sim[:], G.hi[:].bitcast(F32), ALU.subtract))
            dve.wait_ge(root, 2)
            then(dve.tensor_scalar(G.gates[:], G.gates[:], 1.0, None, ALU.add))
            then(dve.reciprocal(G.gates[:], G.gates[:]))

        @block.tensor
        def _(pe):
            pe.wait_ge(step, 1)
            pe.matmul(S.bank[0][:, 0:KT * E], ones[:], G.work[:].rearrange("p k e -> p (k e)"),
                      start=True, stop=True).then_inc(squares, 1)

        @block.scalar
        def _(act):
            act.wait_ge(step, 3)
            act.activation(G.norm[:], G.norm[:], ACT.Sqrt).then_inc(root, 1)
            act.activation(G.gates[:], G.gates[:], ACT.Exp, scale=-1.0).then_inc(root, 1)


GATE_BEFORE, GATE_STEPS = 17, 24


def gate_tiles(sb, n):
    one = {f: sb(f"gate_{f}", [P, n]) for f in ("norm", "top", "second", "order", "peak", "none", "total")}
    all_ = {f: sb(f"gate_{f}", [P, n, E]) for f in ("logit", "tied", "first", "both", "rest", "shifted", "exp")}
    return named(n=n, square_sum=sb("square_sum", [P, n]), **one, **all_)


def gate_chain(dve, step, index, at):
    n = [at]

    def then(ins):
        n[0] += 1
        ins.then_inc(step, 1)
        dve.wait_ge(step, GATE_STEPS * index + n[0])
    return then


def gate_before(S, dve, T, G, dots, step, index):
    then = gate_chain(dve, step, index, 0)
    wide = lambda t: t[:].unsqueeze(2).broadcast_to([P, T.n, E])
    rank = S.rank[:, 0:T.n, :]
    tt, ts = dve.tensor_tensor, dve.tensor_scalar
    then(ts(T.norm[:], T.norm[:], 1e-12, None, ALU.max))
    then(dve.reciprocal(T.norm[:], T.norm[:]))
    then(tt(T.logit[:], dots, wide(T.norm), ALU.mult))
    then(tt(T.logit[:], T.logit[:], G.gates[:].unsqueeze(1).broadcast_to([P, T.n, E]), ALU.subtract))
    then(dve.tensor_reduce(T.top[:], T.logit[:], AX.X, ALU.max))
    then(tt(T.tied[:], T.logit[:], wide(T.top), ALU.is_ge))
    then(tt(T.tied[:], T.tied[:], rank, ALU.mult))
    then(dve.tensor_reduce(T.order[:], T.tied[:], AX.X, ALU.max))
    then(tt(T.first[:], rank, wide(T.order), ALU.is_equal))
    then(dve.scalar_tensor_tensor(T.rest[:], T.first[:], MASKED, T.logit[:], ALU.mult, ALU.add))
    then(dve.tensor_reduce(T.second[:], T.rest[:], AX.X, ALU.max))
    then(tt(T.tied[:], T.rest[:], wide(T.second), ALU.is_ge))
    then(tt(T.tied[:], T.tied[:], rank, ALU.mult))
    then(dve.tensor_reduce(T.order[:], T.tied[:], AX.X, ALU.max))
    then(tt(T.both[:], rank, wide(T.order), ALU.is_equal))
    then(ts(T.peak[:], T.top[:], 0.0, None, ALU.max))
    then(dve.scalar_tensor_tensor(T.shifted[:], T.logit[:], 0.0, wide(T.peak), ALU.max, ALU.subtract))


def gate_after(dve, T, out, exp_done, step, index, ready):
    then = gate_chain(dve, step, index, GATE_BEFORE)
    wide = lambda t: t[:].unsqueeze(2).broadcast_to([P, T.n, E])
    tt = dve.tensor_tensor
    then(tt(T.both[:], T.both[:], T.first[:], ALU.add))
    then(dve.tensor_scalar(T.none[:], T.top[:], 0.0, None, ALU.is_le))
    then(tt(T.both[:], T.both[:], wide(T.none), ALU.mult))
    then(dve.scalar_tensor_tensor(T.both[:], T.logit[:], 0.0, T.both[:], ALU.is_gt, ALU.add))
    dve.wait_ge(exp_done, index + 1)
    then(tt(T.exp[:], T.exp[:], T.both[:], ALU.mult))
    then(dve.tensor_reduce(T.total[:], T.exp[:], AX.X, ALU.add))
    then(dve.reciprocal(T.total[:], T.total[:]))
    tt(out, T.exp[:], wide(T.total), ALU.mult).then_inc(ready, 1)


def parities(eng, count, step):
    for b in range(2):
        step(b, b)
    if count > 6:
        with eng.Fori(1, count // 2 - 2) as i:
            for b in range(2):
                step(2 * i + b, b)
    for n in range(max(2, count - 4), count):
        step(n, n % 2)


def mixture_attention(nc, S, L, W, G, ln_w, ln_b, hs_dram, load_next):
    NS = S.n_seq
    Q3 = 3 * HID
    with ExitStack() as mem:
        def sb(name, shape, dt=F32):
            return mem.enter_context(nc.sbuf_tensor(f"{L}_{name}", shape, dt))

        own_sems = []

        def sem(name):
            own_sems.append(mem.enter_context(nc.semaphore(f"{L}_{name}")))
            return own_sems[-1]

        normed = sb("normed", [P, 2, C])
        square = sb("square", [P, C])
        nT = [sb("nT_hi", [P, 2, KT, P], F32R), sb("nT_lo", [P, 2, KT, P], F32R)]
        T = gate_tiles(sb, 1)
        rw = sb("rw", [P, 2, 1, E])
        rw_out = sb("rw_out", [P, 2, E])
        qkv = sb("qkv", [P, 2, Q3])
        qkv_odd = sb("qkv_odd", [P, 2, Q3])
        qkv_part = sb("qkv_part", [P, 3, Q3])
        qkT = sb("qkT", [P, 2, P])
        neg_max, row_sum, row_scale = sb("neg_max", [P, 1]), sb("row_sum", [P, 1]), sb("row_scale", [P, 1])
        probs, probsT = sb("probs", [P, P]), sb("probsT", [P, P])
        attn = sb("attn", [P, HID])
        aT = [sb("aT_hi", [P, P], F32R), sb("aT_lo", [P, P], F32R)]
        y = sb("y", [P, C])
        hs_even, hs_odd, hs = sb("hs_even", [P, C]), sb("hs_odd", [P, C]), sb("hs", [P, 2, C])
        out_part = sb("out_part", [P, 3, C])
        seq_stats = sb("seq_stats", [P, 6])

        nT_ps = S.bank[0][:, 0:C].rearrange("p (k t) -> p k t", k=KT)
        dots_ps = S.bank[0][:, C:C + E]
        qkT_ps = S.bank[1][:, 0:2 * P].rearrange("p (k t) -> p k t", k=2)
        aT_ps = S.bank[1][:, 0:P]
        scores, attn_ps, pT_ps = S.bank[2][:, 0:P], S.bank[2][:, 0:HID], S.bank[3][:, 0:P]
        q_bank = [S.bank[4][:, 0:Q3], S.bank[5][:, 0:Q3]]
        o_bank = [S.bank[6].rearrange("p (e c) -> p e c", e=2), S.bank[7].rearrange("p (e c) -> p e c", e=2)]

        names = ("n_made scaled n_ready squared rooted tn_ready nhi_ready nlo_ready dots_made "
                 "gate_step gate_exp gate_ready kept q_even_made q_odd_made even_added odd_read odd_added "
                 "qkv_ready turned qkT_ready scored max_ready exp_done recip_done pT_made pT_ready attn_made "
                 "attn_ready aT_made ahi_ready alo_ready o_even_made o_odd_made o_even_added o_odd_read "
                 "o_odd_added y_ready hs_ready x_added stats_done").split()
        M = named(**{n: sem(n) for n in names})
        hs_stored = [sem("hs_even_stored"), sem("hs_odd_stored")]
        has = lambda s, ahead: not any(is_(s, NS - 1 - d) for d in range(ahead))

        with nc.Block() as block:
            @block.sync
            def _(sp):
                next_loaded = load_next(sp)

                def step(s, b):
                    sp.wait_ge(M.hs_ready, s + 1)
                    sp.dma_start(hs_dram[bass.ds(s, 1)].rearrange("s t c -> (s t) c"), hs[:, b]
                                 ).then_inc(hs_stored[b], 16)
                parities(sp, NS, step)
                for b in range(2):
                    sp.wait_ge(hs_stored[b], 8 * NS)
                wait(sp, *next_loaded)

            @block.tensor
            def _(pe):
                def turn_n(s, b):
                    pe.wait_ge(M.n_ready, s + 1)
                    wait(pe, M.gate_step, GATE_STEPS * (s - 1) + 3)
                    for k in range(KT):
                        last = pe.transpose(nT_ps[:, k, :], normed[:, b, k * P:(k + 1) * P], S.ident[:])
                    last.then_inc(M.tn_ready, 1)

                def dot_gate(s, b):
                    pe.wait_ge(M.nlo_ready, s + 1)
                    for k in range(KT):
                        last = mm3(pe, dots_ps, [t[:, b, k, :] for t in nT], [G.hi[:, k, :], G.lo[:, k, :]],
                                   k == 0, k == KT - 1)
                    last.then_inc(M.dots_made, 1)

                def project(s, b, e):
                    if e % 2 == 0:
                        wait(pe, M.even_added, 4 * s + e // 2)
                    else:
                        wait(pe, M.odd_read, 4 * s + e // 2)
                    for k in range(KT):
                        last = mm3(pe, q_bank[e % 2], [t[:, b, k, :] for t in nT],
                                   [w[:, e, k, :] for w in (W.hi, W.lo)], k == 0, k == KT - 1)
                    last.then_inc((M.q_even_made, M.q_odd_made)[e % 2], 1)

                def turn_qk(s, b):
                    pe.wait_ge(M.qkv_ready, s + 1)
                    wait(pe, M.alo_ready, s)
                    for n in range(2):
                        last = pe.transpose(qkT_ps[:, n, :], qkv[:, b, n * HID:(n + 1) * HID], S.ident[:])
                    last.then_inc(M.turned, 1)

                def score(s):
                    pe.wait_ge(M.qkT_ready, s + 1)
                    wait(pe, M.attn_ready, s)
                    pe.matmul(scores, S.ident_bf[:], S.hidden_bf[:, 0:P], start=True, stop=False)
                    pe.matmul(scores, qkT[:, 0, :], qkT[:, 1, :], start=False, stop=True).then_inc(M.scored, 1)

                def turn_p(s):
                    pe.wait_ge(M.exp_done, s + 1)
                    wait(pe, M.pT_ready, s)
                    pe.transpose(pT_ps, probs[:], S.ident[:]).then_inc(M.pT_made, 1)

                def times_v(s, b):
                    pe.wait_ge(M.pT_ready, s + 1)
                    pe.matmul(attn_ps, probsT[:], qkv[:, b, 2 * HID:Q3], start=True, stop=True).then_inc(M.attn_made, 1)

                def turn_a(s):
                    pe.wait_ge(M.attn_ready, s + 1)
                    pe.transpose(aT_ps, attn[:], S.ident[:]).then_inc(M.aT_made, 1)

                def project_out(s):
                    pe.wait_ge(M.alo_ready, s + 1)
                    for n in range(E // 2):
                        if n % 2 == 0:
                            wait(pe, M.o_even_added, 4 * s + n)
                        else:
                            wait(pe, M.o_odd_read, 4 * s + n - 1)
                        mm3(pe, S.bank[6 + n % 2], [t[:] for t in aT],
                            [w[:, 2 * n:2 * n + 2, :].rearrange("p e c -> p (e c)") for w in (W.o_hi, W.o_lo)],
                            True, True).then_inc((M.o_even_made, M.o_odd_made)[n % 2], 1)

                def step(s, b):
                    one, two = has(s, 1), has(s, 2)
                    chain = {0: lambda: turn_qk(s, b), 1: lambda: score(s), 3: lambda: turn_p(s),
                             4: lambda: times_v(s, b), 6: lambda: turn_a(s), 7: lambda: project_out(s)}
                    for e in range(E):
                        if one:
                            project(s + 1, 1 - b, e)
                        if e in chain:
                            chain[e]()
                        if e == 2 and two:
                            turn_n(s + 2, b)
                        if e == 5 and two:
                            dot_gate(s + 2, b)

                for s in range(2):
                    turn_n(s, s)
                    dot_gate(s, s)
                for e in range(E):
                    project(0, 0, e)
                parities(pe, NS, step)

            @block.scalar
            def _(act):
                def squares(s, b):
                    act.wait_ge(M.n_ready, s + 1)
                    wait(act, M.gate_step, GATE_STEPS * (s - 1) + 3)
                    act.activation(square[:], normed[:, b, :], ACT.Square, accum_out=T.square_sum[:]).then_inc(M.squared, 1)
                    act.wait_ge(M.squared, s + 1)
                    act.activation(T.norm[:], T.square_sum[:], ACT.Sqrt).then_inc(M.rooted, 1)

                def round_n(s, b):
                    act.wait_ge(M.tn_ready, s + 1)
                    wait(act, M.q_odd_made, 4 * (s - 1))
                    act.activation(nT[0][:, b], nT_ps, ACT.Copy).then_inc(M.nhi_ready, 1)

                def gate_exp(s):
                    act.wait_ge(M.gate_step, GATE_STEPS * s + GATE_BEFORE)
                    act.activation(T.exp[:], T.shifted[:], ACT.Exp).then_inc(M.gate_exp, 1)

                def weigh_odd(s, b, e):
                    act.wait_ge(M.q_odd_made, 4 * s + e // 2 + 1)
                    if e == 1:
                        act.wait_ge(M.gate_ready, s + 1)
                        wait(act, M.qkv_ready, s - 1)
                        out = qkv_odd[:, b, :]
                    else:
                        wait(act, M.odd_added, 3 * (s - 1) + e // 2)
                        out = qkv_part[:, e // 2 - 1, :]
                    act.activation(out, q_bank[1], ACT.Copy, scale=rw[:, b, 0, e:e + 1]).then_inc(M.odd_read, 1)

                def keep_qk(s):
                    act.wait_ge(M.turned, s + 1)
                    wait(act, M.scored, s)
                    act.activation(qkT[:, 0, :], qkT_ps[:, 0, :], ACT.Copy, scale=float(HID) ** -0.5)
                    act.activation(qkT[:, 1, :], qkT_ps[:, 1, :], ACT.Copy).then_inc(M.qkT_ready, 1)

                def exps(s):
                    act.wait_ge(M.max_ready, s + 1)
                    wait(act, M.pT_made, s)
                    wait(act, M.recip_done, s)
                    act.activation(probs[:], scores, ACT.Exp, bias=neg_max[:], accum_out=row_sum[:]).then_inc(M.exp_done, 1)

                def keep_p(s):
                    act.wait_ge(M.pT_made, s + 1)
                    wait(act, M.attn_made, s)
                    act.activation(probsT[:], pT_ps, ACT.Copy).then_inc(M.pT_ready, 1)

                def round_a(s):
                    act.wait_ge(M.aT_made, s + 1)
                    wait(act, M.o_odd_made, 2 * s)
                    act.activation(aT[0][:], aT_ps, ACT.Copy).then_inc(M.ahi_ready, 1)

                def weigh_out(s, b, n):
                    act.wait_ge(M.o_odd_made, 2 * s + n // 2 + 1)
                    for i in range(2):
                        e = 2 * n + i
                        part = 2 * (n // 2) + i - 1
                        if part < 0:
                            act.wait_ge(M.kept, s + 1)
                            wait(act, M.hs_ready, s)
                            out = hs_odd[:]
                        else:
                            wait(act, M.o_odd_added, 3 * (s - 1) + part + 1)
                            out = out_part[:, part, :]
                        act.activation(out, o_bank[1][:, i, :], ACT.Copy, scale=rw_out[:, b, e:e + 1]).then_inc(M.o_odd_read, 1)

                def step(s, b):
                    one, two = has(s, 1), has(s, 2)
                    keep_qk(s)
                    if one:
                        weigh_odd(s + 1, 1 - b, 1)
                    exps(s)
                    if two:
                        round_n(s + 2, b)
                    if one:
                        weigh_odd(s + 1, 1 - b, 3)
                    keep_p(s)
                    if two:
                        squares(s + 2, b)
                    if one:
                        weigh_odd(s + 1, 1 - b, 5)
                    round_a(s)
                    if two:
                        gate_exp(s + 2)
                    if one:
                        weigh_odd(s + 1, 1 - b, 7)
                    weigh_out(s, b, 1)
                    weigh_out(s, b, 3)

                for s in range(2):
                    round_n(s, s)
                    squares(s, s)
                    gate_exp(s)
                for e in range(1, E, 2):
                    weigh_odd(0, 0, e)
                parities(act, NS, step)

            @block.vector
            def _(dve):
                def norm(s, b):
                    wait(dve, M.tn_ready, s - 1)
                    wait(dve, M.squared, s - 1)
                    dve.tensor_scalar(normed[:, b, :], S.x[:, s, :], S.mean[:, bass.ds(s, 1)],
                                      S.rstd2[:, bass.ds(s, 1)], ALU.subtract, ALU.mult).then_inc(M.n_made, 1)

                def rest_n(s, b):
                    dve.wait_ge(M.nhi_ready, s + 1)
                    dve.tensor_tensor(nT[1][:, b], nT_ps, nT[0][:, b].bitcast(F32), ALU.subtract).then_inc(M.nlo_ready, 1)

                def gate_first(s):
                    dve.wait_ge(M.dots_made, s + 1)
                    dve.wait_ge(M.rooted, s + 1)
                    gate_before(S, dve, T, G, dots_ps.unsqueeze(1), M.gate_step, s)

                def gate_last(s, b):
                    wait(dve, M.odd_read, 4 * (s - 1))
                    gate_after(dve, T, rw[:, b], M.gate_exp, M.gate_step, s, M.gate_ready)

                def keep_gate(s, b):
                    dve.wait_ge(M.gate_ready, s + 1)
                    wait(dve, M.o_odd_read, 4 * (s - 1))
                    dve.tensor_copy(rw_out[:, b, :], rw[:, b, 0, :]).then_inc(M.kept, 1)

                def weigh_even(s, b, e):
                    n = 4 * s + e // 2
                    dve.wait_ge(M.q_even_made, n + 1)
                    wait(dve, M.even_added, n)
                    scale = rw[:, b, 0, e:e + 1]
                    if e == 0:
                        dve.wait_ge(M.gate_ready, s + 1)
                        wait(dve, M.attn_made, s - 1)
                        last = dve.tensor_scalar(qkv[:, b, :], q_bank[0], scale, None, ALU.mult)
                    else:
                        last = dve.scalar_tensor_tensor(qkv[:, b, :], q_bank[0], scale, qkv[:, b, :], ALU.mult, ALU.add)
                    last.then_inc(M.even_added, 1)

                def add_qkv(s, b):
                    dve.wait_ge(M.even_added, 4 * (s + 1))
                    dve.wait_ge(M.odd_added, 3 * (s + 1))
                    dve.tensor_tensor(qkv[:, b, :], qkv[:, b, :], qkv_odd[:, b, :], ALU.add).then_inc(M.qkv_ready, 1)

                def row_max(s):
                    dve.wait_ge(M.scored, s + 1)
                    wait(dve, M.exp_done, s)
                    dve.tensor_reduce(neg_max[:], scores, AX.X, ALU.max, negate=True).then_inc(M.max_ready, 1)

                def sum_scale(s):
                    dve.wait_ge(M.exp_done, s + 1)
                    dve.reciprocal(row_scale[:], row_sum[:]).then_inc(M.recip_done, 1)

                def normalize(s):
                    dve.wait_ge(M.attn_made, s + 1)
                    dve.wait_ge(M.recip_done, s + 1)
                    wait(dve, M.aT_made, s)
                    dve.tensor_scalar(attn[:], attn_ps, row_scale[:], None, ALU.mult).then_inc(M.attn_ready, 1)

                def rest_a(s):
                    dve.wait_ge(M.ahi_ready, s + 1)
                    dve.tensor_tensor(aT[1][:], aT_ps, aT[0][:].bitcast(F32), ALU.subtract).then_inc(M.alo_ready, 1)

                def first_ln(s):
                    wait(dve, M.o_even_added, 4 * (s - 1) + 1)
                    dve.tensor_scalar(y[:], S.x[:, s, :], S.mean[:, bass.ds(s, 1)], S.rstd[:, bass.ds(s, 1)],
                                      ALU.subtract, ALU.mult).then_inc(M.y_ready, 1)

                def weigh_out(s, b, n):
                    dve.wait_ge(M.o_even_made, 2 * s + n // 2 + 1)
                    for i in range(2):
                        at = 4 * s + n + i
                        if n == 0 and i == 0:
                            dve.wait_ge(M.y_ready, s + 1)
                            dve.wait_ge(M.kept, s + 1)
                            wait(dve, M.hs_ready, s)
                        wait(dve, M.o_even_added, at)
                        dve.scalar_tensor_tensor(hs_even[:], o_bank[0][:, i, :], rw_out[:, b, 2 * n + i:2 * n + i + 1],
                                                 (hs_even if n or i else y)[:], ALU.mult, ALU.add).then_inc(M.o_even_added, 1)

                def finish(s, b):
                    dve.wait_ge(M.o_even_added, 4 * (s + 1))
                    dve.wait_ge(M.o_odd_added, 3 * (s + 1))
                    wait(dve, M.x_added, s - 1)
                    wait(dve, hs_stored[b], 8 * (s - b))
                    dve.tensor_tensor(hs[:, b, :], hs_even[:], hs_odd[:], ALU.add).then_inc(M.hs_ready, 1)
                    dve.wait_ge(M.hs_ready, s + 1)
                    dve.bn_stats(seq_stats[:], hs[:, b, :]).then_inc(M.stats_done, 1)
                    dve.wait_ge(M.stats_done, s + 1)
                    dve.tensor_copy(S.stats[:, s, :], seq_stats[:])

                def step(s, b):
                    one, two, three = has(s, 1), has(s, 2), has(s, 3)
                    keep_gate(s, b)
                    if one:
                        weigh_even(s + 1, 1 - b, 0)
                    if not is_(s, 0):
                        finish(s - 1, 1 - b)
                    row_max(s)
                    if one:
                        weigh_even(s + 1, 1 - b, 2)
                    if two:
                        rest_n(s + 2, b)
                    sum_scale(s)
                    first_ln(s)
                    if one:
                        weigh_even(s + 1, 1 - b, 4)
                    normalize(s)
                    if three:
                        norm(s + 3, 1 - b)
                    if one:
                        weigh_even(s + 1, 1 - b, 6)
                    if two:
                        gate_first(s + 2)
                    rest_a(s)
                    if two:
                        gate_last(s + 2, b)
                    weigh_out(s, b, 0)
                    if one:
                        add_qkv(s + 1, 1 - b)
                    weigh_out(s, b, 2)

                norm(0, 0)
                norm(1, 1)
                for s in range(2):
                    rest_n(s, s)
                    gate_first(s)
                    gate_last(s, s)
                norm(2, 0)
                for e in range(0, E, 2):
                    weigh_even(0, 0, e)
                add_qkv(0, 0)
                parities(dve, NS, step)
                finish(NS - 1, 1)

            @block.gpsimd
            def _(pool):
                def affine(s, b):
                    pool.wait_ge(M.n_made, s + 1)
                    pool.tensor_tensor(normed[:, b, :], normed[:, b, :], ln_w[:], ALU.mult).then_inc(M.scaled, 1)
                    pool.wait_ge(M.scaled, s + 1)
                    pool.tensor_tensor(normed[:, b, :], normed[:, b, :], ln_b[:], ALU.add).then_inc(M.n_ready, 1)

                def add_odd(s, b, e):
                    n = e // 2 - 1
                    pool.wait_ge(M.odd_read, 4 * s + e // 2 + 1)
                    wait(pool, M.odd_added, 3 * s + n)
                    pool.tensor_tensor(qkv_odd[:, b, :], qkv_odd[:, b, :], qkv_part[:, n, :], ALU.add).then_inc(M.odd_added, 1)

                def add_out(s, part):
                    pool.wait_ge(M.o_odd_read, 4 * s + part + 2)
                    wait(pool, M.o_odd_added, 3 * s + part)
                    pool.tensor_tensor(hs_odd[:], hs_odd[:], out_part[:, part, :], ALU.add).then_inc(M.o_odd_added, 1)

                def add_hs(s, b):
                    pool.wait_ge(M.hs_ready, s + 1)
                    pool.tensor_tensor(S.x[:, s, :], S.x[:, s, :], hs[:, b, :], ALU.add).then_inc(M.x_added, 1)

                def step(s, b):
                    one, three = has(s, 1), has(s, 3)
                    if not is_(s, 0):
                        add_hs(s - 1, 1 - b)
                    if one:
                        add_odd(s + 1, 1 - b, 3)
                        add_odd(s + 1, 1 - b, 5)
                    if three:
                        affine(s + 3, 1 - b)
                    if one:
                        add_odd(s + 1, 1 - b, 7)
                    for part in range(3):
                        add_out(s, part)

                for s in range(2):
                    affine(s, s)
                affine(2, 0)
                for e in range(3, E, 2):
                    add_odd(0, 0, e)
                parities(pool, NS, step)
                add_hs(NS - 1, 1)
        clear(nc, own_sems)


def mixture_mlp(nc, S, L, W, G, ln_w, ln_b, hs_dram, load_next):
    NS = S.n_seq
    NP = NS // 2
    with ExitStack() as mem:
        def sb(name, shape, dt=F32):
            return mem.enter_context(nc.sbuf_tensor(f"{L}_{name}", shape, dt))

        own_sems = []

        def sem(name):
            own_sems.append(mem.enter_context(nc.semaphore(f"{L}_{name}")))
            return own_sems[-1]

        normed = sb("normed", [P, 2, C])
        square = S.bank[7].rearrange("p (s c) -> p s c", s=2)
        nT = [sb("nT_hi", [P, 2, KT, 2 * P], F32R), sb("nT_lo", [P, 2, KT, 2 * P], F32R)]
        T = gate_tiles(sb, 2)
        rw = sb("rw", [P, 2, 2, E])
        inter = sb("inter", [P, 2, 512])
        iT = [sb("inter_hi", [P, 2, KT, 2 * P], F32R), sb("inter_lo", [P, 2, KT, 2 * P], F32R)]
        hs = sb("hs", [P, 2, 2, C])
        total = sb("total", [P, 2, 2, C])
        seq_stats = sb("seq_stats", [P, 2, 6])

        nT_ps = S.bank[0].rearrange("p (k t) -> p k t", k=KT)
        dots_ps = S.bank[1][:, 0:2 * E].rearrange("p (s e) -> p s e", s=2)
        up_bank = [S.bank[2], S.bank[3], S.bank[6]]
        down_bank = [S.bank[4], S.bank[5]]

        names = ("n_made scaled n_ready squared rooted tn_ready nhi_ready nlo_ready dots_made gate_step gate_exp "
                 "gate_ready up_made inter_ready ihi_ready ilo_ready down_made added stats_done").split()
        M = named(**{n: sem(n) for n in names})
        hs_loaded = [sem("hs_even_loaded"), sem("hs_odd_loaded")]
        has = lambda p, ahead: not any(is_(p, NP - 1 - d) for d in range(ahead))

        with nc.Block() as block:
            @block.sync
            def _(sp):
                def step(p, b):
                    wait(sp, M.n_made, p - 1)
                    sp.dma_start(hs[:, b], hs_dram[bass.ds(2 * p, 2)].rearrange("s t c -> t s c")
                                 ).then_inc(hs_loaded[b], 16)
                next_loaded = load_next(sp)
                parities(sp, NP, step)
                wait(sp, *next_loaded)

            @block.tensor
            def _(pe):
                def turn_n(p):
                    pe.wait_ge(M.n_ready, p + 1)
                    wait(pe, M.nlo_ready, p)
                    for k in range(KT):
                        for s in range(2):
                            last = pe.transpose(nT_ps[:, k, s * P:(s + 1) * P], normed[:, s, k * P:(k + 1) * P], S.ident[:])
                    last.then_inc(M.tn_ready, 1)

                def dot_gate(p, b):
                    pe.wait_ge(M.nlo_ready, p + 1)
                    wait(pe, M.gate_step, GATE_STEPS * (p - 1) + 3)
                    for s in range(2):
                        for k in range(KT):
                            last = mm3(pe, dots_ps[:, s, :], [t[:, b, k, s * P:(s + 1) * P] for t in nT],
                                       [G.hi[:, k, :], G.lo[:, k, :]], k == 0, k == KT - 1)
                    last.then_inc(M.dots_made, 1)

                def up(p, b, e):
                    wait(pe, M.ihi_ready, E * p + e - 1)
                    if e == 0:
                        pe.wait_ge(M.nlo_ready, p + 1)
                    out = up_bank[e % 2].rearrange("p (m t) -> p m t", m=KT)
                    for m in range(KT):
                        for k in range(KT):
                            last = mm3(pe, out[:, m, :], [w[:, 0, e, k, m * P:(m + 1) * P] for w in (W.hi, W.lo)],
                                       [t[:, b, k, :] for t in nT], k == 0, k == KT - 1)
                    last.then_inc(M.up_made, 1)

                def down(p, e):
                    pe.wait_ge(M.ilo_ready, E * p + e + 1)
                    wait(pe, M.added, 2 * (E * p + e - 1))
                    out = down_bank[e % 2].rearrange("p (s c) -> p s c", s=2)
                    for s in range(2):
                        for k in range(KT):
                            last = mm3(pe, out[:, s, :], [t[:, e % 2, k, s * P:(s + 1) * P] for t in iT],
                                       [w[:, 1, e, k, :] for w in (W.hi, W.lo)], k == 0, k == KT - 1)
                    last.then_inc(M.down_made, 1)

                def step(p, b):
                    for e in range(E):
                        up(p, b, e)
                        if e >= 1:
                            down(p, e - 1)
                        elif not is_(p, 0):
                            down(p - 1, E - 1)
                        if e == 1 and has(p, 1):
                            turn_n(p + 1)
                        if e == 4 and has(p, 1):
                            dot_gate(p + 1, 1 - b)

                turn_n(0)
                dot_gate(0, 0)
                parities(pe, NP, step)
                down(NP - 1, E - 1)

            @block.scalar
            def _(act):
                def round_n(p, b):
                    act.wait_ge(M.tn_ready, p + 1)
                    wait(act, M.up_made, E * (p - 1))
                    act.activation(nT[0][:, b], nT_ps, ACT.Copy).then_inc(M.nhi_ready, 1)

                def squares(p):
                    act.wait_ge(M.n_ready, p + 1)
                    wait(act, M.gate_step, GATE_STEPS * (p - 1) + 3)
                    for s in range(2):
                        last = act.activation(square[:, s], normed[:, s, :], ACT.Square, accum_out=T.square_sum[:, s:s + 1])
                    last.then_inc(M.squared, 1)
                    act.wait_ge(M.squared, p + 1)
                    act.activation(T.norm[:], T.square_sum[:], ACT.Sqrt).then_inc(M.rooted, 1)

                def gate_exp(p):
                    act.wait_ge(M.gate_step, GATE_STEPS * p + GATE_BEFORE)
                    act.activation(T.exp[:], T.shifted[:], ACT.Exp).then_inc(M.gate_exp, 1)

                def gelu(p, e):
                    n = E * p + e
                    act.wait_ge(M.up_made, n + 1)
                    wait(act, M.ilo_ready, n - 1)
                    wait(act, M.down_made, n - 1)
                    act.activation(inter[:, e % 2], up_bank[e % 2], ACT.Gelu).then_inc(M.inter_ready, 1)
                    act.activation(iT[0][:, e % 2].rearrange("p k t -> p (k t)"), up_bank[e % 2], ACT.Gelu).then_inc(M.ihi_ready, 1)

                def step(p, b):
                    for e in range(E):
                        gelu(p, e)
                        if has(p, 1):
                            if e == 1:
                                round_n(p + 1, 1 - b)
                            if e == 3:
                                squares(p + 1)
                            if e == 5:
                                gate_exp(p + 1)

                round_n(0, 0)
                squares(0)
                gate_exp(0)
                parities(act, NP, step)

            @block.vector
            def _(dve):
                def norm(p, b):
                    dve.wait_ge(hs_loaded[b], 8 * (p - b) + 16)
                    wait(dve, M.tn_ready, p)
                    wait(dve, M.squared, p)
                    for s in range(2):
                        n = 2 * p + s
                        last = dve.tensor_scalar(normed[:, s, :], hs[:, b, s, :], S.mean[:, bass.ds(n, 1)],
                                                 S.rstd[:, bass.ds(n, 1)], ALU.subtract, ALU.mult)
                    last.then_inc(M.n_made, 1)

                def rest_n(p, b):
                    dve.wait_ge(M.nhi_ready, p + 1)
                    dve.tensor_tensor(nT[1][:, b], nT_ps, nT[0][:, b].bitcast(F32), ALU.subtract).then_inc(M.nlo_ready, 1)

                def gate_first(p):
                    dve.wait_ge(M.dots_made, p + 1)
                    dve.wait_ge(M.rooted, p + 1)
                    gate_before(S, dve, T, G, dots_ps, M.gate_step, p)

                def gate_last(p, b):
                    gate_after(dve, T, rw[:, b], M.gate_exp, M.gate_step, p, M.gate_ready)

                def rest_i(p, e):
                    n = E * p + e
                    dve.wait_ge(M.ihi_ready, n + 1)
                    dve.tensor_tensor(iT[1][:, e % 2].rearrange("p k t -> p (k t)"), inter[:, e % 2],
                                      iT[0][:, e % 2].rearrange("p k t -> p (k t)").bitcast(F32), ALU.subtract
                                      ).then_inc(M.ilo_ready, 1)

                def add(p, b, e):
                    n = E * p + e
                    dve.wait_ge(M.down_made, n + 1)
                    if e == 0:
                        dve.wait_ge(M.gate_ready, p + 1)
                    wait(dve, M.added, 2 * n)
                    out = down_bank[e % 2].rearrange("p (s c) -> p s c", s=2)
                    for s in range(2):
                        dve.scalar_tensor_tensor(total[:, b, s, :], out[:, s, :], rw[:, b, s, e:e + 1],
                                                 total[:, b, s, :] if e else S.x[:, 2 * p + s, :],
                                                 ALU.mult, ALU.add).then_inc(M.added, 1)

                def finish(p, b):
                    dve.wait_ge(M.added, 2 * E * (p + 1))
                    for s in range(2):
                        dve.bn_stats(seq_stats[:, s, :], total[:, b, s, :]).then_inc(M.stats_done, 1)
                    dve.tensor_copy(S.x[:, bass.ds(2 * p, 2), :], total[:, b])
                    dve.wait_ge(M.stats_done, 2 * p + 2)
                    dve.tensor_copy(S.stats[:, bass.ds(2 * p, 2), :], seq_stats[:])

                def step(p, b):
                    for e in range(E):
                        rest_i(p, e)
                        if e >= 1:
                            add(p, b, e - 1)
                        elif not is_(p, 0):
                            add(p - 1, 1 - b, E - 1)
                        if e == 1:
                            if not is_(p, 0):
                                finish(p - 1, 1 - b)
                            if has(p, 1):
                                rest_n(p + 1, 1 - b)
                        if e == 4 and has(p, 1):
                            gate_first(p + 1)
                        if e == 6:
                            if has(p, 1):
                                gate_last(p + 1, 1 - b)
                            if has(p, 2):
                                norm(p + 2, b)

                norm(0, 0)
                rest_n(0, 0)
                gate_first(0)
                gate_last(0, 0)
                norm(1, 1)
                parities(dve, NP, step)
                add(NP - 1, 1, E - 1)
                finish(NP - 1, 1)

            @block.gpsimd
            def _(pool):
                def affine(p):
                    pool.wait_ge(M.n_made, p + 1)
                    wide = lambda t: t[:].unsqueeze(1).broadcast_to([P, 2, C])
                    pool.tensor_tensor(normed[:], normed[:], wide(ln_w), ALU.mult).then_inc(M.scaled, 1)
                    pool.wait_ge(M.scaled, p + 1)
                    pool.tensor_tensor(normed[:], normed[:], wide(ln_b), ALU.add).then_inc(M.n_ready, 1)

                def step(p, b):
                    if has(p, 2):
                        affine(p + 2)

                affine(0)
                affine(1)
                parities(pool, NP, step)
        clear(nc, own_sems)


def routed_experts(nc, S, L, W, R, out_dram):
    NP = S.n_seq // 2
    SLOTS = E
    with ExitStack() as mem:
        def sb(name, shape, dt=F32):
            return mem.enter_context(nc.sbuf_tensor(f"{L}_{name}", shape, dt))

        own_sems = []

        def sem(name):
            own_sems.append(mem.enter_context(nc.semaphore(f"{L}_{name}")))
            return own_sems[-1]

        normed = sb("normed", [P, 2, C])
        nT = [sb("nT_hi", [P, 2, KT, 2 * P], F32R), sb("nT_lo", [P, 2, KT, 2 * P], F32R)]
        logit, tied, first, exp = (sb(n, [P, 2, E]) for n in ("logit", "tied", "first", "exp"))
        top, order, weight = (sb(n, [P, 2]) for n in ("top", "order", "weight"))
        gate = sb("gate", [P, 2, 2, P])
        gateT = sb("gateT", [P, 2, 2, P])
        even, odd = sb("even", [P, 2, C]), sb("odd", [P, 2, C])
        part = sb("part", [P, 2, 3, C])
        result = sb("result", [P, 2, 2, C])

        nT_ps = S.bank[0].rearrange("p (k t) -> p k t", k=KT)
        dots_ps = S.bank[1][:, 0:2 * E].rearrange("p (s e) -> p s e", s=2)
        gateT_ps = S.bank[2][:, 0:2 * P].rearrange("p (s t) -> p s t", s=2)
        bias_ps = S.bank[3].rearrange("p (s c) -> p s c", s=2)
        y_bank = [S.bank[4 + n].rearrange("p (e c) -> p e c", e=2) for n in range(4)]

        names = ("n_ready tn_ready nhi_ready nlo_ready dots_made dots_read step exp_done gate_cleared gate_ready gT_made gT_ready "
                 "bias_made even_made odd_made even_added odd_read odd_added result_ready").split()
        M = named(**{n: sem(n) for n in names})
        stored = [sem("even_stored"), sem("odd_stored")]
        has = lambda p, ahead: not any(is_(p, NP - 1 - d) for d in range(ahead))
        STEPS = 9

        with nc.Block() as block:
            @block.sync
            def _(sp):
                def step(p, b):
                    sp.wait_ge(M.result_ready, 2 * p + 2)
                    sp.dma_start(out_dram[bass.ds(2 * p, 2)].rearrange("s t c -> t s c"), result[:, b]
                                 ).then_inc(stored[b], 16)
                parities(sp, NP, step)
                for b in range(2):
                    sp.wait_ge(stored[b], 8 * NP)

            @block.tensor
            def _(pe):
                def turn_n(p):
                    pe.wait_ge(M.n_ready, p + 1)
                    wait(pe, M.nlo_ready, p)
                    for k in range(KT):
                        for s in range(2):
                            last = pe.transpose(nT_ps[:, k, s * P:(s + 1) * P], normed[:, s, k * P:(k + 1) * P], S.ident[:])
                    last.then_inc(M.tn_ready, 1)

                def dot_router(p, b):
                    pe.wait_ge(M.nlo_ready, p + 1)
                    wait(pe, M.dots_read, p)
                    for s in range(2):
                        for k in range(KT):
                            last = mm3(pe, dots_ps[:, s, :], [t[:, b, k, s * P:(s + 1) * P] for t in nT],
                                       [R.hi[:, k, :], R.lo[:, k, :]], k == 0, k == KT - 1)
                    last.then_inc(M.dots_made, 1)

                def turn_gate(p, b):
                    pe.wait_ge(M.gate_ready, p + 1)
                    wait(pe, M.gT_ready, p)
                    for s in range(2):
                        last = pe.transpose(gateT_ps[:, s, :], gate[:, b, s, :], S.ident[:])
                    last.then_inc(M.gT_made, 1)

                def bias(p, b):
                    pe.wait_ge(M.gT_ready, p + 1)
                    wait(pe, M.even_added, 10 * p - 4)
                    for s in range(2):
                        last = pe.matmul(bias_ps[:, s, :], gateT[:, b, s, :], R.expert_b[:], start=True, stop=True)
                    last.then_inc(M.bias_made, 1)

                def expert(p, b, t):
                    s, n = divmod(t, 4)
                    if n % 2 == 0:
                        wait(pe, M.even_added, 10 * p + 5 * s - 5 + n + 3)
                    else:
                        wait(pe, M.odd_read, 8 * p + 4 * s - 4 + n + 1)
                    for k in range(KT):
                        last = mm3(pe, S.bank[4 + n], [t_[:, b, k, s * P:(s + 1) * P] for t_ in nT],
                                   [w[:, k, 2 * n:2 * n + 2, :].rearrange("p e c -> p (e c)") for w in (W.hi, W.lo)],
                                   k == 0, k == KT - 1)
                    last.then_inc((M.even_made, M.odd_made)[n % 2], 1)

                def step(p, b):
                    bias(p, b)
                    for t in range(SLOTS):
                        expert(p, b, t)
                        if has(p, 1):
                            if t == 0:
                                turn_n(p + 1)
                            if t == 2:
                                dot_router(p + 1, 1 - b)
                            if t == 7:
                                turn_gate(p + 1, 1 - b)

                turn_n(0)
                dot_router(0, 0)
                turn_gate(0, 0)
                parities(pe, NP, step)

            @block.scalar
            def _(act):
                def round_n(p, b):
                    act.wait_ge(M.tn_ready, p + 1)
                    wait(act, M.odd_made, 4 * (p - 1))
                    act.activation(nT[0][:, b], nT_ps, ACT.Copy).then_inc(M.nhi_ready, 1)

                def gate_exp(p):
                    act.wait_ge(M.step, STEPS * p + 4)
                    act.activation(exp[:], logit[:], ACT.Exp).then_inc(M.exp_done, 1)

                def keep_gate(p, b):
                    act.wait_ge(M.gT_made, p + 1)
                    wait(act, M.bias_made, p - 1)
                    act.activation(gateT[:, b], gateT_ps, ACT.Copy).then_inc(M.gT_ready, 1)

                def weigh(p, b, t):
                    s, n = divmod(t, 4)
                    q = 2 * p + s
                    act.wait_ge(M.odd_made, 2 * q + n // 2 + 1)
                    for i in range(2):
                        k = 2 * (n // 2) + i - 1
                        if k < 0:
                            act.wait_ge(M.gate_ready, p + 1)
                            wait(act, M.result_ready, q - 1)
                            out = odd[:, s, :]
                        else:
                            wait(act, M.odd_added, 3 * (q - 2) + k + 1)
                            out = part[:, s, k, :]
                        act.activation(out, y_bank[n][:, i, :], ACT.Copy, scale=gate[:, b, s, 2 * n + i:2 * n + i + 1]
                                       ).then_inc(M.odd_read, 1)

                def step(p, b):
                    for t in range(SLOTS):
                        if t % 2:
                            weigh(p, b, t)
                        if has(p, 1):
                            if t == 0:
                                round_n(p + 1, 1 - b)
                            if t == 4:
                                gate_exp(p + 1)
                            if t == 7:
                                keep_gate(p + 1, 1 - b)

                round_n(0, 0)
                gate_exp(0)
                keep_gate(0, 0)
                parities(act, NP, step)

            @block.vector
            def _(dve):
                def norm(p):
                    wait(dve, M.tn_ready, p)
                    for s in range(2):
                        n = 2 * p + s
                        last = dve.tensor_scalar(normed[:, s, :], S.x[:, n, :], S.mean[:, bass.ds(n, 1)],
                                                 S.rstd[:, bass.ds(n, 1)], ALU.subtract, ALU.mult)
                    last.then_inc(M.n_ready, 1)

                def rest_n(p, b):
                    dve.wait_ge(M.nhi_ready, p + 1)
                    dve.tensor_tensor(nT[1][:, b], nT_ps, nT[0][:, b].bitcast(F32), ALU.subtract).then_inc(M.nlo_ready, 1)

                wide = lambda t: t[:].unsqueeze(2).broadcast_to([P, 2, E])

                def chain(p, at):
                    n = [at]

                    def then(ins):
                        n[0] += 1
                        ins.then_inc(M.step, 1)
                        dve.wait_ge(M.step, STEPS * p + n[0])
                    return then

                def gate_first(p):
                    then = chain(p, 0)
                    tt = dve.tensor_tensor
                    dve.wait_ge(M.dots_made, p + 1)
                    tt(logit[:], dots_ps, R.bias[:].unsqueeze(1).broadcast_to([P, 2, E]), ALU.add).then_inc(M.dots_read, 1)
                    dve.wait_ge(M.dots_read, p + 1)
                    then(dve.tensor_reduce(top[:], logit[:], AX.X, ALU.max))
                    then(tt(tied[:], logit[:], wide(top), ALU.is_ge))
                    then(tt(tied[:], tied[:], S.rank[:], ALU.mult))
                    then(tt(logit[:], logit[:], wide(top), ALU.subtract))
                    then(dve.tensor_reduce(order[:], tied[:], AX.X, ALU.max))
                    then(tt(first[:], S.rank[:], wide(order), ALU.is_equal))

                def gate_last(p, b):
                    then = chain(p, 6)
                    dve.wait_ge(M.exp_done, p + 1)
                    then(dve.tensor_reduce(weight[:], exp[:], AX.X, ALU.add))
                    then(dve.reciprocal(weight[:], weight[:]))
                    wait(dve, M.gT_made, p - 1)
                    wait(dve, M.odd_read, 8 * (p - 1))
                    then(dve.tensor_tensor(first[:], first[:], wide(weight), ALU.mult))
                    dve.tensor_copy(gate[:, b, :, 0:E], first[:]).then_inc(M.gate_ready, 1)

                def start(p, s):
                    q = 2 * p + s
                    dve.wait_ge(M.bias_made, p + 1)
                    wait(dve, M.result_ready, q - 1)
                    dve.tensor_tensor(even[:, s, :], bias_ps[:, s, :], S.x[:, q, :], ALU.add).then_inc(M.even_added, 1)

                def weigh(p, b, t):
                    s, n = divmod(t, 4)
                    q = 2 * p + s
                    dve.wait_ge(M.even_made, 2 * q + n // 2 + 1)
                    for i in range(2):
                        dve.wait_ge(M.even_added, 5 * q + n + i + 1)
                        dve.scalar_tensor_tensor(even[:, s, :], y_bank[n][:, i, :], gate[:, b, s, 2 * n + i:2 * n + i + 1],
                                                 even[:, s, :], ALU.mult, ALU.add).then_inc(M.even_added, 1)

                def finish(p, b, s):
                    q = 2 * p + s
                    dve.wait_ge(M.even_added, 5 * q + 5)
                    dve.wait_ge(M.odd_added, 3 * q + 3)
                    wait(dve, stored[b], 8 * (p - b))
                    dve.tensor_tensor(result[:, b, s, :], even[:, s, :], odd[:, s, :], ALU.add).then_inc(M.result_ready, 1)

                def step(p, b):
                    for t in range(SLOTS):
                        if t % 4 == 0:
                            start(p, t // 4)
                        if t % 2 == 0:
                            weigh(p, b, t)
                        if t == 1:
                            if not is_(p, 0):
                                finish(p - 1, 1 - b, 1)
                            if has(p, 1):
                                rest_n(p + 1, 1 - b)
                        if t == 4 and has(p, 1):
                            gate_first(p + 1)
                        if t == 5:
                            finish(p, b, 0)
                            if has(p, 2):
                                norm(p + 2)
                        if t == 6 and has(p, 1):
                            gate_last(p + 1, 1 - b)

                dve.memset(gate[:], 0.0).then_inc(M.gate_cleared, 1)
                norm(0)
                rest_n(0, 0)
                gate_first(0)
                dve.wait_ge(M.gate_cleared, 1)
                gate_last(0, 0)
                norm(1)
                parities(dve, NP, step)
                finish(NP - 1, 1, 1)

            @block.gpsimd
            def _(pool):
                def step(p, b):
                    for s in range(2):
                        q = 2 * p + s
                        for k in range(3):
                            pool.wait_ge(M.odd_read, 4 * q + k + 2)
                            wait(pool, M.odd_added, 3 * q + k)
                            pool.tensor_tensor(odd[:, s, :], odd[:, s, :], part[:, s, k, :], ALU.add).then_inc(M.odd_added, 1)
                parities(pool, NP, step)
        clear(nc, own_sems)


def load_mixture_attention_raw(dma, S, q, k, v, o, done):
    qkv = S.raw[:, 0:E * KT * 3 * HID].rearrange("p (e k w) -> p e k w", e=E, k=KT)
    for n, w in enumerate((q, k, v)):
        for e in range(E):
            dma.dma_start(qkv[:, e, :, n * HID:(n + 1) * HID], w[e].rearrange("(k p) h -> p k h", p=P)).then_inc(done, 16)
    out = S.raw[:, E * KT * 3 * HID:].rearrange("p (e c) -> p e c", e=E)
    dma.dma_start(out, o.rearrange("e h c -> h e c")).then_inc(done, 16)
    return 16 * (3 * E + 1)


def load_mixture_mlp_raw(dma, S, w1, w2, done):
    raw = S.raw[:].rearrange("p (w e k c) -> p w e k c", w=2, e=E, k=KT)
    for n, w in enumerate((w1, w2)):
        for e in range(E):
            dma.dma_start(raw[:, n, e], w[e].rearrange("(k p) c -> p k c", p=P)).then_inc(done, 16)
    return 16 * 2 * E


def load_experts_raw(dma, S, w, done):
    raw = S.raw[:, 0:E * KT * C].rearrange("p (e o d) -> p e o d", e=E, o=KT)
    for e in range(E):
        dma.dma_start(raw[:, e], w[e].rearrange("(o p) d -> p o d", p=P)).then_inc(done, 16)
    return 16 * E


def expert_weights(nc, S, name, W, R):
    raw = S.raw[:, 0:E * KT * C].rearrange("p (e o d) -> p e o d", e=E, o=KT)
    split_weights(nc, S, f"{name}_router", [(R.hi[:], R.lo[:], R.raw[:])])

    def turn(pe, e):
        out = S.bank[e % len(S.bank)].rearrange("p (k c) -> p k c", k=KT)
        for k in range(KT):
            for o in range(KT):
                last = pe.transpose(out[:, k, o * P:(o + 1) * P], raw[:, e, o, k * P:(k + 1) * P], S.ident[:])
        return last

    split_weights(nc, S, name, [
        (W.hi[:, :, e, :], W.lo[:, :, e, :], S.bank[e % len(S.bank)].rearrange("p (k c) -> p k c", k=KT))
        for e in range(E)], turn)


def load_attention_raw(dma, S, W4, transposed, done):
    raw = S.raw[:, 0:4 * KT * C].rearrange("p (w k c) -> p w k c", w=4, k=KT)
    n = 0
    for w in range(4):
        if w == 3 and transposed:
            to = raw[:, w].rearrange("p o (k i e d) -> p o k e i d", k=KT, e=2, i=UH)
            columns = W4[w].rearrange("(o p) (k e i d) -> p o k e i d", p=P, k=KT, e=2, i=UH)
            for o in range(KT):
                for k in range(KT):
                    for e in range(2):
                        dma.dma_start(to[:, o, k, e], columns[:, o, k, e]).then_inc(done, 16)
                        n += 1
        elif w < 3:
            dma.dma_start(raw[:, w], W4[w].rearrange("(k p) c -> p k c", p=P)).then_inc(done, 16)
            n += 1
        else:
            rows = W4[w].rearrange("(k e i d) c -> e i d k c", k=KT, e=2, i=UH)
            for e in range(2):
                for i in range(UH):
                    dma.dma_start(raw[32 * i + D * e:32 * i + D * (e + 1), w], rows[e, i]).then_inc(done, 16)
                    n += 1
    return 16 * n


def setup(nc, S, a, consts):
    chunk = 8
    chunks = S.n_seq // chunk
    const_in, raw_in = S.sem("constants_loaded"), S.sem("raw0_loaded")
    x_in = [S.sem(f"x{n}_loaded") for n in range(chunks)]
    stats_done, cleared = S.sem("first_stats_done"), S.sem("expert_bias_cleared")
    with nc.Block() as block:
        @block.sync
        def _(sp):
            for n in range(chunks):
                sp.dma_start(S.x[:, n * chunk:(n + 1) * chunk, :],
                             a["x"][n * chunk:(n + 1) * chunk].rearrange("s t c -> t s c")).then_inc(x_in[n], 16)

        @block.scalar
        def _(act):
            total = load_attention_raw(act, S, [a[f"L0_xattn_{n}"] for n in ("Wq", "Wk", "Wv", "Wo")], True, raw_in)
            n = 0
            for name, tile in S.const_tiles:
                act.dma_start(tile[:], consts[name]).then_inc(const_in, 16)
                n += 16
            for tile, row in S.row_tiles:
                act.dma_start(tile, a[row].partition_broadcast(P)).then_inc(const_in, 16)
                n += 16
            for tile, name in S.column_tiles:
                act.dma_start(tile, a[name].rearrange("(k p) -> p k", p=P),
                              allow_slow_non_contiguous=True).then_inc(const_in, 16)
                n += 16
            for tile, source in S.sim_tiles:
                act.dma_start(tile, source, allow_slow_non_contiguous=True).then_inc(const_in, 16)
                n += 16
            act.wait_ge(cleared, 1)
            act.dma_start(S.expert_b[0:E, :], a["L1_ffn_expert_b"]).then_inc(const_in, 16)
            n += 16
            act.wait_ge(raw_in, total)
            act.wait_ge(const_in, n)

        @block.vector
        def _(dve):
            dve.memset(S.expert_b[:], 0.0).then_inc(cleared, 1)
            for n in range(chunks):
                dve.wait_ge(x_in[n], 16)
                with dve.Fori(n * chunk, (n + 1) * chunk) as s:
                    last = dve.bn_stats(S.stats[:, s, :], S.x[:, s, :])
                    last.then_inc(stats_done, 1)
            dve.wait_ge(stats_done, S.n_seq)


def program(nc, a, consts, out, phases=5):
    with ExitStack() as mem:
        def sb(name, shape, dt=F32):
            return mem.enter_context(nc.sbuf_tensor(name, shape, dt))

        S = Named()
        S.n_seq = a["x"].shape[0]
        S.sem = lambda name: mem.enter_context(nc.semaphore(name))
        S.bank = [mem.enter_context(nc.psum_tensor(f"bank{n}", [P, 512], F32))[:] for n in range(8)]
        S.x = sb("x_all", [P, S.n_seq, C])
        S.stats = sb("stats", [P, S.n_seq, 6])
        S.mean, S.var, S.root = (sb(n, [P, S.n_seq]) for n in ("mean", "var", "root"))
        S.rstd, S.rstd2 = sb("rstd", [P, S.n_seq]), sb("rstd2", [P, S.n_seq])
        S.raw = sb("raw_weights", [P, 2 * E * KT * C])

        S.ident = sb("ident", [P, P])
        S.ident_bf = sb("ident_bf", [P, P], BF16)
        S.hidden_bf = sb("hidden_bf", [P, UH * P], BF16)
        S.count_bf, S.plain_bf = sb("count_bf", [P, UNITS, P], BF16), sb("plain_bf", [P, UNITS, P], BF16)
        S.ones_half = sb("ones_half", [P, 2, 32])
        S.head_rows = sb("head_rows", [P, P // D])
        S.rank = sb("rank", [P, 2, E])
        S.const_tiles = [("ident", S.ident), ("ident_bf", S.ident_bf), ("hidden_bf", S.hidden_bf),
                         ("count_bf", S.count_bf), ("plain_bf", S.plain_bf), ("ones_half", S.ones_half),
                         ("head_rows", S.head_rows), ("rank", S.rank)]
        S.row_tiles, S.column_tiles, S.sim_tiles = [], [], []

        def row(name, width):
            tile = sb(f"{name}_row", [P, width])
            S.row_tiles.append((tile[:], name))
            return tile

        def column(name):
            tile = sb(f"{name}_column", [P, KT])
            S.column_tiles.append((tile[:], name))
            return tile

        def gate(name):
            G = named(sim=sb(f"{name}_sim", [P, KT, E]), work=sb(f"{name}_work", [P, KT, E]),
                                norm=sb(f"{name}_norm", [P, E]), hi=sb(f"{name}_hi", [P, KT, E], F32R),
                                lo=sb(f"{name}_lo", [P, KT, E], F32R), gates=row(f"{name}_gates", E))
            S.sim_tiles.append((G.sim[:], a[f"{name}_sim"].rearrange("(k p) e -> p k e", p=P)))
            return G

        B = {L: named(q=column(f"{L}_bq"), k=column(f"{L}_bk"), v=row(f"{L}_bv", C), o=row(f"{L}_bo", C))
             for L in ("L0_xattn", "L1_xattn")}
        ln1 = row("L0_ffn_ln1_w", C), row("L0_ffn_ln1_b", C)
        ln2 = row("L0_ffn_ln2_w", C), row("L0_ffn_ln2_b", C)
        attention_gate, mlp_gate = gate("L0_ffn_smha"), gate("L0_ffn_moe")
        R = named(raw=sb("router", [P, KT, E]), hi=sb("router_hi", [P, KT, E], F32R),
                            lo=sb("router_lo", [P, KT, E], F32R), bias=row("L1_ffn_router_b", E),
                            expert_b=sb("expert_bias", [P, C]))
        S.sim_tiles.extend((R.raw[:, k, :], a["L1_ffn_router_w"][:, k * P:(k + 1) * P].rearrange("e p -> p e"))
                           for k in range(KT))
        S.expert_b = R.expert_b
        hs_dram = nc.dram_tensor("x_plus_hs", a["x"].shape, F32).ap()

        def weights(own, name, shape):
            return [own.enter_context(nc.sbuf_tensor(f"{name}_{part}", shape, F32R)) for part in ("hi", "lo")]

        names = ("Wq", "Wk", "Wv", "Wo")
        loaded = [S.sem(f"raw{n}_loaded") for n in range(1, 5)]
        load_next = [
            lambda dma: (loaded[0], load_mixture_attention_raw(
                dma, S, *(a[f"L0_ffn_{n}_proj"] for n in "qkvo"), loaded[0])),
            lambda dma: (loaded[1], load_mixture_mlp_raw(dma, S, a["L0_ffn_w1"], a["L0_ffn_w2"], loaded[1])),
            lambda dma: (loaded[2], load_attention_raw(dma, S, [a[f"L1_xattn_{n}"] for n in names], False, loaded[2])),
            lambda dma: (loaded[3], load_experts_raw(dma, S, a["L1_ffn_expert_w"], loaded[3])),
        ]

        setup(nc, S, a, consts)

        with ExitStack() as own:
            W = Named()
            W.hi, W.lo = weights(own, "W0", [P, 4, KT, C])
            attention_weights(nc, S, "W0", W, True)
            ln_scales(nc, S, "ln0")
            attention(nc, S, "L0", a["ctx_1024"], W, B["L0_xattn"], S.count_bf, load_next[0])

        if phases >= 2:
            with ExitStack() as own:
                W = Named()
                W.hi, W.lo = weights(own, "W1", [P, E, KT, 3 * HID])
                W.o_hi, W.o_lo = weights(own, "W1_o", [P, E, C])
                raw = S.raw[:, 0:E * KT * 3 * HID].rearrange("p (e k w) -> p e k w", e=E, k=KT)
                raw_o = S.raw[:, E * KT * 3 * HID:].rearrange("p (e c) -> p e c", e=E)
                split_weights(nc, S, "W1", [(W.hi[:, e], W.lo[:, e], raw[:, e]) for e in range(E)]
                              + [(W.o_hi[:, e:e + 4], W.o_lo[:, e:e + 4], raw_o[:, e:e + 4]) for e in (0, 4)])
                gate_weights(nc, S, "gate1", attention_gate)
                ln_scales(nc, S, "ln1", twice=True)
                mixture_attention(nc, S, "M1", W, attention_gate, *ln1, hs_dram, load_next[1])

        if phases >= 3:
            with ExitStack() as own:
                W = Named()
                W.hi, W.lo = weights(own, "W2", [P, 2, E, KT, C])
                raw = S.raw[:].rearrange("p (w e k c) -> p w e k c", w=2, e=E, k=KT)
                split_weights(nc, S, "W2", [(W.hi[:, w, e:e + 2], W.lo[:, w, e:e + 2], raw[:, w, e:e + 2])
                                            for w in range(2) for e in range(0, E, 2)])
                gate_weights(nc, S, "gate2", mlp_gate)
                ln_scales(nc, S, "ln2")
                mixture_mlp(nc, S, "M2", W, mlp_gate, *ln2, hs_dram, load_next[2])

        if phases >= 4:
            with ExitStack() as own:
                W = Named()
                W.hi, W.lo = weights(own, "W3", [P, 4, KT, C])
                attention_weights(nc, S, "W3", W, False)
                ln_scales(nc, S, "ln3")
                attention(nc, S, "L1", a["ctx_1024"], W, B["L1_xattn"], S.plain_bf, load_next[3])

        if phases >= 5:
            with ExitStack() as own:
                W = Named()
                W.hi, W.lo = weights(own, "W4", [P, KT, E, C])
                expert_weights(nc, S, "W4", W, R)
                ln_scales(nc, S, "ln4")
                routed_experts(nc, S, "M4", W, R, out)
        else:
            store(nc, S, out)


def store(nc, S, out):
    stored = S.sem("out_stored")
    with nc.Block() as block:
        @block.sync
        def _(sp):
            sp.dma_start(out.rearrange("s t c -> t s c"), S.x[:]).then_inc(stored, 16)
            sp.wait_ge(stored, 16)


def kernel(**inputs):
    import concourse.bacc as bacc
    from concourse.bass_utils import run_bass_kernel_spmd
    nc = bacc.Bacc("TRN2", target_bir_lowering=False, num_devices=1)
    arrays, a, consts = {}, {}, {}
    for group, source in ((a, inputs), (consts, host_constants())):
        for name, value in source.items():
            value = np.ascontiguousarray(value)
            arrays[f"in_{name}"] = value
            group[name] = nc.dram_tensor(f"in_{name}", value.shape, mybir.dt.from_np(value.dtype), kind="ExternalInput").ap()
    out = nc.dram_tensor("out", a["x"].shape, F32, kind="ExternalOutput").ap()
    program(nc, a, consts, out)
    return run_bass_kernel_spmd(nc, [arrays], core_ids=[0]).results[0]["out"]
```

```python
from collections import namedtuple
from contextlib import ExitStack

import numpy as np

import concourse.bass as bass
from concourse import mybir

F32 = mybir.dt.float32
F32R = mybir.dt.float32r
BF16 = mybir.dt.bfloat16
ALU = mybir.AluOpType
ACT = mybir.ActivationFunctionType
AX = mybir.AxisListType

P = 128
C = 256
KT = C // P
H = 16
D = C // H
E = 8
HID = 128
UH = 4
UNITS = H // UH
LN_EPS = 1e-5
HIDDEN = 1e30
LARGEST = 3e38


class Named:
    pass


def named(**values):
    return namedtuple("named", values)(*values.values())


def wait(eng, sem, value):
    if isinstance(value, int) and value <= 0:
        return
    eng.wait_ge(sem, value)


def is_(index, value):
    return isinstance(index, int) and index == value


def mm3(pe, out, left, right, first, last):
    pe.matmul(out, left[0], right[0], start=first, stop=False)
    pe.matmul(out, left[1], right[0], start=False, stop=False)
    return pe.matmul(out, left[0], right[1], start=False, stop=last)


def clear(nc, sems):
    with nc.Block() as block:
        @block.sync
        def _(sp):
            for sem in sems:
                sp.sem_clear(sem)


def host_constants():
    k = np.arange(P)
    causal = k[:, None] <= k[None, :]
    count = np.zeros((P, UNITS, P), np.float32)
    for j in range(UNITS):
        same2 = (k[:, None] % 2 == j // 2) & (k[None, :] % 2 == j // 2)
        same4 = (k[:, None] % 4 == j) & (k[None, :] % 4 == j)
        count[:, j, :] = causal * (1.0 + same2 + same4)
    hidden = np.where(causal.T, 0.0, HIDDEN).astype(np.float32)
    ones_half = np.zeros((P, 2, 32), np.float32)
    ones_half[:, 0, :D] = 1.0
    ones_half[:, 1, D:] = 1.0
    head_rows = (k[:, None] // D == np.arange(P // D)[None, :]) * np.float32(-D ** -0.5)
    bf = np.dtype("bfloat16")
    return {
        "ident": np.eye(P, dtype=np.float32),
        "hidden": hidden,
        "count_bf": count.astype(bf),
        "ones_half": ones_half,
        "head_rows": head_rows.astype(np.float32),
        "minus_half": np.full((P, 2), -0.5, np.float32),
        "euler": np.full((P, 2, E), np.e, np.float32),
        "rank": np.tile(np.arange(E, 0, -1, dtype=np.float32), (P, 2, 1)),
    }


def split_weights(nc, S, name, pieces, transposes=None):
    turned = S.sem(f"{name}_turned")
    hi_done = S.sem(f"{name}_hi")
    lo_done = S.sem(f"{name}_lo")
    with nc.Block() as block:
        if transposes:
            @block.tensor
            def _(pe):
                for n in range(len(pieces)):
                    wait(pe, lo_done, n - len(S.bank) + 1)
                    transposes(pe, n).then_inc(turned, 1)

        @block.scalar
        def _(act):
            for n, (hi, _, src) in enumerate(pieces):
                if transposes:
                    act.wait_ge(turned, n + 1)
                act.activation(hi, src, ACT.Copy).then_inc(hi_done, 1)

        @block.vector
        def _(dve):
            for n, (hi, lo, src) in enumerate(pieces):
                dve.wait_ge(hi_done, n + 1)
                dve.tensor_tensor(lo, src, hi.bitcast(F32), ALU.subtract).then_inc(lo_done, 1)


def ln_scales(nc, S, name, twice=False):
    step = S.sem(f"{name}_step")
    root = S.sem(f"{name}_root")
    even, odd = S.stats[:, :, 0:3], S.stats[:, :, 3:6]
    with nc.Block() as block:
        @block.vector
        def _(dve):
            n = [0]

            def then(ins):
                n[0] += 1
                ins.then_inc(step, 1)
                dve.wait_ge(step, n[0])

            diff, var = S.rstd2, S.var
            then(dve.tensor_tensor(S.mean[:], even[:, :, 1], odd[:, :, 1], ALU.add))
            then(dve.tensor_tensor(diff[:], even[:, :, 1], odd[:, :, 1], ALU.subtract))
            then(dve.tensor_scalar(S.mean[:], S.mean[:], 0.5, None, ALU.mult))
            then(dve.tensor_tensor(diff[:], diff[:], diff[:], ALU.mult))
            then(dve.tensor_tensor(var[:], even[:, :, 2], odd[:, :, 2], ALU.add))
            then(dve.tensor_scalar(diff[:], diff[:], 0.25, LN_EPS, ALU.mult, ALU.add))
            then(dve.scalar_tensor_tensor(var[:], var[:], 1.0 / C, diff[:], ALU.mult, ALU.add))
            sqrt_at = n[0]
            dve.wait_ge(root, 1)
            then(dve.reciprocal(S.rstd[:], S.root[:]))
            if twice:
                then(dve.tensor_scalar(var[:], var[:], LN_EPS, None, ALU.subtract))
                then(dve.tensor_tensor(var[:], var[:], S.rstd[:], ALU.mult))
                then(dve.tensor_tensor(var[:], var[:], S.rstd[:], ALU.mult))
                then(dve.tensor_scalar(var[:], var[:], LN_EPS, None, ALU.add))
                dve.wait_ge(root, 2)
                then(dve.reciprocal(S.rstd2[:], S.root[:]))
                then(dve.tensor_tensor(S.rstd2[:], S.rstd2[:], S.rstd[:], ALU.mult))

        @block.scalar
        def _(act):
            act.wait_ge(step, 7)
            act.activation(S.root[:], S.var[:], ACT.Sqrt).then_inc(root, 1)
            if twice:
                act.wait_ge(step, 12)
                act.activation(S.root[:], S.var[:], ACT.Sqrt).then_inc(root, 1)


def attention_weights(nc, S, name, W, transposed):
    raw = S.raw[:, 0:4 * KT * C].rearrange("p (w k c) -> p w k c", w=4, k=KT)
    if not transposed:
        split_weights(nc, S, name, [(W.hi[:, w], W.lo[:, w], raw[:, w]) for w in range(4)])
        return

    def turn(pe, n):
        out = S.bank[n % len(S.bank)].rearrange("p (k c) -> p k c", k=KT)
        for k in range(KT):
            for o in range(KT):
                last = pe.transpose(out[:, k, o * P:(o + 1) * P], raw[:, n, o, k * P:(k + 1) * P], S.ident[:])
        return last

    split_weights(nc, S, name, [
        (W.hi[:, n], W.lo[:, n], S.bank[n % len(S.bank)].rearrange("p (k c) -> p k c", k=KT))
        for n in range(4)], turn)


def attention(nc, S, L, ctx_dram, W, bias, count, load_next):
    NP = S.n_seq // 2
    UP = 2 * UNITS
    with ExitStack() as mem:
        def sb(name, shape, dt=F32):
            return mem.enter_context(nc.sbuf_tensor(f"{L}_{name}", shape, dt))

        own_sems = []

        def sem(name):
            own_sems.append(mem.enter_context(nc.semaphore(f"{L}_{name}")))
            return own_sems[-1]

        normed = sb("normed", [P, 2, C])
        ctx_in = sb("ctx_in", [P, 2, 2, C])
        n_raw, c_raw = sb("nT", [P, KT, 2 * P]), sb("cT", [P, KT, 2 * P])
        nT = [sb("nT_hi", [P, KT, 2 * P], F32R), sb("nT_lo", [P, KT, 2 * P], F32R)]
        cT = [sb("cT_hi", [P, KT, 2 * P], F32R), sb("cT_lo", [P, KT, 2 * P], F32R)]
        q_sb = sb("q", [P, KT, 2 * P])
        q_heads = sb("q_heads", [P, 2, KT, P // D, P])
        kT = sb("kT", [P, 2, KT, 2 * P])
        v_pad = sb("v_pad", [P, 2, 2, H * 32])
        masked = sb("masked", [P, 2, UH, P])
        probs = sb("probs", [P, 2, UH, P])
        probsT = sb("probsT", [P, 2, UH, P])
        neg_max = sb("neg_max", [P, 2, UH])
        o_raw, sum_raw, recip = sb("o_raw", [P, KT, P]), sb("sum", [P, KT, P]), sb("recip", [P, KT, P])
        o_sb = sb("o", [P, KT, P])
        oT = [sb("oT_hi", [P, KT, P], F32R), sb("oT_lo", [P, KT, P], F32R)]

        scores = [S.bank[0].rearrange("p (h k) -> p h k", h=UH), S.bank[1].rearrange("p (h k) -> p h k", h=UH)]
        pT_ps = [S.bank[2].rearrange("p (h k) -> p h k", h=UH), S.bank[3].rearrange("p (h k) -> p h k", h=UH)]
        o_ps = S.bank[4][:, 0:KT * P].rearrange("p (m q) -> p m q", q=P)
        sum_ps = S.bank[5][:, 0:KT * P].rearrange("p (m q) -> p m q", q=P)
        bank_a, bank_b = S.bank[6], S.bank[7]
        tiles = lambda bank: bank.rearrange("p (k t) -> p k t", k=KT)

        ctx_loaded = [sem("ctx_even_loaded"), sem("ctx_odd_loaded")]
        n_ready, bo_added, x_done = sem("n_ready"), sem("bo_added"), sem("x_done")
        tn_ready, tc_ready = sem("tn_ready"), sem("tc_ready")
        nhi_ready, nlo_ready = sem("nhi_ready"), sem("nlo_ready")
        chi_ready, clo_ready = sem("chi_ready"), sem("clo_ready")
        q_made, k_made, v_made = sem("q_made"), sem("k_made"), sem("v_made")
        q_ready, kT_ready, v_ready, v_cleared = sem("q_ready"), sem("kT_ready"), sem("v_ready"), sem("v_cleared")
        q_heads_ready = sem("q_heads_ready")
        scores_ready, max_ready, exp_done = sem("scores_ready"), sem("max_ready"), sem("exp_done")
        pT_made, pv_done, o_kept = sem("pT_made"), sem("pv_done"), sem("o_kept")
        pT_ready = [sem("pT_even_ready"), sem("pT_odd_ready")]
        pT_count = lambda p, u: UP // 2 * p + u // 2
        recip_done, o_done, o_ready = sem("recip_done"), sem("o_done"), sem("o_ready")
        y_made, stats_done = sem("y_made"), sem("stats_done")

        def pairs(eng, step):
            for b in range(2):
                step(b, b)
            if NP > 4:
                with eng.Fori(1, NP // 2 - 1) as i:
                    for b in range(2):
                        step(2 * i + b, b)
            for b in range(2):
                step(NP - 2 + b, b)

        with nc.Block() as block:
            @block.sync
            def _(sp):
                def load(p, b):
                    wait(sp, tc_ready, p - 1)
                    sp.dma_start(ctx_in[:, b], ctx_dram[bass.ds(2 * p, 2)].rearrange("s t c -> t s c")
                                 ).then_inc(ctx_loaded[b], 16)
                load(0, 0)
                next_loaded = load_next(sp)
                load(1, 1)
                if NP > 4:
                    with sp.Fori(1, NP // 2 - 1) as i:
                        for b in range(2):
                            load(2 * i + b, b)
                for b in range(2):
                    load(NP - 2 + b, b)
                wait(sp, *next_loaded)

            @block.tensor
            def _(pe):
                def turn_n(p):
                    wait(pe, n_ready, p + 1)
                    wait(pe, v_ready, p)
                    for k in range(KT):
                        for s in range(2):
                            last = pe.transpose(tiles(bank_a)[:, k, s * P:(s + 1) * P],
                                                normed[:, s, k * P:(k + 1) * P], S.ident[:])
                    last.then_inc(tn_ready, 1)

                def turn_c(p, b):
                    wait(pe, ctx_loaded[b], 8 * (p - b) + 16)
                    wait(pe, x_done, 2 * p - 3)
                    for k in range(KT):
                        for s in range(2):
                            last = pe.transpose(tiles(bank_b)[:, k, s * P:(s + 1) * P],
                                                ctx_in[:, b, s, k * P:(k + 1) * P], S.ident[:])
                    last.then_inc(tc_ready, 1)

                def project_q(p):
                    wait(pe, nlo_ready, p + 1)
                    for m in range(KT):
                        for k in range(KT):
                            last = mm3(pe, tiles(bank_a)[:, m, :],
                                       [w[:, 0, k, m * P:(m + 1) * P] for w in (W.hi, W.lo)],
                                       [t[:, k, :] for t in nT], k == 0, k == KT - 1)
                    last.then_inc(q_made, 1)

                def project_k(p):
                    wait(pe, clo_ready, p + 1)
                    for m in range(KT):
                        for k in range(KT):
                            last = mm3(pe, tiles(bank_b)[:, m, :],
                                       [w[:, 1, k, m * P:(m + 1) * P] for w in (W.hi, W.lo)],
                                       [t[:, k, :] for t in cT], k == 0, k == KT - 1)
                    last.then_inc(k_made, 1)

                def project_v(p, s):
                    if s == 0:
                        wait(pe, q_ready, p + 1)
                        wait(pe, x_done, 2 * p - 2)
                    for k in range(KT):
                        last = mm3(pe, tiles(bank_a)[:, s, :], [t[:, k, s * P:(s + 1) * P] for t in cT],
                                   [w[:, 2, k, :] for w in (W.hi, W.lo)], k == 0, k == KT - 1)
                    if s == 1:
                        last.then_inc(v_made, 1)

                def project_o(p, s):
                    wait(pe, o_ready, 2 * p + s + 1)
                    if s == 0:
                        pe.wait_ge(kT_ready, NP if is_(p, NP - 1) else p + 2)
                    elif is_(p, NP - 1):
                        pe.wait_ge(x_done, 2 * p)
                    elif is_(p, NP - 2):
                        pe.wait_ge(v_ready, NP)
                    else:
                        pe.wait_ge(q_ready, p + 3)
                    out = (bank_b, bank_a)[s][:, 0:C]
                    for k in range(KT):
                        last = mm3(pe, out, [t[:, k, :] for t in oT], [w[:, 3, k, :] for w in (W.hi, W.lo)],
                                   k == 0, k == KT - 1)
                    last.then_inc(y_made, 1)

                def score(p, b, u):
                    s, j = divmod(u, UNITS)
                    wait(pe, max_ready, UP * p + u - 1)
                    if u % UNITS == 0:
                        pe.wait_ge(q_heads_ready, 2 * p + s + 1)
                    if u == 0:
                        pe.wait_ge(kT_ready, p + 1)
                    bank = scores[u % 2]
                    for i in range(UH):
                        last = pe.matmul(bank[:, i, :], q_heads[:, s, j // 2, (j % 2) * UH + i, :],
                                         kT[:, b, j // 2, s * P:(s + 1) * P], start=True, stop=True)
                    last.then_inc(scores_ready, 1)

                def turn_p(p, u):
                    wait(pe, exp_done, UP * p + u + 1)
                    wait(pe, pT_ready[u % 2], pT_count(p, u))
                    for i in range(UH):
                        last = pe.transpose(pT_ps[u % 2][:, i, :], probs[:, u % 2, i, :], S.ident[:])
                    last.then_inc(pT_made, 1)

                def times_v(p, b, u):
                    s, j = divmod(u, UNITS)
                    m, e = divmod(j, 2)
                    wait(pe, pT_ready[u % 2], pT_count(p, u) + 1)
                    if j == 0:
                        wait(pe, o_kept, 2 * p + s)
                    if u == 0:
                        pe.wait_ge(v_ready, p + 1)
                    for to_sum in range(2):
                        for i in range(UH):
                            h = UH * j + i
                            left = S.ones_half[:, e, :] if to_sum else v_pad[:, b, s, h * 32:(h + 1) * 32]
                            out = (o_ps, sum_ps)[to_sum][32 * i:32 * (i + 1), m, :]
                            last = pe.matmul(out, left, probsT[:, u % 2, i, :], start=e == 0, stop=e == 1)
                    last.then_inc(pv_done, 1)

                def step(p, b):
                    first = is_(p, 0)
                    more = not is_(p, NP - 1)
                    for k in range(UP):
                        score(p, b, k)
                        if k >= 1:
                            turn_p(p, k - 1)
                        elif not first:
                            turn_p(p - 1, UP - 1)
                        if k == 0 and not first:
                            project_o(p - 1, 0)
                        if k == 1 and more:
                            turn_n(p + 1)
                        if k == 2 and more:
                            turn_c(p + 1, 1 - b)
                        if k == 3 and more:
                            project_q(p + 1)
                        if k == 4 and not first:
                            project_o(p - 1, 1)
                        if k == 5 and more:
                            project_k(p + 1)
                        if k == 6 and more:
                            project_v(p + 1, 0)
                        if k == 7 and more:
                            project_v(p + 1, 1)
                        if k >= 2:
                            times_v(p, b, k - 2)
                        elif not first:
                            times_v(p - 1, 1 - b, UP - 2 + k)

                turn_n(0)
                turn_c(0, 0)
                project_q(0)
                project_k(0)
                project_v(0, 0)
                project_v(0, 1)
                pairs(pe, step)
                turn_p(NP - 1, UP - 1)
                times_v(NP - 1, 1, UP - 2)
                times_v(NP - 1, 1, UP - 1)
                for s in range(2):
                    project_o(NP - 1, s)

            @block.scalar
            def _(act):
                def round_n(p):
                    act.wait_ge(tn_ready, p + 1)
                    wait(act, q_made, p)
                    act.activation(n_raw[:], tiles(bank_a), ACT.Copy)
                    act.activation(nT[0][:], tiles(bank_a), ACT.Copy).then_inc(nhi_ready, 1)

                def round_c(p):
                    act.wait_ge(tc_ready, p + 1)
                    wait(act, v_made, p)
                    act.activation(c_raw[:], tiles(bank_b), ACT.Copy)
                    act.activation(cT[0][:], tiles(bank_b), ACT.Copy).then_inc(chi_ready, 1)

                def keep_q(p):
                    act.wait_ge(q_made, p + 1)
                    wait(act, q_heads_ready, 2 * p)
                    for m in range(KT):
                        last = act.activation(q_sb[:, m, :], tiles(bank_a)[:, m, :], ACT.Identity,
                                              bias=bias.q[:, m:m + 1])
                    last.then_inc(q_ready, 1)

                def keep_k(p, b):
                    act.wait_ge(k_made, p + 1)
                    wait(act, scores_ready, UP * (p - 1))
                    for m in range(KT):
                        last = act.activation(kT[:, b, m, :], tiles(bank_b)[:, m, :], ACT.Identity,
                                              bias=bias.k[:, m:m + 1])
                    last.then_inc(kT_ready, 1)

                def exps(p, u):
                    act.wait_ge(max_ready, UP * p + u + 1)
                    wait(act, pT_made, UP * p + u - 1)
                    for i in range(UH):
                        last = act.activation(probs[:, u % 2, i, :], masked[:, u % 2, i, :], ACT.Exp,
                                              bias=neg_max[:, u % 2, i:i + 1], scale=-1.0)
                    last.then_inc(exp_done, 1)

                def keep_p(p, u):
                    act.wait_ge(pT_made, UP * p + u + 1)
                    wait(act, pv_done, UP * p + u - 1)
                    act.activation(probsT[:, u % 2], pT_ps[u % 2], ACT.Copy).then_inc(pT_ready[u % 2], 1)

                def keep_o(p, s):
                    n = 2 * p + s
                    act.wait_ge(pv_done, UP * p + (s + 1) * UNITS)
                    wait(act, o_done, n)
                    act.activation(sum_raw[:], sum_ps, ACT.Copy)
                    act.activation(o_raw[:], o_ps, ACT.Copy).then_inc(o_kept, 1)

                def step(p, b):
                    first = is_(p, 0)
                    more = not is_(p, NP - 1)
                    for k in range(UP):
                        exps(p, k)
                        if count is None and k % 2 == 0:
                            if k >= 2:
                                keep_p(p, k - 1)
                            elif not first:
                                keep_p(p - 1, UP - 1)
                        if k == 1:
                            if more:
                                round_n(p + 1)
                            if not first:
                                keep_o(p - 1, 1)
                        if k == 2 and more:
                            round_c(p + 1)
                        if k == 3 and more:
                            keep_q(p + 1)
                        if k == 5:
                            if more:
                                keep_k(p + 1, 1 - b)
                            keep_o(p, 0)

                round_n(0)
                round_c(0)
                keep_q(0)
                keep_k(0, 0)
                pairs(act, step)
                if count is None:
                    keep_p(NP - 1, UP - 1)
                keep_o(NP - 1, 1)

            @block.vector
            def _(dve):
                def norm(p):
                    wait(dve, tn_ready, p)
                    for s in range(2):
                        q = 2 * p + s
                        last = dve.tensor_scalar(normed[:, s, :], S.x[:, q, :], S.mean[:, bass.ds(q, 1)],
                                                 S.rstd[:, bass.ds(q, 1)], ALU.subtract, ALU.mult)
                    last.then_inc(n_ready, 1)

                def keep_v(p, b):
                    dve.wait_ge(v_made, p + 1)
                    wait(dve, pv_done, UP * (p - 1))
                    for s in range(2):
                        for m in range(KT):
                            out = v_pad[:, b, s, m * 256:(m + 1) * 256]
                            src = tiles(bank_a)[:, s, m * P:(m + 1) * P].rearrange("p (e i d) -> p e i d", e=2, i=UH)
                            add = bias.v[:, m * P:(m + 1) * P].rearrange("p (e i d) -> p e i d", e=2, i=UH)
                            for e in range(2):
                                half = out[:, e * P:(e + 1) * P].rearrange("p (i z) -> p i z", i=UH)
                                last = dve.tensor_tensor(half[:, :, e * D:(e + 1) * D], src[:, e], add[:, e], ALU.add)
                    last.then_inc(v_ready, 1)

                def row_max(p, u):
                    dve.wait_ge(scores_ready, UP * p + u + 1)
                    wait(dve, exp_done, UP * p + u - 1)
                    dve.memset(S.carrier[:, u % 2:u % 2 + 1], 0.0)
                    for i in range(UH):
                        last = dve.tensor_tensor_reduce(masked[:, u % 2, i, :], scores[u % 2][:, i, :], S.hidden[:], 1.0,
                                                        LARGEST, ALU.add, ALU.min, neg_max[:, u % 2, i:i + 1])
                    last.then_inc(max_ready, 1)

                def keep_p(p, u):
                    dve.wait_ge(pT_made, UP * p + u + 1)
                    wait(dve, pv_done, UP * p + u - 1)
                    if count is None:
                        last = dve.tensor_copy(probsT[:, u % 2], pT_ps[u % 2])
                    else:
                        seen = count[:, u % UNITS, :].unsqueeze(1).broadcast_to([P, UH, P])
                        last = dve.tensor_tensor(probsT[:, u % 2], pT_ps[u % 2], seen, ALU.mult)
                    last.then_inc(pT_ready[u % 2], 1)

                def invert(p, s, m):
                    dve.wait_ge(o_kept, 2 * p + s + 1)
                    dve.reciprocal(recip[:, m, :], sum_raw[:, m, :]).then_inc(recip_done, 1)

                def residual(p, s):
                    n = 2 * p + s
                    y = (bank_b, bank_a)[s][:, 0:C]
                    dve.wait_ge(y_made, n + 1)
                    dve.wait_ge(bo_added, p + 1)
                    dve.tensor_tensor(S.x[:, n, :], y, S.x[:, n, :], ALU.add).then_inc(x_done, 1)
                    dve.wait_ge(x_done, n + 1)

                def stats(p, s):
                    n = 2 * p + s
                    dve.bn_stats(S.stats[:, n, :], S.x[:, n, :]).then_inc(stats_done, 1)

                def step(p, b):
                    first = is_(p, 0)
                    more = not is_(p, NP - 1)
                    more2 = not (is_(p, NP - 1) or is_(p, NP - 2))
                    for k in range(UP):
                        row_max(p, k)
                        if k == 1 and not first:
                            residual(p - 1, 0)
                        if k == 2 and not first:
                            invert(p - 1, 1, 0)
                        if k == 5 and not first:
                            residual(p - 1, 1)
                        if k == 6:
                            invert(p, 0, 0)
                        if count is None and k % 2 == 0:
                            pass
                        elif k >= 1:
                            keep_p(p, k - 1)
                        elif not first:
                            keep_p(p - 1, UP - 1)
                        if k == 0 and not first:
                            keep_v(p, b)
                        if k == 1 and not first:
                            stats(p - 1, 0)
                        if k == 2 and not first:
                            invert(p - 1, 1, 1)
                        if k == 3 and more2:
                            norm(p + 2)
                        if k == 5 and not first:
                            stats(p - 1, 1)
                        if k == 6:
                            invert(p, 0, 1)

                dve.memset(v_pad[:], 0.0).then_inc(v_cleared, 1)
                norm(0)
                norm(1)
                dve.wait_ge(v_cleared, 1)
                keep_v(0, 0)
                pairs(dve, step)
                if count is not None:
                    keep_p(NP - 1, UP - 1)
                residual(NP - 1, 0)
                stats(NP - 1, 0)
                for m in range(KT):
                    invert(NP - 1, 1, m)
                residual(NP - 1, 1)
                stats(NP - 1, 1)

            @block.gpsimd
            def _(pool):
                def spread_q(p, s):
                    pool.wait_ge(q_ready, p + 1)
                    wait(pool, scores_ready, UP * (p - 1) + (s + 1) * UNITS)
                    for m in range(KT):
                        last = pool.tensor_tensor(
                            q_heads[:, s, m],
                            q_sb[:, m, s * P:(s + 1) * P].unsqueeze(1).broadcast_to([P, P // D, P]),
                            S.head_rows[:].unsqueeze(2).broadcast_to([P, P // D, P]), ALU.mult)
                    last.then_inc(q_heads_ready, 1)

                def add_bo(p):
                    pool.wait_ge(n_ready, p + 1)
                    for s in range(2):
                        n = 2 * p + s
                        last = pool.tensor_tensor(S.x[:, n, :], S.x[:, n, :], bias.o[:], ALU.add)
                    last.then_inc(bo_added, 1)

                def normalize(p, s):
                    n = 2 * p + s
                    pool.wait_ge(recip_done, KT * (n + 1))
                    wait(pool, y_made, n)
                    pool.tensor_tensor(o_sb[:], o_raw[:], recip[:], ALU.mult)
                    pool.tensor_tensor(oT[0][:], o_raw[:], recip[:], ALU.mult).then_inc(o_done, 1)
                    pool.wait_ge(o_done, n + 1)
                    pool.tensor_tensor(oT[1][:], o_sb[:], oT[0][:].bitcast(F32), ALU.subtract).then_inc(o_ready, 1)

                def rest_n(p):
                    pool.wait_ge(nhi_ready, p + 1)
                    pool.tensor_tensor(nT[1][:], n_raw[:], nT[0][:].bitcast(F32), ALU.subtract).then_inc(nlo_ready, 1)

                def rest_c(p):
                    pool.wait_ge(chi_ready, p + 1)
                    pool.tensor_tensor(cT[1][:], c_raw[:], cT[0][:].bitcast(F32), ALU.subtract).then_inc(clo_ready, 1)

                def step(p, b):
                    more = not is_(p, NP - 1)
                    add_bo(p)
                    if more:
                        rest_n(p + 1)
                    if not is_(p, 0):
                        normalize(p - 1, 1)
                    if more:
                        rest_c(p + 1)
                        spread_q(p + 1, 0)
                    normalize(p, 0)
                    if more:
                        spread_q(p + 1, 1)

                rest_n(0)
                rest_c(0)
                for s in range(2):
                    spread_q(0, s)
                pairs(pool, step)
                normalize(NP - 1, 1)
        clear(nc, own_sems)


def gate_weights(nc, S, name, G):
    step, squares, root = (S.sem(f"{name}_{n}") for n in ("step", "squares", "root"))
    with nc.sbuf_tensor(f"{name}_ones", [P, P], F32) as ones, nc.Block() as block:
        @block.vector
        def _(dve):
            n = [0]

            def then(ins):
                n[0] += 1
                ins.then_inc(step, 1)
                dve.wait_ge(step, n[0])

            dve.memset(ones[:], 1.0)
            then(dve.tensor_tensor(G.work[:], G.sim[:], G.sim[:], ALU.mult))
            dve.wait_ge(squares, 1)
            then(dve.tensor_copy(G.norm[:], S.bank[0][:, 0:E]))
            then(dve.tensor_tensor(G.norm[:], S.bank[0][:, E:2 * E], G.norm[:], ALU.add))
            dve.wait_ge(root, 1)
            then(dve.tensor_scalar(G.norm[:], G.norm[:], 1e-12, None, ALU.max))
            then(dve.reciprocal(G.norm[:], G.norm[:]))
            then(dve.tensor_tensor(G.sim[:], G.sim[:], G.norm[:].unsqueeze(1).broadcast_to([P, KT, E]), ALU.mult))
            hi, lo = G.split[:, :, 0:E], G.split[:, :, E:2 * E]
            then(dve.tensor_copy(hi, G.sim[:]))
            then(dve.tensor_tensor(lo, G.sim[:], hi.bitcast(F32), ALU.subtract))
            dve.wait_ge(root, 2)
            then(dve.tensor_scalar(G.gates[:], G.gates[:], 1.0, None, ALU.add))
            then(dve.reciprocal(G.gates[:], G.gates[:]))

        @block.tensor
        def _(pe):
            pe.wait_ge(step, 1)
            pe.matmul(S.bank[0][:, 0:KT * E], ones[:], G.work[:].rearrange("p k e -> p (k e)"),
                      start=True, stop=True).then_inc(squares, 1)

        @block.scalar
        def _(act):
            act.wait_ge(step, 3)
            act.activation(G.norm[:], G.norm[:], ACT.Sqrt).then_inc(root, 1)
            act.activation(G.gates[:], G.gates[:], ACT.Exp, scale=-1.0).then_inc(root, 1)


GATE_BEFORE, GATE_STEPS = 6, 11


def gate_tiles(sb, n):
    one = {f: sb(f"gate_{f}", [P, n]) for f in ("square_sum", "squared", "rnorm", "peak", "none", "total")}
    all_ = {f: sb(f"gate_{f}", [P, n, E]) for f in ("partial", "logit", "gated", "best", "tied", "above", "key", "order",
                                                    "active", "shifted", "exp")}
    return named(n=n, **one, **all_)


def gate_products(pe, out, left, columns):
    for k in range(KT):
        pe.matmul(out, left[0][k], columns[:, k, :], start=k == 0, stop=False)
        last = pe.matmul(out[:, 0:E], left[1][k], columns[:, k, 0:E], start=False, stop=k == KT - 1)
    return last


def gate_chain(dve, step, index, at):
    n = [at]

    def then(ins):
        n[0] += 1
        ins.then_inc(step, 1)
        dve.wait_ge(step, GATE_STEPS * index + n[0])
    return then


def gate_before(S, dve, T, G, dots, step, index):
    then = gate_chain(dve, step, index, 0)
    each = range(T.n)
    ts, stt = dve.tensor_scalar, dve.scalar_tensor_tensor
    for i in each:
        last = stt(T.partial[:, i, :], dots[:, i, E:2 * E], T.rnorm[:, i:i + 1], G.gates[:], ALU.mult, ALU.subtract)
    then(last)
    for i in each:
        last = stt(T.logit[:, i, :], dots[:, i, 0:E], T.rnorm[:, i:i + 1], T.partial[:, i, :], ALU.mult, ALU.add)
    then(last)
    ts(T.gated[:], T.logit[:], 0.0, None, ALU.max)
    for i in each:
        last = dve.max(T.best[:, i, :], T.logit[:, i, :])
    then(last)
    for i in each:
        second = T.best[:, i, 1:2]
        stt(T.tied[:, i, :], T.logit[:, i, :], second, S.rank[:, i, :], ALU.is_ge, ALU.mult)
        ts(T.above[:, i, :], T.logit[:, i, :], second, 2.0 * E, ALU.is_gt, ALU.mult)
    ts(T.peak[:], T.best[:, :, 0], 0.0, None, ALU.max)
    then(ts(T.none[:], T.best[:, :, 0], 0.0, None, ALU.is_le))
    then(dve.tensor_tensor(T.key[:], T.tied[:], T.above[:], ALU.add))
    for i in each:
        ts(T.shifted[:, i, :], T.gated[:, i, :], T.peak[:, i:i + 1], None, ALU.subtract)
    for i in each:
        last = dve.max(T.order[:, i, :], T.key[:, i, :])
    then(last)


def gate_after(dve, T, out, exp_done, step, index, ready):
    then = gate_chain(dve, step, index, GATE_BEFORE)
    each = range(T.n)
    ts = dve.tensor_scalar
    for i in each:
        last = ts(T.active[:, i, :], T.key[:, i, :], T.order[:, i, 1:2], T.none[:, i:i + 1], ALU.is_ge, ALU.mult)
    then(last)
    then(dve.scalar_tensor_tensor(T.active[:], T.logit[:], 0.0, T.active[:], ALU.is_gt, ALU.add))
    dve.wait_ge(exp_done, index + 1)
    then(dve.tensor_tensor(T.exp[:], T.exp[:], T.active[:], ALU.mult))
    then(dve.tensor_reduce(T.total[:], T.exp[:], AX.X, ALU.add))
    then(dve.reciprocal(T.total[:], T.total[:]))
    for i in each:
        last = ts(out[:, i, :], T.exp[:, i, :], T.total[:, i:i + 1], None, ALU.mult)
    last.then_inc(ready, 1)


def parities(eng, count, step, ahead=2):
    for n in range(ahead):
        step(n, n % 2)
    if count > ahead + 4:
        with eng.Fori(ahead // 2, count // 2 - 2) as i:
            for b in range(2):
                step(2 * i + b, b)
    for n in range(max(ahead, count - 4), count):
        step(n, n % 2)


def mixture_attention(nc, S, L, W, G, ln_w, ln_b, hs_dram, load_next):
    NS = S.n_seq
    Q3 = 3 * HID
    with ExitStack() as mem:
        def sb(name, shape, dt=F32):
            return mem.enter_context(nc.sbuf_tensor(f"{L}_{name}", shape, dt))

        own_sems = []

        def sem(name):
            own_sems.append(mem.enter_context(nc.semaphore(f"{L}_{name}")))
            return own_sems[-1]

        normed = sb("normed", [P, 2, C])
        square = sb("square", [P, C])
        nT = [sb("nT_hi", [P, 2, KT, P], F32R), sb("nT_lo", [P, 2, KT, P], F32R)]
        T = gate_tiles(sb, 1)
        rw = sb("rw", [P, 2, 1, E])
        rw_out = sb("rw_out", [P, 2, E])
        qkv = sb("qkv", [P, 2, Q3])
        qkv_odd = sb("qkv_odd", [P, 2, Q3])
        qkv_part = sb("qkv_part", [P, 3, Q3])
        qkT = sb("qkT", [P, 2, P])
        neg_max, row_sum, row_scale = sb("neg_max", [P, 1]), sb("row_sum", [P, 1]), sb("row_scale", [P, 1])
        masked, probs, probsT = sb("masked", [P, P]), sb("probs", [P, P]), sb("probsT", [P, P])
        attn = sb("attn", [P, HID])
        aT = [sb("aT_hi", [P, P], F32R), sb("aT_lo", [P, P], F32R)]
        y = sb("y", [P, C])
        hs_even, hs_odd, hs = sb("hs_even", [P, C]), sb("hs_odd", [P, C]), sb("hs", [P, 2, C])
        out_part = sb("out_part", [P, 3, C])
        seq_stats = sb("seq_stats", [P, 6])

        nT_ps = S.bank[0][:, 0:C].rearrange("p (k t) -> p k t", k=KT)
        dots_ps = S.bank[0][:, C:C + 2 * E]
        qkT_ps = S.bank[1][:, 0:2 * P].rearrange("p (k t) -> p k t", k=2)
        aT_ps = S.bank[1][:, 0:P]
        scores, attn_ps, pT_ps = S.bank[2][:, 0:P], S.bank[2][:, 0:HID], S.bank[3][:, 0:P]
        q_bank = [S.bank[4][:, 0:Q3], S.bank[5][:, 0:Q3]]
        o_bank = [S.bank[6].rearrange("p (e c) -> p e c", e=2), S.bank[7].rearrange("p (e c) -> p e c", e=2)]

        names = ("n_made scaled n_ready squared guarded rooted tn_ready nhi_ready nlo_ready dots_made "
                 "gate_step gate_exp gate_ready kept q_even_made q_odd_made even_added odd_read odd_added "
                 "qkv_ready turned qkT_ready scored max_ready exp_done recip_done pT_made pT_ready attn_made "
                 "attn_ready aT_made ahi_ready alo_ready o_even_made o_odd_made o_even_added o_odd_read "
                 "o_odd_added y_ready hs_ready x_added stats_done").split()
        M = named(**{n: sem(n) for n in names})
        hs_stored = [sem("hs_even_stored"), sem("hs_odd_stored")]
        has = lambda s, ahead: not any(is_(s, NS - 1 - d) for d in range(ahead))

        with nc.Block() as block:
            @block.sync
            def _(sp):
                next_loaded = load_next(sp)

                def step(s, b):
                    sp.wait_ge(M.hs_ready, s + 1)
                    sp.dma_start(hs_dram[bass.ds(s, 1)].rearrange("s t c -> (s t) c"), hs[:, b]
                                 ).then_inc(hs_stored[b], 16)
                parities(sp, NS, step)
                for b in range(2):
                    sp.wait_ge(hs_stored[b], 8 * NS)
                wait(sp, *next_loaded)

            @block.tensor
            def _(pe):
                def turn_n(s, b):
                    pe.wait_ge(M.n_ready, s + 1)
                    wait(pe, M.gate_step, GATE_STEPS * (s - 1) + 2)
                    for k in range(KT):
                        last = pe.transpose(nT_ps[:, k, :], normed[:, b, k * P:(k + 1) * P], S.ident[:])
                    last.then_inc(M.tn_ready, 1)

                def dot_gate(s, b):
                    pe.wait_ge(M.nlo_ready, s + 1)
                    gate_products(pe, dots_ps, [[t[:, b, k, :] for k in range(KT)] for t in nT], G.split
                                  ).then_inc(M.dots_made, 1)

                def project(s, b, e):
                    if e % 2 == 0:
                        wait(pe, M.even_added, 4 * s + e // 2)
                    else:
                        wait(pe, M.odd_read, 4 * s + e // 2)
                    for k in range(KT):
                        last = mm3(pe, q_bank[e % 2], [t[:, b, k, :] for t in nT],
                                   [w[:, e, k, :] for w in (W.hi, W.lo)], k == 0, k == KT - 1)
                    last.then_inc((M.q_even_made, M.q_odd_made)[e % 2], 1)

                def turn_qk(s, b):
                    pe.wait_ge(M.qkv_ready, s + 1)
                    wait(pe, M.alo_ready, s)
                    for n in range(2):
                        last = pe.transpose(qkT_ps[:, n, :], qkv[:, b, n * HID:(n + 1) * HID], S.ident[:])
                    last.then_inc(M.turned, 1)

                def score(s):
                    pe.wait_ge(M.qkT_ready, s + 1)
                    wait(pe, M.attn_ready, s)
                    pe.matmul(scores, qkT[:, 0, :], qkT[:, 1, :], start=True, stop=True).then_inc(M.scored, 1)

                def turn_p(s):
                    pe.wait_ge(M.exp_done, s + 1)
                    wait(pe, M.pT_ready, s)
                    pe.transpose(pT_ps, probs[:], S.ident[:]).then_inc(M.pT_made, 1)

                def times_v(s, b):
                    pe.wait_ge(M.pT_ready, s + 1)
                    pe.matmul(attn_ps, probsT[:], qkv[:, b, 2 * HID:Q3], start=True, stop=True).then_inc(M.attn_made, 1)

                def turn_a(s):
                    pe.wait_ge(M.attn_ready, s + 1)
                    pe.transpose(aT_ps, attn[:], S.ident[:]).then_inc(M.aT_made, 1)

                def project_out(s, n):
                    if n == 0:
                        pe.wait_ge(M.alo_ready, s + 1)
                    if n % 2 == 0:
                        wait(pe, M.o_even_added, 4 * s + n)
                    else:
                        wait(pe, M.o_odd_read, 4 * s + n - 1)
                    mm3(pe, S.bank[6 + n % 2], [t[:] for t in aT],
                        [w[:, 2 * n:2 * n + 2, :].rearrange("p e c -> p (e c)") for w in (W.o_hi, W.o_lo)],
                        True, True).then_inc((M.o_even_made, M.o_odd_made)[n % 2], 1)

                def step(s, b):
                    first, one, two = is_(s, 0), has(s, 1), has(s, 2)
                    for e in range(E):
                        if one:
                            project(s + 1, 1 - b, e)
                        if e == 0 and two:
                            turn_n(s + 2, b)
                        if e == 1:
                            turn_qk(s, b)
                        if e == 2:
                            score(s)
                        if e == 4:
                            turn_p(s)
                        if e == 5:
                            times_v(s, b)
                        if e == 6:
                            turn_a(s)
                        if e in (0, 2, 3, 5) and not first:
                            project_out(s - 1, (0, 2, 3, 5).index(e))
                        if e == 2 and two:
                            dot_gate(s + 2, b)

                for s in range(2):
                    turn_n(s, s)
                    dot_gate(s, s)
                for e in range(E):
                    project(0, 0, e)
                parities(pe, NS, step, 4)
                for n in range(E // 2):
                    project_out(NS - 1, n)

            @block.scalar
            def _(act):
                def squares(s, b):
                    act.wait_ge(M.n_ready, s + 1)
                    wait(act, M.guarded, s)
                    act.activation(square[:], normed[:, b, :], ACT.Square, accum_out=T.square_sum[:]).then_inc(M.squared, 1)

                def round_n(s, b):
                    act.wait_ge(M.tn_ready, s + 1)
                    wait(act, M.q_odd_made, 4 * (s - 1))
                    act.activation(nT[0][:, b], nT_ps, ACT.Copy).then_inc(M.nhi_ready, 1)

                def gate_exp(s):
                    act.wait_ge(M.gate_step, GATE_STEPS * s + GATE_BEFORE)
                    act.activation(T.exp[:], T.shifted[:], ACT.Exp).then_inc(M.gate_exp, 1)

                def weigh_odd(s, b, e):
                    act.wait_ge(M.q_odd_made, 4 * s + e // 2 + 1)
                    if e == 1:
                        act.wait_ge(M.gate_ready, s + 1)
                        wait(act, M.qkv_ready, s - 1)
                        out = qkv_odd[:, b, :]
                    else:
                        wait(act, M.odd_added, 3 * (s - 1) + e // 2)
                        out = qkv_part[:, e // 2 - 1, :]
                    act.activation(out, q_bank[1], ACT.Copy, scale=rw[:, b, 0, e:e + 1]).then_inc(M.odd_read, 1)

                def keep_qk(s):
                    act.wait_ge(M.turned, s + 1)
                    wait(act, M.scored, s)
                    act.activation(qkT[:, 0, :], qkT_ps[:, 0, :], ACT.Copy, scale=-float(HID) ** -0.5)
                    act.activation(qkT[:, 1, :], qkT_ps[:, 1, :], ACT.Copy).then_inc(M.qkT_ready, 1)

                def exps(s):
                    act.wait_ge(M.max_ready, s + 1)
                    wait(act, M.pT_made, s)
                    wait(act, M.recip_done, s)
                    act.activation(probs[:], masked[:], ACT.Exp, bias=neg_max[:], scale=-1.0, accum_out=row_sum[:]).then_inc(M.exp_done, 1)

                def keep_p(s):
                    act.wait_ge(M.pT_made, s + 1)
                    wait(act, M.attn_made, s)
                    act.activation(probsT[:], pT_ps, ACT.Copy).then_inc(M.pT_ready, 1)

                def round_a(s):
                    act.wait_ge(M.aT_made, s + 1)
                    wait(act, M.o_odd_made, 2 * s)
                    act.activation(aT[0][:], aT_ps, ACT.Copy).then_inc(M.ahi_ready, 1)

                def weigh_out(s, b, n):
                    act.wait_ge(M.o_odd_made, 2 * s + n // 2 + 1)
                    for i in range(2):
                        e = 2 * n + i
                        part = 2 * (n // 2) + i - 1
                        if part < 0:
                            act.wait_ge(M.kept, s + 1)
                            wait(act, M.hs_ready, s)
                            out = hs_odd[:]
                        else:
                            wait(act, M.o_odd_added, 3 * (s - 1) + part + 1)
                            out = out_part[:, part, :]
                        act.activation(out, o_bank[1][:, i, :], ACT.Copy, scale=rw_out[:, b, e:e + 1]).then_inc(M.o_odd_read, 1)

                def step(s, b):
                    first, one, two = is_(s, 0), has(s, 1), has(s, 2)
                    if two:
                        squares(s + 2, b)
                        round_n(s + 2, b)
                    if one:
                        weigh_odd(s + 1, 1 - b, 1)
                    keep_qk(s)
                    if not first:
                        weigh_out(s - 1, 1 - b, 1)
                    exps(s)
                    if one:
                        weigh_odd(s + 1, 1 - b, 3)
                    if two:
                        gate_exp(s + 2)
                    keep_p(s)
                    if one:
                        weigh_odd(s + 1, 1 - b, 5)
                    if not first:
                        weigh_out(s - 1, 1 - b, 3)
                    round_a(s)
                    if one:
                        weigh_odd(s + 1, 1 - b, 7)

                for s in range(2):
                    round_n(s, s)
                    squares(s, s)
                    gate_exp(s)
                for e in range(1, E, 2):
                    weigh_odd(0, 0, e)
                parities(act, NS, step, 4)
                weigh_out(NS - 1, 1, 1)
                weigh_out(NS - 1, 1, 3)

            @block.vector
            def _(dve):
                def norm(s, b):
                    wait(dve, M.tn_ready, s - 1)
                    wait(dve, M.squared, s - 1)
                    dve.tensor_scalar(normed[:, b, :], S.x[:, s, :], S.mean[:, bass.ds(s, 1)],
                                      S.rstd2[:, bass.ds(s, 1)], ALU.subtract, ALU.mult).then_inc(M.n_made, 1)

                def rest_n(s, b):
                    dve.wait_ge(M.nhi_ready, s + 1)
                    dve.tensor_tensor(nT[1][:, b], nT_ps, nT[0][:, b].bitcast(F32), ALU.subtract).then_inc(M.nlo_ready, 1)

                def guard(s):
                    dve.wait_ge(M.squared, s + 1)
                    wait(dve, M.rooted, s)
                    dve.tensor_scalar(T.squared[:], T.square_sum[:], 1e-24, None, ALU.max).then_inc(M.guarded, 1)

                def gate_first(s):
                    dve.wait_ge(M.dots_made, s + 1)
                    dve.wait_ge(M.rooted, s + 1)
                    gate_before(S, dve, T, G, dots_ps.unsqueeze(1), M.gate_step, s)

                def gate_last(s, b):
                    wait(dve, M.odd_read, 4 * (s - 1))
                    gate_after(dve, T, rw[:, b], M.gate_exp, M.gate_step, s, M.gate_ready)

                def keep_gate(s, b):
                    dve.wait_ge(M.gate_ready, s + 1)
                    wait(dve, M.o_odd_read, 4 * (s - 1))
                    dve.tensor_copy(rw_out[:, b, :], rw[:, b, 0, :]).then_inc(M.kept, 1)

                def weigh_even(s, b, e):
                    n = 4 * s + e // 2
                    dve.wait_ge(M.q_even_made, n + 1)
                    wait(dve, M.even_added, n)
                    scale = rw[:, b, 0, e:e + 1]
                    if e == 0:
                        dve.wait_ge(M.gate_ready, s + 1)
                        wait(dve, M.attn_made, s - 1)
                        last = dve.tensor_scalar(qkv[:, b, :], q_bank[0], scale, None, ALU.mult)
                    else:
                        last = dve.scalar_tensor_tensor(qkv[:, b, :], q_bank[0], scale, qkv[:, b, :], ALU.mult, ALU.add)
                    last.then_inc(M.even_added, 1)

                def add_qkv(s, b):
                    dve.wait_ge(M.even_added, 4 * (s + 1))
                    dve.wait_ge(M.odd_added, 3 * (s + 1))
                    dve.tensor_tensor(qkv[:, b, :], qkv[:, b, :], qkv_odd[:, b, :], ALU.add).then_inc(M.qkv_ready, 1)

                def row_max(s):
                    dve.wait_ge(M.scored, s + 1)
                    wait(dve, M.exp_done, s)
                    dve.memset(S.carrier[:, 0:1], 0.0)
                    dve.tensor_tensor_reduce(masked[:], scores, S.hidden[:], 1.0, LARGEST, ALU.add, ALU.min, neg_max[:]
                                             ).then_inc(M.max_ready, 1)

                def sum_scale(s):
                    dve.wait_ge(M.exp_done, s + 1)
                    dve.reciprocal(row_scale[:], row_sum[:]).then_inc(M.recip_done, 1)

                def normalize(s):
                    dve.wait_ge(M.attn_made, s + 1)
                    dve.wait_ge(M.recip_done, s + 1)
                    wait(dve, M.aT_made, s)
                    dve.tensor_scalar(attn[:], attn_ps, row_scale[:], None, ALU.mult).then_inc(M.attn_ready, 1)

                def rest_a(s):
                    dve.wait_ge(M.ahi_ready, s + 1)
                    dve.tensor_tensor(aT[1][:], aT_ps, aT[0][:].bitcast(F32), ALU.subtract).then_inc(M.alo_ready, 1)

                def first_ln(s):
                    wait(dve, M.o_even_added, 4 * (s - 1) + 1)
                    dve.tensor_scalar(y[:], S.x[:, s, :], S.mean[:, bass.ds(s, 1)], S.rstd[:, bass.ds(s, 1)],
                                      ALU.subtract, ALU.mult).then_inc(M.y_ready, 1)

                def weigh_out(s, b, n):
                    dve.wait_ge(M.o_even_made, 2 * s + n // 2 + 1)
                    for i in range(2):
                        at = 4 * s + n + i
                        if n == 0 and i == 0:
                            dve.wait_ge(M.y_ready, s + 1)
                            dve.wait_ge(M.kept, s + 1)
                            wait(dve, M.hs_ready, s)
                        wait(dve, M.o_even_added, at)
                        dve.scalar_tensor_tensor(hs_even[:], o_bank[0][:, i, :], rw_out[:, b, 2 * n + i:2 * n + i + 1],
                                                 (hs_even if n or i else y)[:], ALU.mult, ALU.add).then_inc(M.o_even_added, 1)

                def finish(s, b):
                    dve.wait_ge(M.o_even_added, 4 * (s + 1))
                    dve.wait_ge(M.o_odd_added, 3 * (s + 1))
                    wait(dve, M.x_added, s - 1)
                    wait(dve, hs_stored[b], 8 * (s - b))
                    dve.tensor_tensor(hs[:, b, :], hs_even[:], hs_odd[:], ALU.add).then_inc(M.hs_ready, 1)
                    dve.wait_ge(M.hs_ready, s + 1)
                    dve.bn_stats(seq_stats[:], hs[:, b, :]).then_inc(M.stats_done, 1)
                    dve.wait_ge(M.stats_done, s + 1)
                    dve.tensor_copy(S.stats[:, s, :], seq_stats[:])

                def step(s, b):
                    first, one, two, three = is_(s, 0), has(s, 1), has(s, 2), has(s, 3)
                    keep_gate(s, b)
                    if three:
                        norm(s + 3, 1 - b)
                    if one:
                        weigh_even(s + 1, 1 - b, 0)
                    add_qkv(s, b)
                    if not (first or is_(s, 1)):
                        finish(s - 2, b)
                    if two:
                        rest_n(s + 2, b)
                    if not first:
                        weigh_out(s - 1, 1 - b, 0)
                    if two:
                        guard(s + 2)
                    if one:
                        weigh_even(s + 1, 1 - b, 2)
                    row_max(s)
                    if two:
                        gate_first(s + 2)
                    if not first:
                        weigh_out(s - 1, 1 - b, 2)
                    first_ln(s)
                    sum_scale(s)
                    if one:
                        weigh_even(s + 1, 1 - b, 4)
                    normalize(s)
                    if two:
                        gate_last(s + 2, b)
                    if one:
                        weigh_even(s + 1, 1 - b, 6)
                    rest_a(s)

                norm(0, 0)
                norm(1, 1)
                for s in range(2):
                    rest_n(s, s)
                    guard(s)
                    gate_first(s)
                    gate_last(s, s)
                norm(2, 0)
                for e in range(0, E, 2):
                    weigh_even(0, 0, e)
                parities(dve, NS, step, 4)
                finish(NS - 2, 0)
                weigh_out(NS - 1, 1, 0)
                weigh_out(NS - 1, 1, 2)
                finish(NS - 1, 1)

            @block.gpsimd
            def _(pool):
                def root(s):
                    pool.wait_ge(M.guarded, s + 1)
                    wait(pool, M.gate_step, GATE_STEPS * (s - 1) + 2)
                    pool.tensor_tensor(T.rnorm[:], T.squared[:], S.minus_half[:, 0:T.n], ALU.pow).then_inc(M.rooted, 1)

                def affine(s, b):
                    pool.wait_ge(M.n_made, s + 1)
                    pool.tensor_tensor(normed[:, b, :], normed[:, b, :], ln_w[:], ALU.mult).then_inc(M.scaled, 1)
                    pool.wait_ge(M.scaled, s + 1)
                    pool.tensor_tensor(normed[:, b, :], normed[:, b, :], ln_b[:], ALU.add).then_inc(M.n_ready, 1)

                def add_odd(s, b, e):
                    n = e // 2 - 1
                    pool.wait_ge(M.odd_read, 4 * s + e // 2 + 1)
                    wait(pool, M.odd_added, 3 * s + n)
                    pool.tensor_tensor(qkv_odd[:, b, :], qkv_odd[:, b, :], qkv_part[:, n, :], ALU.add).then_inc(M.odd_added, 1)

                def add_out(s, part):
                    pool.wait_ge(M.o_odd_read, 4 * s + part + 2)
                    wait(pool, M.o_odd_added, 3 * s + part)
                    pool.tensor_tensor(hs_odd[:], hs_odd[:], out_part[:, part, :], ALU.add).then_inc(M.o_odd_added, 1)

                def add_hs(s, b):
                    pool.wait_ge(M.hs_ready, s + 1)
                    pool.tensor_tensor(S.x[:, s, :], S.x[:, s, :], hs[:, b, :], ALU.add).then_inc(M.x_added, 1)

                def step(s, b):
                    first, one, two, three = is_(s, 0), has(s, 1), has(s, 2), has(s, 3)
                    if three:
                        affine(s + 3, 1 - b)
                    if not (first or is_(s, 1)):
                        add_hs(s - 2, b)
                    if two:
                        root(s + 2)
                    if one:
                        add_odd(s + 1, 1 - b, 3)
                    if not first:
                        add_out(s - 1, 0)
                    if one:
                        add_odd(s + 1, 1 - b, 5)
                    if not first:
                        add_out(s - 1, 1)
                        add_out(s - 1, 2)
                    if one:
                        add_odd(s + 1, 1 - b, 7)

                for s in range(2):
                    affine(s, s)
                    root(s)
                affine(2, 0)
                for e in range(3, E, 2):
                    add_odd(0, 0, e)
                parities(pool, NS, step, 4)
                add_hs(NS - 2, 0)
                for part in range(3):
                    add_out(NS - 1, part)
                add_hs(NS - 1, 1)
        clear(nc, own_sems)


def mixture_mlp(nc, S, L, W, G, ln_w, ln_b, hs_dram, load_next):
    NS = S.n_seq
    NP = NS // 2
    with ExitStack() as mem:
        def sb(name, shape, dt=F32):
            return mem.enter_context(nc.sbuf_tensor(f"{L}_{name}", shape, dt))

        own_sems = []

        def sem(name):
            own_sems.append(mem.enter_context(nc.semaphore(f"{L}_{name}")))
            return own_sems[-1]

        normed = sb("normed", [P, 2, C])
        square = S.bank[7].rearrange("p (s c) -> p s c", s=2)
        nT = [sb("nT_hi", [P, 2, KT, 2 * P], F32R), sb("nT_lo", [P, 2, KT, 2 * P], F32R)]
        T = gate_tiles(sb, 2)
        rw = sb("rw", [P, 2, 2, E])
        inter = sb("inter", [P, 2, 512])
        iT = [sb("inter_hi", [P, 2, KT, 2 * P], F32R), sb("inter_lo", [P, 2, KT, 2 * P], F32R)]
        hs = sb("hs", [P, 2, 2, C])
        total = sb("total", [P, 2, 2, C])
        seq_stats = sb("seq_stats", [P, 2, 6])

        nT_ps = S.bank[0].rearrange("p (k t) -> p k t", k=KT)
        dots_ps = S.bank[1][:, 0:4 * E].rearrange("p (s e) -> p s e", s=2)
        up_bank = [S.bank[2], S.bank[3], S.bank[6]]
        down_bank = [S.bank[4], S.bank[5]]

        names = ("n_made scaled n_ready squared guarded rooted tn_ready nhi_ready nlo_ready dots_made gate_step gate_exp "
                 "gate_ready up_made inter_ready ihi_ready ilo_ready down_made added stats_done").split()
        M = named(**{n: sem(n) for n in names})
        hs_loaded = [sem("hs_even_loaded"), sem("hs_odd_loaded")]
        has = lambda p, ahead: not any(is_(p, NP - 1 - d) for d in range(ahead))

        with nc.Block() as block:
            @block.sync
            def _(sp):
                def step(p, b):
                    wait(sp, M.n_made, p - 1)
                    sp.dma_start(hs[:, b], hs_dram[bass.ds(2 * p, 2)].rearrange("s t c -> t s c")
                                 ).then_inc(hs_loaded[b], 16)
                next_loaded = load_next(sp)
                parities(sp, NP, step)
                wait(sp, *next_loaded)

            @block.tensor
            def _(pe):
                def turn_n(p):
                    pe.wait_ge(M.n_ready, p + 1)
                    wait(pe, M.nlo_ready, p)
                    for k in range(KT):
                        for s in range(2):
                            last = pe.transpose(nT_ps[:, k, s * P:(s + 1) * P], normed[:, s, k * P:(k + 1) * P], S.ident[:])
                    last.then_inc(M.tn_ready, 1)

                def dot_gate(p, b):
                    pe.wait_ge(M.nlo_ready, p + 1)
                    wait(pe, M.gate_step, GATE_STEPS * (p - 1) + 2)
                    for s in range(2):
                        last = gate_products(pe, dots_ps[:, s, :], [[t[:, b, k, s * P:(s + 1) * P] for k in range(KT)]
                                                                    for t in nT], G.split)
                    last.then_inc(M.dots_made, 1)

                def up(p, b, e):
                    wait(pe, M.ihi_ready, E * p + e - 1)
                    if e == 0:
                        pe.wait_ge(M.nlo_ready, p + 1)
                    out = up_bank[e % 2].rearrange("p (m t) -> p m t", m=KT)
                    for m in range(KT):
                        for k in range(KT):
                            last = mm3(pe, out[:, m, :], [w[:, 0, e, k, m * P:(m + 1) * P] for w in (W.hi, W.lo)],
                                       [t[:, b, k, :] for t in nT], k == 0, k == KT - 1)
                    last.then_inc(M.up_made, 1)

                def down(p, e):
                    pe.wait_ge(M.ilo_ready, E * p + e + 1)
                    wait(pe, M.added, 2 * (E * p + e - 1))
                    out = down_bank[e % 2].rearrange("p (s c) -> p s c", s=2)
                    for s in range(2):
                        for k in range(KT):
                            last = mm3(pe, out[:, s, :], [t[:, e % 2, k, s * P:(s + 1) * P] for t in iT],
                                       [w[:, 1, e, k, :] for w in (W.hi, W.lo)], k == 0, k == KT - 1)
                    last.then_inc(M.down_made, 1)

                def step(p, b):
                    for e in range(E):
                        up(p, b, e)
                        if e >= 1:
                            down(p, e - 1)
                        elif not is_(p, 0):
                            down(p - 1, E - 1)
                        if e == 1 and has(p, 1):
                            turn_n(p + 1)
                        if e == 4 and has(p, 1):
                            dot_gate(p + 1, 1 - b)

                turn_n(0)
                dot_gate(0, 0)
                parities(pe, NP, step)
                down(NP - 1, E - 1)

            @block.scalar
            def _(act):
                def round_n(p, b):
                    act.wait_ge(M.tn_ready, p + 1)
                    wait(act, M.up_made, E * (p - 1))
                    act.activation(nT[0][:, b], nT_ps, ACT.Copy).then_inc(M.nhi_ready, 1)

                def squares(p):
                    act.wait_ge(M.n_ready, p + 1)
                    wait(act, M.guarded, p)
                    for s in range(2):
                        last = act.activation(square[:, s], normed[:, s, :], ACT.Square, accum_out=T.square_sum[:, s:s + 1])
                    last.then_inc(M.squared, 1)

                def gelu(p, e):
                    n = E * p + e
                    act.wait_ge(M.up_made, n + 1)
                    wait(act, M.ilo_ready, n - 1)
                    wait(act, M.down_made, n - 1)
                    act.activation(inter[:, e % 2], up_bank[e % 2], ACT.Gelu).then_inc(M.inter_ready, 1)
                    act.activation(iT[0][:, e % 2].rearrange("p k t -> p (k t)"), up_bank[e % 2], ACT.Gelu).then_inc(M.ihi_ready, 1)

                def step(p, b):
                    for e in range(E):
                        gelu(p, e)
                        if has(p, 1):
                            if e == 1:
                                round_n(p + 1, 1 - b)
                            if e == 2:
                                squares(p + 1)

                round_n(0, 0)
                squares(0)
                parities(act, NP, step)

            @block.vector
            def _(dve):
                def norm(p, b):
                    dve.wait_ge(hs_loaded[b], 8 * (p - b) + 16)
                    wait(dve, M.tn_ready, p)
                    wait(dve, M.squared, p)
                    for s in range(2):
                        n = 2 * p + s
                        last = dve.tensor_scalar(normed[:, s, :], hs[:, b, s, :], S.mean[:, bass.ds(n, 1)],
                                                 S.rstd[:, bass.ds(n, 1)], ALU.subtract, ALU.mult)
                    last.then_inc(M.n_made, 1)

                def rest_n(p, b):
                    dve.wait_ge(M.nhi_ready, p + 1)
                    dve.tensor_tensor(nT[1][:, b], nT_ps, nT[0][:, b].bitcast(F32), ALU.subtract).then_inc(M.nlo_ready, 1)

                def guard(p):
                    dve.wait_ge(M.squared, p + 1)
                    wait(dve, M.rooted, p)
                    dve.tensor_scalar(T.squared[:], T.square_sum[:], 1e-24, None, ALU.max).then_inc(M.guarded, 1)

                def gate_first(p):
                    dve.wait_ge(M.dots_made, p + 1)
                    dve.wait_ge(M.rooted, p + 1)
                    gate_before(S, dve, T, G, dots_ps, M.gate_step, p)

                def gate_last(p, b):
                    gate_after(dve, T, rw[:, b], M.gate_exp, M.gate_step, p, M.gate_ready)

                def rest_i(p, e):
                    n = E * p + e
                    dve.wait_ge(M.ihi_ready, n + 1)
                    dve.tensor_tensor(iT[1][:, e % 2].rearrange("p k t -> p (k t)"), inter[:, e % 2],
                                      iT[0][:, e % 2].rearrange("p k t -> p (k t)").bitcast(F32), ALU.subtract
                                      ).then_inc(M.ilo_ready, 1)

                def add(p, b, e):
                    n = E * p + e
                    dve.wait_ge(M.down_made, n + 1)
                    if e == 0:
                        dve.wait_ge(M.gate_ready, p + 1)
                    wait(dve, M.added, 2 * n)
                    out = down_bank[e % 2].rearrange("p (s c) -> p s c", s=2)
                    for s in range(2):
                        dve.scalar_tensor_tensor(total[:, b, s, :], out[:, s, :], rw[:, b, s, e:e + 1],
                                                 total[:, b, s, :] if e else S.x[:, 2 * p + s, :],
                                                 ALU.mult, ALU.add).then_inc(M.added, 1)

                def finish(p, b):
                    dve.wait_ge(M.added, 2 * E * (p + 1))
                    for s in range(2):
                        dve.bn_stats(seq_stats[:, s, :], total[:, b, s, :]).then_inc(M.stats_done, 1)
                    dve.tensor_copy(S.x[:, bass.ds(2 * p, 2), :], total[:, b])
                    dve.wait_ge(M.stats_done, 2 * p + 2)
                    dve.tensor_copy(S.stats[:, bass.ds(2 * p, 2), :], seq_stats[:])

                def step(p, b):
                    for e in range(E):
                        rest_i(p, e)
                        if e >= 1:
                            add(p, b, e - 1)
                        elif not is_(p, 0):
                            add(p - 1, 1 - b, E - 1)
                        if e == 1:
                            if not is_(p, 0):
                                finish(p - 1, 1 - b)
                            if has(p, 1):
                                rest_n(p + 1, 1 - b)
                        if e == 3 and has(p, 1):
                            guard(p + 1)
                        if e == 3 and has(p, 2):
                            norm(p + 2, b)
                        if e == 4 and has(p, 1):
                            gate_first(p + 1)
                        if e == 7:
                            if has(p, 1):
                                gate_last(p + 1, 1 - b)

                norm(0, 0)
                rest_n(0, 0)
                guard(0)
                gate_first(0)
                gate_last(0, 0)
                norm(1, 1)
                parities(dve, NP, step)
                add(NP - 1, 1, E - 1)
                finish(NP - 1, 1)

            @block.gpsimd
            def _(pool):
                def root(p):
                    pool.wait_ge(M.guarded, p + 1)
                    wait(pool, M.gate_step, GATE_STEPS * (p - 1) + 2)
                    pool.tensor_tensor(T.rnorm[:], T.squared[:], S.minus_half[:, 0:T.n], ALU.pow).then_inc(M.rooted, 1)

                def gate_exp(p):
                    pool.wait_ge(M.gate_step, GATE_STEPS * p + GATE_BEFORE)
                    pool.tensor_tensor(T.exp[:], S.euler[:], T.shifted[:], ALU.pow).then_inc(M.gate_exp, 1)

                def affine(p):
                    pool.wait_ge(M.n_made, p + 1)
                    wide = lambda t: t[:].unsqueeze(1).broadcast_to([P, 2, C])
                    pool.tensor_tensor(normed[:], normed[:], wide(ln_w), ALU.mult).then_inc(M.scaled, 1)
                    pool.wait_ge(M.scaled, p + 1)
                    pool.tensor_tensor(normed[:], normed[:], wide(ln_b), ALU.add).then_inc(M.n_ready, 1)

                def step(p, b):
                    if has(p, 1):
                        root(p + 1)
                        gate_exp(p + 1)
                    if has(p, 2):
                        affine(p + 2)

                affine(0)
                root(0)
                gate_exp(0)
                affine(1)
                parities(pool, NP, step)
        clear(nc, own_sems)


def routed_experts(nc, S, L, W, R, out_dram):
    NP = S.n_seq // 2
    SLOTS = E
    with ExitStack() as mem:
        def sb(name, shape, dt=F32):
            return mem.enter_context(nc.sbuf_tensor(f"{L}_{name}", shape, dt))

        own_sems = []

        def sem(name):
            own_sems.append(mem.enter_context(nc.semaphore(f"{L}_{name}")))
            return own_sems[-1]

        normed = sb("normed", [P, 2, C])
        nT = [sb("nT_hi", [P, 2, KT, 2 * P], F32R), sb("nT_lo", [P, 2, KT, 2 * P], F32R)]
        partial, logit, tied, first, exp = (sb(n, [P, 2, E]) for n in ("partial", "logit", "tied", "first", "exp"))
        top, order, weight = (sb(n, [P, 2]) for n in ("top", "order", "weight"))
        gate = sb("gate", [P, 2, 2, P])
        gateT = sb("gateT", [P, 2, 2, P])
        even, odd, base, both = (sb(n, [P, 2, C]) for n in ("even", "odd", "base", "both"))
        part = sb("part", [P, 2, 3, C])
        result = sb("result", [P, 2, 2, C])

        nT_ps = S.bank[0].rearrange("p (k t) -> p k t", k=KT)
        dots_ps = S.bank[1][:, 0:4 * E].rearrange("p (s e) -> p s e", s=2)
        gateT_ps = S.bank[2][:, 0:2 * P].rearrange("p (s t) -> p s t", s=2)
        bias_ps = S.bank[3].rearrange("p (s c) -> p s c", s=2)
        y_bank = [S.bank[4 + n].rearrange("p (e c) -> p e c", e=2) for n in range(4)]

        names = ("n_ready tn_ready nhi_ready nlo_ready dots_made dots_read step exp_done gate_cleared gate_ready gT_made gT_ready "
                 "bias_made base_ready even_made odd_made even_added odd_read odd_added both_done result_ready").split()
        M = named(**{n: sem(n) for n in names})
        stored = [sem("even_stored"), sem("odd_stored")]
        has = lambda p, ahead: not any(is_(p, NP - 1 - d) for d in range(ahead))
        STEPS = 9

        with nc.Block() as block:
            @block.sync
            def _(sp):
                def step(p, b):
                    sp.wait_ge(M.result_ready, 2 * p + 2)
                    sp.dma_start(out_dram[bass.ds(2 * p, 2)].rearrange("s t c -> t s c"), result[:, b]
                                 ).then_inc(stored[b], 16)
                parities(sp, NP, step)
                for b in range(2):
                    sp.wait_ge(stored[b], 8 * NP)

            @block.tensor
            def _(pe):
                def turn_n(p):
                    pe.wait_ge(M.n_ready, p + 1)
                    wait(pe, M.nlo_ready, p)
                    for k in range(KT):
                        for s in range(2):
                            last = pe.transpose(nT_ps[:, k, s * P:(s + 1) * P], normed[:, s, k * P:(k + 1) * P], S.ident[:])
                    last.then_inc(M.tn_ready, 1)

                def dot_router(p, b):
                    pe.wait_ge(M.nlo_ready, p + 1)
                    wait(pe, M.dots_read, 2 * p)
                    for s in range(2):
                        last = gate_products(pe, dots_ps[:, s, :], [[t[:, b, k, s * P:(s + 1) * P] for k in range(KT)]
                                                                    for t in nT], R.split)
                    last.then_inc(M.dots_made, 1)

                def turn_gate(p, b):
                    pe.wait_ge(M.gate_ready, p + 1)
                    wait(pe, M.gT_ready, p)
                    for s in range(2):
                        last = pe.transpose(gateT_ps[:, s, :], gate[:, b, s, :], S.ident[:])
                    last.then_inc(M.gT_made, 1)

                def bias(p, b):
                    pe.wait_ge(M.gT_ready, p + 1)
                    wait(pe, M.base_ready, p)
                    for s in range(2):
                        last = pe.matmul(bias_ps[:, s, :], gateT[:, b, s, :], R.expert_b[:], start=True, stop=True)
                    last.then_inc(M.bias_made, 1)

                def expert(p, b, t):
                    s, n = divmod(t, 4)
                    if n % 2 == 0:
                        wait(pe, M.even_added, 8 * p + 4 * s - 4 + n + 2)
                    else:
                        wait(pe, M.odd_read, 8 * p + 4 * s - 4 + n + 1)
                    for k in range(KT):
                        last = mm3(pe, S.bank[4 + n], [t_[:, b, k, s * P:(s + 1) * P] for t_ in nT],
                                   [w[:, k, 2 * n:2 * n + 2, :].rearrange("p e c -> p (e c)") for w in (W.hi, W.lo)],
                                   k == 0, k == KT - 1)
                    last.then_inc((M.even_made, M.odd_made)[n % 2], 1)

                def step(p, b):
                    for t in range(SLOTS):
                        expert(p, b, t)
                        if t == 1:
                            turn_gate(p, b)
                        if t == 3:
                            bias(p, b)
                        if has(p, 1):
                            if t == 0:
                                turn_n(p + 1)
                            if t == 2:
                                dot_router(p + 1, 1 - b)

                turn_n(0)
                dot_router(0, 0)
                parities(pe, NP, step)

            @block.scalar
            def _(act):
                def round_n(p, b):
                    act.wait_ge(M.tn_ready, p + 1)
                    wait(act, M.odd_made, 4 * (p - 1))
                    act.activation(nT[0][:, b], nT_ps, ACT.Copy).then_inc(M.nhi_ready, 1)

                def gate_exp(p):
                    act.wait_ge(M.step, STEPS * p + 4)
                    act.activation(exp[:], logit[:], ACT.Exp).then_inc(M.exp_done, 1)

                def keep_gate(p, b):
                    act.wait_ge(M.gT_made, p + 1)
                    wait(act, M.bias_made, p - 1)
                    act.activation(gateT[:, b], gateT_ps, ACT.Copy).then_inc(M.gT_ready, 1)

                def weigh(p, b, t):
                    s, n = divmod(t, 4)
                    q = 2 * p + s
                    act.wait_ge(M.odd_made, 2 * q + n // 2 + 1)
                    for i in range(2):
                        k = 2 * (n // 2) + i - 1
                        if k < 0:
                            act.wait_ge(M.gate_ready, p + 1)
                            wait(act, M.both_done, q - 1)
                            out = odd[:, s, :]
                        else:
                            wait(act, M.odd_added, 3 * (q - 2) + k + 1)
                            out = part[:, s, k, :]
                        act.activation(out, y_bank[n][:, i, :], ACT.Copy, scale=gate[:, b, s, 2 * n + i:2 * n + i + 1]
                                       ).then_inc(M.odd_read, 1)

                def step(p, b):
                    for t in range(SLOTS):
                        if t % 2:
                            weigh(p, b, t)
                        if t == 1:
                            keep_gate(p, b)
                        if has(p, 1):
                            if t == 0:
                                round_n(p + 1, 1 - b)
                            if t == 5:
                                gate_exp(p + 1)

                round_n(0, 0)
                gate_exp(0)
                parities(act, NP, step)

            @block.vector
            def _(dve):
                def norm(p):
                    wait(dve, M.tn_ready, p)
                    for s in range(2):
                        n = 2 * p + s
                        last = dve.tensor_scalar(normed[:, s, :], S.x[:, n, :], S.mean[:, bass.ds(n, 1)],
                                                 S.rstd[:, bass.ds(n, 1)], ALU.subtract, ALU.mult)
                    last.then_inc(M.n_ready, 1)

                def rest_n(p, b):
                    dve.wait_ge(M.nhi_ready, p + 1)
                    dve.tensor_tensor(nT[1][:, b], nT_ps, nT[0][:, b].bitcast(F32), ALU.subtract).then_inc(M.nlo_ready, 1)

                wide = lambda t: t[:].unsqueeze(2).broadcast_to([P, 2, E])

                def chain(p, at):
                    n = [at]

                    def then(ins):
                        n[0] += 1
                        ins.then_inc(M.step, 1)
                        dve.wait_ge(M.step, STEPS * p + n[0])
                    return then

                def gate_first(p):
                    then = chain(p, 0)
                    tt = dve.tensor_tensor
                    dve.wait_ge(M.dots_made, p + 1)
                    tt(partial[:], dots_ps[:, :, E:2 * E], R.bias[:].unsqueeze(1).broadcast_to([P, 2, E]), ALU.add
                       ).then_inc(M.dots_read, 1)
                    dve.wait_ge(M.dots_read, 2 * p + 1)
                    tt(logit[:], dots_ps[:, :, 0:E], partial[:], ALU.add).then_inc(M.dots_read, 1)
                    dve.wait_ge(M.dots_read, 2 * p + 2)
                    then(dve.tensor_reduce(top[:], logit[:], AX.X, ALU.max))
                    then(tt(tied[:], logit[:], wide(top), ALU.is_ge))
                    then(tt(tied[:], tied[:], S.rank[:], ALU.mult))
                    then(tt(logit[:], logit[:], wide(top), ALU.subtract))
                    then(dve.tensor_reduce(order[:], tied[:], AX.X, ALU.max))
                    then(tt(first[:], S.rank[:], wide(order), ALU.is_equal))

                def gate_last(p, b):
                    then = chain(p, 6)
                    dve.wait_ge(M.exp_done, p + 1)
                    then(dve.tensor_reduce(weight[:], exp[:], AX.X, ALU.add))
                    then(dve.reciprocal(weight[:], weight[:]))
                    wait(dve, M.gT_made, p - 1)
                    wait(dve, M.odd_read, 8 * (p - 1))
                    then(dve.tensor_tensor(first[:], first[:], wide(weight), ALU.mult))
                    dve.tensor_copy(gate[:, b, :, 0:E], first[:]).then_inc(M.gate_ready, 1)

                def add_bias(p):
                    dve.wait_ge(M.bias_made, p + 1)
                    dve.tensor_tensor(base[:], bias_ps, S.x[:, bass.ds(2 * p, 2), :], ALU.add).then_inc(M.base_ready, 1)

                def weigh(p, b, t):
                    s, n = divmod(t, 4)
                    q = 2 * p + s
                    dve.wait_ge(M.even_made, 2 * q + n // 2 + 1)
                    for i in range(2):
                        y, scale = y_bank[n][:, i, :], gate[:, b, s, 2 * n + i:2 * n + i + 1]
                        if n + i == 0:
                            dve.wait_ge(M.gate_ready, p + 1)
                            wait(dve, M.both_done, q - 1)
                            last = dve.tensor_scalar(even[:, s, :], y, scale, None, ALU.mult)
                        else:
                            dve.wait_ge(M.even_added, 4 * q + n + i)
                            last = dve.scalar_tensor_tensor(even[:, s, :], y, scale, even[:, s, :], ALU.mult, ALU.add)
                        last.then_inc(M.even_added, 1)

                def finish(p, b, s):
                    q = 2 * p + s
                    dve.wait_ge(M.even_added, 4 * q + 4)
                    dve.wait_ge(M.odd_added, 3 * q + 3)
                    dve.tensor_tensor(both[:, s, :], even[:, s, :], odd[:, s, :], ALU.add).then_inc(M.both_done, 1)
                    dve.wait_ge(M.both_done, q + 1)
                    dve.wait_ge(M.base_ready, p + 1)
                    wait(dve, stored[b], 8 * (p - b))
                    dve.tensor_tensor(result[:, b, s, :], both[:, s, :], base[:, s, :], ALU.add).then_inc(M.result_ready, 1)

                def step(p, b):
                    for t in range(SLOTS):
                        if t % 2 == 0:
                            weigh(p, b, t)
                        if t == 1:
                            if not is_(p, 0):
                                finish(p - 1, 1 - b, 1)
                            if has(p, 1):
                                rest_n(p + 1, 1 - b)
                        if t == 3 and has(p, 1):
                            gate_first(p + 1)
                        if t == 4:
                            add_bias(p)
                        if t == 5:
                            finish(p, b, 0)
                            if has(p, 2):
                                norm(p + 2)
                        if t == 6 and has(p, 1):
                            gate_last(p + 1, 1 - b)

                dve.memset(gate[:], 0.0).then_inc(M.gate_cleared, 1)
                norm(0)
                rest_n(0, 0)
                gate_first(0)
                dve.wait_ge(M.gate_cleared, 1)
                gate_last(0, 0)
                norm(1)
                parities(dve, NP, step)
                finish(NP - 1, 1, 1)

            @block.gpsimd
            def _(pool):
                def step(p, b):
                    for s in range(2):
                        q = 2 * p + s
                        for k in range(3):
                            pool.wait_ge(M.odd_read, 4 * q + k + 2)
                            wait(pool, M.odd_added, 3 * q + k)
                            pool.tensor_tensor(odd[:, s, :], odd[:, s, :], part[:, s, k, :], ALU.add).then_inc(M.odd_added, 1)
                parities(pool, NP, step)
        clear(nc, own_sems)


def load_mixture_attention_raw(dma, S, q, k, v, o, done):
    qkv = S.raw[:, 0:E * KT * 3 * HID].rearrange("p (e k w) -> p e k w", e=E, k=KT)
    for n, w in enumerate((q, k, v)):
        for e in range(E):
            dma.dma_start(qkv[:, e, :, n * HID:(n + 1) * HID], w[e].rearrange("(k p) h -> p k h", p=P)).then_inc(done, 16)
    out = S.raw[:, E * KT * 3 * HID:].rearrange("p (e c) -> p e c", e=E)
    dma.dma_start(out, o.rearrange("e h c -> h e c")).then_inc(done, 16)
    return 16 * (3 * E + 1)


def load_mixture_mlp_raw(dma, S, w1, w2, done):
    raw = S.raw[:].rearrange("p (w e k c) -> p w e k c", w=2, e=E, k=KT)
    for n, w in enumerate((w1, w2)):
        for e in range(E):
            dma.dma_start(raw[:, n, e], w[e].rearrange("(k p) c -> p k c", p=P)).then_inc(done, 16)
    return 16 * 2 * E


def load_experts_raw(dma, S, w, done):
    raw = S.raw[:, 0:E * KT * C].rearrange("p (e o d) -> p e o d", e=E, o=KT)
    for e in range(E):
        dma.dma_start(raw[:, e], w[e].rearrange("(o p) d -> p o d", p=P)).then_inc(done, 16)
    return 16 * E


def expert_weights(nc, S, name, W, R):
    raw = S.raw[:, 0:E * KT * C].rearrange("p (e o d) -> p e o d", e=E, o=KT)
    split_weights(nc, S, f"{name}_router", [(R.split[:, :, 0:E], R.split[:, :, E:2 * E], R.raw[:])])

    def turn(pe, e):
        out = S.bank[e % len(S.bank)].rearrange("p (k c) -> p k c", k=KT)
        for k in range(KT):
            for o in range(KT):
                last = pe.transpose(out[:, k, o * P:(o + 1) * P], raw[:, e, o, k * P:(k + 1) * P], S.ident[:])
        return last

    split_weights(nc, S, name, [
        (W.hi[:, :, e, :], W.lo[:, :, e, :], S.bank[e % len(S.bank)].rearrange("p (k c) -> p k c", k=KT))
        for e in range(E)], turn)


def load_attention_raw(dma, S, W4, transposed, done):
    raw = S.raw[:, 0:4 * KT * C].rearrange("p (w k c) -> p w k c", w=4, k=KT)
    n = 0
    for w in range(4):
        if w == 3 and transposed:
            to = raw[:, w].rearrange("p o (k i e d) -> p o k e i d", k=KT, e=2, i=UH)
            columns = W4[w].rearrange("(o p) (k e i d) -> p o k e i d", p=P, k=KT, e=2, i=UH)
            for o in range(KT):
                for k in range(KT):
                    for e in range(2):
                        dma.dma_start(to[:, o, k, e], columns[:, o, k, e]).then_inc(done, 16)
                        n += 1
        elif w < 3:
            dma.dma_start(raw[:, w], W4[w].rearrange("(k p) c -> p k c", p=P)).then_inc(done, 16)
            n += 1
        else:
            rows = W4[w].rearrange("(k e i d) c -> e i d k c", k=KT, e=2, i=UH)
            for e in range(2):
                for i in range(UH):
                    dma.dma_start(raw[32 * i + D * e:32 * i + D * (e + 1), w], rows[e, i]).then_inc(done, 16)
                    n += 1
    return 16 * n


def setup(nc, S, a, consts):
    chunk = 8
    chunks = S.n_seq // chunk
    const_in, raw_in = S.sem("constants_loaded"), S.sem("raw0_loaded")
    x_in = [S.sem(f"x{n}_loaded") for n in range(chunks)]
    stats_done, cleared = S.sem("first_stats_done"), S.sem("expert_bias_cleared")
    with nc.Block() as block:
        @block.sync
        def _(sp):
            for n in range(chunks):
                sp.dma_start(S.x[:, n * chunk:(n + 1) * chunk, :],
                             a["x"][n * chunk:(n + 1) * chunk].rearrange("s t c -> t s c")).then_inc(x_in[n], 16)

        @block.scalar
        def _(act):
            total = load_attention_raw(act, S, [a[f"L0_xattn_{n}"] for n in ("Wq", "Wk", "Wv", "Wo")], True, raw_in)
            n = 0
            for name, tile in S.const_tiles:
                act.dma_start(tile[:], consts[name]).then_inc(const_in, 16)
                n += 16
            for tile, row in S.row_tiles:
                act.dma_start(tile, a[row].partition_broadcast(P)).then_inc(const_in, 16)
                n += 16
            for tile, name in S.column_tiles:
                act.dma_start(tile, a[name].rearrange("(k p) -> p k", p=P),
                              allow_slow_non_contiguous=True).then_inc(const_in, 16)
                n += 16
            for tile, source in S.sim_tiles:
                act.dma_start(tile, source, allow_slow_non_contiguous=True).then_inc(const_in, 16)
                n += 16
            act.wait_ge(cleared, 1)
            act.dma_start(S.expert_b[0:E, :], a["L1_ffn_expert_b"]).then_inc(const_in, 16)
            n += 16
            act.wait_ge(raw_in, total)
            act.wait_ge(const_in, n)

        @block.vector
        def _(dve):
            dve.memset(S.expert_b[:], 0.0).then_inc(cleared, 1)
            for n in range(chunks):
                dve.wait_ge(x_in[n], 16)
                with dve.Fori(n * chunk, (n + 1) * chunk) as s:
                    last = dve.bn_stats(S.stats[:, s, :], S.x[:, s, :])
                    last.then_inc(stats_done, 1)
            dve.wait_ge(stats_done, S.n_seq)


def program(nc, a, consts, out, phases=5):
    with ExitStack() as mem:
        def sb(name, shape, dt=F32):
            return mem.enter_context(nc.sbuf_tensor(name, shape, dt))

        S = Named()
        S.n_seq = a["x"].shape[0]
        S.sem = lambda name: mem.enter_context(nc.semaphore(name))
        S.bank = [mem.enter_context(nc.psum_tensor(f"bank{n}", [P, 512], F32))[:] for n in range(8)]
        S.x = sb("x_all", [P, S.n_seq, C])
        S.stats = sb("stats", [P, S.n_seq, 6])
        S.mean, S.var, S.root = (sb(n, [P, S.n_seq]) for n in ("mean", "var", "root"))
        S.rstd, S.rstd2 = sb("rstd", [P, S.n_seq]), sb("rstd2", [P, S.n_seq])
        S.raw = sb("raw_weights", [P, 2 * E * KT * C])

        S.ident = sb("ident", [P, P])
        S.hidden = sb("hidden", [P, P])
        S.carrier = sb("carrier", [P, 2])
        S.count_bf = sb("count_bf", [P, UNITS, P], BF16)
        S.ones_half = sb("ones_half", [P, 2, 32])
        S.head_rows = sb("head_rows", [P, P // D])
        S.rank = sb("rank", [P, 2, E])
        S.minus_half, S.euler = sb("minus_half", [P, 2]), sb("euler", [P, 2, E])
        S.const_tiles = [("minus_half", S.minus_half), ("euler", S.euler), ("ident", S.ident), ("hidden", S.hidden),
                         ("count_bf", S.count_bf), ("ones_half", S.ones_half),
                         ("head_rows", S.head_rows), ("rank", S.rank)]
        S.row_tiles, S.column_tiles, S.sim_tiles = [], [], []

        def row(name, width):
            tile = sb(f"{name}_row", [P, width])
            S.row_tiles.append((tile[:], name))
            return tile

        def column(name):
            tile = sb(f"{name}_column", [P, KT])
            S.column_tiles.append((tile[:], name))
            return tile

        def gate(name):
            G = named(sim=sb(f"{name}_sim", [P, KT, E]), work=sb(f"{name}_work", [P, KT, E]),
                                norm=sb(f"{name}_norm", [P, E]), split=sb(f"{name}_split", [P, KT, 2 * E], F32R)[:],
                                gates=row(f"{name}_gates", E))
            S.sim_tiles.append((G.sim[:], a[f"{name}_sim"].rearrange("(k p) e -> p k e", p=P)))
            return G

        B = {L: named(q=column(f"{L}_bq"), k=column(f"{L}_bk"), v=row(f"{L}_bv", C), o=row(f"{L}_bo", C))
             for L in ("L0_xattn", "L1_xattn")}
        ln1 = row("L0_ffn_ln1_w", C), row("L0_ffn_ln1_b", C)
        ln2 = row("L0_ffn_ln2_w", C), row("L0_ffn_ln2_b", C)
        attention_gate, mlp_gate = gate("L0_ffn_smha"), gate("L0_ffn_moe")
        R = named(raw=sb("router", [P, KT, E]), split=sb("router_split", [P, KT, 2 * E], F32R)[:],
                            bias=row("L1_ffn_router_b", E),
                            expert_b=sb("expert_bias", [P, C]))
        S.sim_tiles.extend((R.raw[:, k, :], a["L1_ffn_router_w"][:, k * P:(k + 1) * P].rearrange("e p -> p e"))
                           for k in range(KT))
        S.expert_b = R.expert_b
        hs_dram = nc.dram_tensor("x_plus_hs", a["x"].shape, F32).ap()

        def weights(own, name, shape):
            return [own.enter_context(nc.sbuf_tensor(f"{name}_{part}", shape, F32R)) for part in ("hi", "lo")]

        names = ("Wq", "Wk", "Wv", "Wo")
        loaded = [S.sem(f"raw{n}_loaded") for n in range(1, 5)]
        load_next = [
            lambda dma: (loaded[0], load_mixture_attention_raw(
                dma, S, *(a[f"L0_ffn_{n}_proj"] for n in "qkvo"), loaded[0])),
            lambda dma: (loaded[1], load_mixture_mlp_raw(dma, S, a["L0_ffn_w1"], a["L0_ffn_w2"], loaded[1])),
            lambda dma: (loaded[2], load_attention_raw(dma, S, [a[f"L1_xattn_{n}"] for n in names], False, loaded[2])),
            lambda dma: (loaded[3], load_experts_raw(dma, S, a["L1_ffn_expert_w"], loaded[3])),
        ]

        setup(nc, S, a, consts)

        with ExitStack() as own:
            W = Named()
            W.hi, W.lo = weights(own, "W0", [P, 4, KT, C])
            attention_weights(nc, S, "W0", W, True)
            ln_scales(nc, S, "ln0")
            attention(nc, S, "L0", a["ctx_1024"], W, B["L0_xattn"], S.count_bf, load_next[0])

        if phases >= 2:
            with ExitStack() as own:
                W = Named()
                W.hi, W.lo = weights(own, "W1", [P, E, KT, 3 * HID])
                W.o_hi, W.o_lo = weights(own, "W1_o", [P, E, C])
                raw = S.raw[:, 0:E * KT * 3 * HID].rearrange("p (e k w) -> p e k w", e=E, k=KT)
                raw_o = S.raw[:, E * KT * 3 * HID:].rearrange("p (e c) -> p e c", e=E)
                split_weights(nc, S, "W1", [(W.hi[:, e], W.lo[:, e], raw[:, e]) for e in range(E)]
                              + [(W.o_hi[:, e:e + 4], W.o_lo[:, e:e + 4], raw_o[:, e:e + 4]) for e in (0, 4)])
                gate_weights(nc, S, "gate1", attention_gate)
                ln_scales(nc, S, "ln1", twice=True)
                mixture_attention(nc, S, "M1", W, attention_gate, *ln1, hs_dram, load_next[1])

        if phases >= 3:
            with ExitStack() as own:
                W = Named()
                W.hi, W.lo = weights(own, "W2", [P, 2, E, KT, C])
                raw = S.raw[:].rearrange("p (w e k c) -> p w e k c", w=2, e=E, k=KT)
                split_weights(nc, S, "W2", [(W.hi[:, w, e:e + 2], W.lo[:, w, e:e + 2], raw[:, w, e:e + 2])
                                            for w in range(2) for e in range(0, E, 2)])
                gate_weights(nc, S, "gate2", mlp_gate)
                ln_scales(nc, S, "ln2")
                mixture_mlp(nc, S, "M2", W, mlp_gate, *ln2, hs_dram, load_next[2])

        if phases >= 4:
            with ExitStack() as own:
                W = Named()
                W.hi, W.lo = weights(own, "W3", [P, 4, KT, C])
                attention_weights(nc, S, "W3", W, False)
                ln_scales(nc, S, "ln3")
                attention(nc, S, "L1", a["ctx_1024"], W, B["L1_xattn"], None, load_next[3])

        if phases >= 5:
            with ExitStack() as own:
                W = Named()
                W.hi, W.lo = weights(own, "W4", [P, KT, E, C])
                expert_weights(nc, S, "W4", W, R)
                ln_scales(nc, S, "ln4")
                routed_experts(nc, S, "M4", W, R, out)
        else:
            store(nc, S, out)


def store(nc, S, out):
    stored = S.sem("out_stored")
    with nc.Block() as block:
        @block.sync
        def _(sp):
            sp.dma_start(out.rearrange("s t c -> t s c"), S.x[:]).then_inc(stored, 16)
            sp.wait_ge(stored, 16)


def kernel(**inputs):
    import concourse.bacc as bacc
    from concourse.bass_utils import run_bass_kernel_spmd
    nc = bacc.Bacc("TRN2", target_bir_lowering=False, num_devices=1)
    arrays, a, consts = {}, {}, {}
    for group, source in ((a, inputs), (consts, host_constants())):
        for name, value in source.items():
            value = np.ascontiguousarray(value)
            arrays[f"in_{name}"] = value
            group[name] = nc.dram_tensor(f"in_{name}", value.shape, mybir.dt.from_np(value.dtype), kind="ExternalInput").ap()
    out = nc.dram_tensor("out", a["x"].shape, F32, kind="ExternalOutput").ap()
    program(nc, a, consts, out)
    return run_bass_kernel_spmd(nc, [arrays], core_ids=[0]).results[0]["out"]
```

```python
from collections import namedtuple
from contextlib import ExitStack

import numpy as np

import concourse.bass as bass
from concourse import mybir

F32 = mybir.dt.float32
F32R = mybir.dt.float32r
ALU = mybir.AluOpType
ACT = mybir.ActivationFunctionType
AX = mybir.AxisListType

P = 128
C = 256
KT = C // P
H = 16
D = C // H
E = 8
HID = 128
UH = 4
UNITS = H // UH
LN_EPS = 1e-5
HIDDEN = 1e30
CHUNK = 8
LARGEST = 3e38


class Named:
    pass


def named(**values):
    return namedtuple("named", values)(*values.values())


def wait(eng, sem, value):
    if isinstance(value, int) and value <= 0:
        return
    eng.wait_ge(sem, value)


def is_(index, value):
    return isinstance(index, int) and index == value


def mm3(pe, out, left, right, first, last):
    pe.matmul(out, left[0], right[0], start=first, stop=False)
    pe.matmul(out, left[1], right[0], start=False, stop=False)
    return pe.matmul(out, left[0], right[1], start=False, stop=last)


def clear(nc, sems):
    with nc.Block() as block:
        @block.sync
        def _(sp):
            for sem in sems:
                sp.sem_clear(sem)


def constants():
    k = np.arange(P)
    causal = k[:, None] <= k[None, :]
    count = np.zeros((P, UNITS, P))
    for j in range(UNITS):
        same2 = (k[:, None] % 2 == j // 2) & (k[None, :] % 2 == j // 2)
        same4 = (k[:, None] % 4 == j) & (k[None, :] % 4 == j)
        count[:, j, :] = causal * (1.0 + same2 + same4)
    ones_half = np.zeros((P, 2, 32))
    ones_half[:, 0, :D] = 1.0
    ones_half[:, 1, D:] = 1.0
    return {
        "ident": np.eye(P),
        "hidden": np.where(causal.T, 0.0, HIDDEN),
        "count": count,
        "ones_half": ones_half,
        "head_rows": (k[:, None] // D == np.arange(P // D)[None, :]) * -D ** -0.5,
        "rank": np.tile(np.arange(E, 0, -1), (P, 2, 1)),
        "minus_half": np.full((P, 2), -0.5),
        "euler": np.full((P, 2, E), np.e),
    }


ROWS = [(f"{L}_xattn_{n}", C) for L in ("L0", "L1") for n in ("bv", "bo")] + [
    (f"L0_ffn_{n}", C) for n in ("ln1_w", "ln1_b", "ln2_w", "ln2_b")] + [
    ("L0_ffn_smha_gates", E), ("L0_ffn_moe_gates", E), ("L1_ffn_router_b", E)]
COLUMNS = [(f"{L}_xattn_{n}", 1) for L in ("L0", "L1") for n in ("bq", "bk")] + [
    ("L0_ffn_smha_sim", E), ("L0_ffn_moe_sim", E), ("L1_ffn_router_w", E)]


def layouts(a):
    on_partitions = lambda w: w.reshape(KT, P, -1).transpose(1, 0, 2).reshape(P, -1)

    def attention_order(w):
        return w.reshape(KT, 2, UH, D, C).transpose(0, 2, 1, 3, 4).reshape(C, C)

    def attention_weights(wq, wk, wv, wo):
        return np.concatenate([on_partitions(w) for w in (wq, wk, wv, attention_order(wo))], 1)

    L0, L1 = ([a[f"{L}_xattn_{n}"] for n in ("Wq", "Wk", "Wv", "Wo")] for L in ("L0", "L1"))
    qkv = np.concatenate([a[f"L0_ffn_{n}_proj"] for n in "qkv"], 2)
    columns = {**a, "L1_ffn_router_w": a["L1_ffn_router_w"].T}
    expert_b = np.zeros((P, C), a["L1_ffn_expert_b"].dtype)
    expert_b[:E] = a["L1_ffn_expert_b"]
    return {
        "x": a["x"], "ctx": a["ctx_1024"],
        "constants": np.concatenate([c.reshape(P, -1).astype(np.float32) for c in constants().values()], 1),
        "rows": np.concatenate([a[n] for n, _ in ROWS]),
        "columns": np.concatenate([on_partitions(columns[n]) for n, _ in COLUMNS], 1),
        "expert_b": expert_b,
        "weights0": attention_weights(*(w.T for w in L0)),
        "weights1": np.concatenate([on_partitions(w) for w in qkv] + [w for w in a["L0_ffn_o_proj"]], 1),
        "weights2": np.concatenate([on_partitions(w) for n in ("w1", "w2") for w in a[f"L0_ffn_{n}"]], 1),
        "weights3": attention_weights(*L1),
        "weights4": np.concatenate([on_partitions(w.T) for w in a["L1_ffn_expert_w"]], 1),
    }


def prepare(nc, S, name, pieces=(), norms=0):
    hi_done = S.sem(f"{name}_hi")
    lo_done = S.sem(f"{name}_lo")
    step = S.sem(f"{name}_step")
    root = S.sem(f"{name}_root")
    even, odd = S.stats[:, :, 0:3], S.stats[:, :, 3:6]
    numbered = list(enumerate(pieces))
    parts = numbered[:2], numbered[2:4], numbered[4:]
    FIRST_VAR, SECOND_VAR = 7, 12

    def rests(eng, some, by_pool):
        for n, (hi, lo, src) in some:
            if (n % 4 == 1 and n + 1 < len(pieces)) == by_pool:
                eng.wait_ge(hi_done, n + 1)
                eng.tensor_tensor(lo, src, hi.bitcast(F32), ALU.subtract).then_inc(lo_done, 1)

    with nc.Block() as block:
        @block.scalar
        def _(act):
            def rounds(some):
                for _, (hi, _, src) in some:
                    act.activation(hi, src, ACT.Copy).then_inc(hi_done, 1)

            rounds(parts[0])
            if norms >= 1:
                act.wait_ge(step, FIRST_VAR)
                act.activation(S.root[:], S.var[:], ACT.Sqrt).then_inc(root, 1)
            rounds(parts[1])
            if norms >= 2:
                act.wait_ge(step, SECOND_VAR)
                act.activation(S.root[:], S.var[:], ACT.Sqrt).then_inc(root, 1)
            rounds(parts[2])

        @block.vector
        def _(dve):
            done = [0]

            def then(ins):
                done[0] += 1
                ins.then_inc(step, 1)
                dve.wait_ge(step, done[0])

            diff, var = S.rstd2, S.var
            if norms >= 1:
                then(dve.tensor_tensor(S.mean[:], even[:, :, 1], odd[:, :, 1], ALU.add))
                then(dve.tensor_tensor(diff[:], even[:, :, 1], odd[:, :, 1], ALU.subtract))
                then(dve.tensor_scalar(S.mean[:], S.mean[:], 0.5, None, ALU.mult))
                then(dve.tensor_tensor(diff[:], diff[:], diff[:], ALU.mult))
                then(dve.tensor_tensor(var[:], even[:, :, 2], odd[:, :, 2], ALU.add))
                then(dve.tensor_scalar(diff[:], diff[:], 0.25, LN_EPS, ALU.mult, ALU.add))
                then(dve.scalar_tensor_tensor(var[:], var[:], 1.0 / C, diff[:], ALU.mult, ALU.add))
            rests(dve, parts[0], False)
            if norms >= 1:
                dve.wait_ge(root, 1)
                then(dve.reciprocal(S.rstd[:], S.root[:]))
            if norms >= 2:
                then(dve.tensor_scalar(var[:], var[:], LN_EPS, None, ALU.subtract))
                then(dve.tensor_tensor(var[:], var[:], S.rstd[:], ALU.mult))
                then(dve.tensor_tensor(var[:], var[:], S.rstd[:], ALU.mult))
                then(dve.tensor_scalar(var[:], var[:], LN_EPS, None, ALU.add))
            rests(dve, parts[1], False)
            if norms >= 2:
                dve.wait_ge(root, 2)
                then(dve.reciprocal(S.rstd2[:], S.root[:]))
                then(dve.tensor_tensor(S.rstd2[:], S.rstd2[:], S.rstd[:], ALU.mult))
            rests(dve, parts[2], False)

        @block.gpsimd
        def _(pool):
            for some in parts:
                rests(pool, some, True)


def attention_pieces(S, W):
    raw = S.raw[:, 0:4 * KT * C].rearrange("p (w k c) -> p w k c", w=4, k=KT)
    return [(W.hi[:, w], W.lo[:, w], raw[:, w]) for w in range(4)]


def attention(nc, S, L, ctx_dram, W, bias, count, load_next):
    NP = S.n_seq // 2
    UP = 2 * UNITS
    with ExitStack() as mem:
        def sb(name, shape, dt=F32):
            return mem.enter_context(nc.sbuf_tensor(f"{L}_{name}", shape, dt))

        own_sems = []

        def sem(name):
            own_sems.append(mem.enter_context(nc.semaphore(f"{L}_{name}")))
            return own_sems[-1]

        normed = sb("normed", [P, 2, C])
        ctx_in = sb("ctx_in", [P, 2, 2, C])
        n_raw, c_raw = sb("nT", [P, KT, 2 * P]), sb("cT", [P, KT, 2 * P])
        nT = [sb("nT_hi", [P, KT, 2 * P], F32R), sb("nT_lo", [P, KT, 2 * P], F32R)]
        cT = [sb("cT_hi", [P, KT, 2 * P], F32R), sb("cT_lo", [P, KT, 2 * P], F32R)]
        q_sb = sb("q", [P, KT, 2 * P])
        q_heads = sb("q_heads", [P, 2, KT, P // D, P])
        kT = sb("kT", [P, 2, KT, 2 * P])
        v_pad = sb("v_pad", [P, 2, 2, H * 32])
        masked = sb("masked", [P, 2, UH, P])
        probs = sb("probs", [P, 2, UH, P])
        probsT = sb("probsT", [P, 2, UH, P])
        neg_max = sb("neg_max", [P, 2, UH])
        o_raw, sum_raw, recip = sb("o_raw", [P, KT, P]), sb("sum", [P, KT, P]), sb("recip", [P, KT, P])
        o_sb = sb("o", [P, KT, P])
        oT = [sb("oT_hi", [P, KT, P], F32R), sb("oT_lo", [P, KT, P], F32R)]

        scores = [S.bank[0].rearrange("p (h k) -> p h k", h=UH), S.bank[1].rearrange("p (h k) -> p h k", h=UH)]
        pT_ps = [S.bank[2].rearrange("p (h k) -> p h k", h=UH), S.bank[3].rearrange("p (h k) -> p h k", h=UH)]
        o_ps = S.bank[4][:, 0:KT * P].rearrange("p (m q) -> p m q", q=P)
        sum_ps = S.bank[5][:, 0:KT * P].rearrange("p (m q) -> p m q", q=P)
        bank_a, bank_b = S.bank[6], S.bank[7]
        tiles = lambda bank: bank.rearrange("p (k t) -> p k t", k=KT)

        ctx_loaded = [sem("ctx_even_loaded"), sem("ctx_odd_loaded")]
        n_ready, bo_added, x_done = sem("n_ready"), sem("bo_added"), sem("x_done")
        tn_ready, tc_ready = sem("tn_ready"), sem("tc_ready")
        nhi_ready, nlo_ready = sem("nhi_ready"), sem("nlo_ready")
        chi_ready, clo_ready = sem("chi_ready"), sem("clo_ready")
        q_made, k_made, v_made = sem("q_made"), sem("k_made"), sem("v_made")
        q_ready, kT_ready, v_ready, v_cleared = sem("q_ready"), sem("kT_ready"), sem("v_ready"), sem("v_cleared")
        q_heads_ready = sem("q_heads_ready")
        scores_ready, max_ready, exp_done = sem("scores_ready"), sem("max_ready"), sem("exp_done")
        pT_made, pv_done, o_kept = sem("pT_made"), sem("pv_done"), sem("o_kept")
        pT_ready = [sem("pT_even_ready"), sem("pT_odd_ready")]
        pT_count = lambda p, u: UP // 2 * p + u // 2
        recip_done, o_done, o_ready = sem("recip_done"), sem("o_done"), sem("o_ready")
        y_made, stats_done = sem("y_made"), sem("stats_done")

        def pairs(eng, step):
            for b in range(2):
                step(b, b)
            if NP > 4:
                with eng.Fori(1, NP // 2 - 1) as i:
                    for b in range(2):
                        step(2 * i + b, b)
            for b in range(2):
                step(NP - 2 + b, b)

        with nc.Block() as block:
            @block.sync
            def _(sp):
                def load(p, b):
                    wait(sp, tc_ready, p - 1)
                    sp.dma_start(ctx_in[:, b], ctx_dram[bass.ds(2 * p, 2)].rearrange("s t c -> t s c")
                                 ).then_inc(ctx_loaded[b], 16)
                load(0, 0)
                load(1, 1)
                next_loaded = load_next(sp)
                if NP > 4:
                    with sp.Fori(1, NP // 2 - 1) as i:
                        for b in range(2):
                            load(2 * i + b, b)
                for b in range(2):
                    load(NP - 2 + b, b)
                wait(sp, *next_loaded)

            @block.tensor
            def _(pe):
                def turn_n(p):
                    wait(pe, n_ready, p + 1)
                    wait(pe, v_ready, p)
                    for k in range(KT):
                        for s in range(2):
                            last = pe.transpose(tiles(bank_a)[:, k, s * P:(s + 1) * P],
                                                normed[:, s, k * P:(k + 1) * P], S.ident[:])
                    last.then_inc(tn_ready, 1)

                def turn_c(p, b):
                    wait(pe, ctx_loaded[b], 8 * (p - b) + 16)
                    wait(pe, x_done, 2 * p - 3)
                    for k in range(KT):
                        for s in range(2):
                            last = pe.transpose(tiles(bank_b)[:, k, s * P:(s + 1) * P],
                                                ctx_in[:, b, s, k * P:(k + 1) * P], S.ident[:])
                    last.then_inc(tc_ready, 1)

                def project_q(p):
                    wait(pe, nlo_ready, p + 1)
                    for m in range(KT):
                        for k in range(KT):
                            last = mm3(pe, tiles(bank_a)[:, m, :],
                                       [w[:, 0, k, m * P:(m + 1) * P] for w in (W.hi, W.lo)],
                                       [t[:, k, :] for t in nT], k == 0, k == KT - 1)
                    last.then_inc(q_made, 1)

                def project_k(p):
                    wait(pe, clo_ready, p + 1)
                    for m in range(KT):
                        for k in range(KT):
                            last = mm3(pe, tiles(bank_b)[:, m, :],
                                       [w[:, 1, k, m * P:(m + 1) * P] for w in (W.hi, W.lo)],
                                       [t[:, k, :] for t in cT], k == 0, k == KT - 1)
                    last.then_inc(k_made, 1)

                def project_v(p, s):
                    if s == 0:
                        wait(pe, q_ready, p + 1)
                        wait(pe, x_done, 2 * p - 2)
                    for k in range(KT):
                        last = mm3(pe, tiles(bank_a)[:, s, :], [t[:, k, s * P:(s + 1) * P] for t in cT],
                                   [w[:, 2, k, :] for w in (W.hi, W.lo)], k == 0, k == KT - 1)
                    if s == 1:
                        last.then_inc(v_made, 1)

                def project_o(p, s):
                    wait(pe, o_ready, 2 * p + s + 1)
                    if s == 0:
                        pe.wait_ge(kT_ready, NP if is_(p, NP - 1) else p + 2)
                    elif is_(p, NP - 1):
                        pe.wait_ge(x_done, 2 * p)
                    elif is_(p, NP - 2):
                        pe.wait_ge(v_ready, NP)
                    else:
                        pe.wait_ge(q_ready, p + 3)
                    out = (bank_b, bank_a)[s][:, 0:C]
                    for k in range(KT):
                        last = mm3(pe, out, [t[:, k, :] for t in oT], [w[:, 3, k, :] for w in (W.hi, W.lo)],
                                   k == 0, k == KT - 1)
                    last.then_inc(y_made, 1)

                def score(p, b, u):
                    s, j = divmod(u, UNITS)
                    wait(pe, max_ready, UP * p + u - 1)
                    if u % UNITS == 0:
                        pe.wait_ge(q_heads_ready, 2 * p + s + 1)
                    if u == 0:
                        pe.wait_ge(kT_ready, p + 1)
                    bank = scores[u % 2]
                    for i in range(UH):
                        last = pe.matmul(bank[:, i, :], q_heads[:, s, j // 2, (j % 2) * UH + i, :],
                                         kT[:, b, j // 2, s * P:(s + 1) * P], start=True, stop=True)
                    last.then_inc(scores_ready, 1)

                def turn_p(p, u):
                    wait(pe, exp_done, UP * p + u + 1)
                    wait(pe, pT_ready[u % 2], pT_count(p, u))
                    for i in range(UH):
                        last = pe.transpose(pT_ps[u % 2][:, i, :], probs[:, u % 2, i, :], S.ident[:])
                    last.then_inc(pT_made, 1)

                def times_v(p, b, u):
                    s, j = divmod(u, UNITS)
                    m, e = divmod(j, 2)
                    wait(pe, pT_ready[u % 2], pT_count(p, u) + 1)
                    if j == 0:
                        wait(pe, o_kept, 2 * p + s)
                    if u == 0:
                        pe.wait_ge(v_ready, p + 1)
                    for to_sum in range(2):
                        for i in range(UH):
                            h = UH * j + i
                            left = S.ones_half[:, e, :] if to_sum else v_pad[:, b, s, h * 32:(h + 1) * 32]
                            out = (o_ps, sum_ps)[to_sum][32 * i:32 * (i + 1), m, :]
                            last = pe.matmul(out, left, probsT[:, u % 2, i, :], start=e == 0, stop=e == 1)
                    last.then_inc(pv_done, 1)

                def step(p, b):
                    first = is_(p, 0)
                    more = not is_(p, NP - 1)
                    for k in range(UP):
                        score(p, b, k)
                        if k >= 1:
                            turn_p(p, k - 1)
                        elif not first:
                            turn_p(p - 1, UP - 1)
                        if k == 0 and not first:
                            project_o(p - 1, 0)
                        if k == 1 and more:
                            turn_n(p + 1)
                        if k == 2 and more:
                            turn_c(p + 1, 1 - b)
                        if k == 3 and more:
                            project_q(p + 1)
                        if k == 4 and not first:
                            project_o(p - 1, 1)
                        if k == 5 and more:
                            project_k(p + 1)
                        if k == 6 and more:
                            project_v(p + 1, 0)
                        if k == 7 and more:
                            project_v(p + 1, 1)
                        if k >= 2:
                            times_v(p, b, k - 2)
                        elif not first:
                            times_v(p - 1, 1 - b, UP - 2 + k)

                turn_n(0)
                turn_c(0, 0)
                project_q(0)
                project_k(0)
                project_v(0, 0)
                project_v(0, 1)
                pairs(pe, step)
                turn_p(NP - 1, UP - 1)
                times_v(NP - 1, 1, UP - 2)
                times_v(NP - 1, 1, UP - 1)
                for s in range(2):
                    project_o(NP - 1, s)

            @block.scalar
            def _(act):
                def round_n(p):
                    act.wait_ge(tn_ready, p + 1)
                    wait(act, q_made, p)
                    act.activation(n_raw[:], tiles(bank_a), ACT.Copy)
                    act.activation(nT[0][:], tiles(bank_a), ACT.Copy).then_inc(nhi_ready, 1)

                def round_c(p):
                    act.wait_ge(tc_ready, p + 1)
                    wait(act, v_made, p)
                    act.activation(c_raw[:], tiles(bank_b), ACT.Copy)
                    act.activation(cT[0][:], tiles(bank_b), ACT.Copy).then_inc(chi_ready, 1)

                def keep_q(p):
                    act.wait_ge(q_made, p + 1)
                    wait(act, q_heads_ready, 2 * p)
                    for m in range(KT):
                        last = act.activation(q_sb[:, m, :], tiles(bank_a)[:, m, :], ACT.Identity,
                                              bias=bias.q[:, m:m + 1])
                    last.then_inc(q_ready, 1)

                def keep_k(p, b):
                    act.wait_ge(k_made, p + 1)
                    wait(act, scores_ready, UP * (p - 1))
                    for m in range(KT):
                        last = act.activation(kT[:, b, m, :], tiles(bank_b)[:, m, :], ACT.Identity,
                                              bias=bias.k[:, m:m + 1])
                    last.then_inc(kT_ready, 1)

                def exps(p, u):
                    act.wait_ge(max_ready, UP * p + u + 1)
                    wait(act, pT_made, UP * p + u - 1)
                    for i in range(UH):
                        last = act.activation(probs[:, u % 2, i, :], masked[:, u % 2, i, :], ACT.Exp,
                                              bias=neg_max[:, u % 2, i:i + 1], scale=-1.0)
                    last.then_inc(exp_done, 1)

                def keep_p(p, u):
                    act.wait_ge(pT_made, UP * p + u + 1)
                    wait(act, pv_done, UP * p + u - 1)
                    act.activation(probsT[:, u % 2], pT_ps[u % 2], ACT.Copy).then_inc(pT_ready[u % 2], 1)

                def keep_o(p, s):
                    n = 2 * p + s
                    act.wait_ge(pv_done, UP * p + (s + 1) * UNITS)
                    wait(act, o_done, n)
                    act.activation(sum_raw[:], sum_ps, ACT.Copy)
                    act.activation(o_raw[:], o_ps, ACT.Copy).then_inc(o_kept, 1)

                def step(p, b):
                    first = is_(p, 0)
                    more = not is_(p, NP - 1)
                    for k in range(UP):
                        exps(p, k)
                        if count is None and k % 2 == 0:
                            if k >= 2:
                                keep_p(p, k - 1)
                            elif not first:
                                keep_p(p - 1, UP - 1)
                        if k == 1:
                            if more:
                                round_n(p + 1)
                            if not first:
                                keep_o(p - 1, 1)
                        if k == 2 and more:
                            round_c(p + 1)
                        if k == 3 and more:
                            keep_q(p + 1)
                        if k == 5:
                            if more:
                                keep_k(p + 1, 1 - b)
                            keep_o(p, 0)

                round_n(0)
                round_c(0)
                keep_q(0)
                keep_k(0, 0)
                pairs(act, step)
                if count is None:
                    keep_p(NP - 1, UP - 1)
                keep_o(NP - 1, 1)

            @block.vector
            def _(dve):
                def norm(p):
                    wait(dve, tn_ready, p)
                    for s in range(2):
                        q = 2 * p + s
                        last = dve.tensor_scalar(normed[:, s, :], S.x[:, q, :], S.mean[:, bass.ds(q, 1)],
                                                 S.rstd[:, bass.ds(q, 1)], ALU.subtract, ALU.mult)
                    last.then_inc(n_ready, 1)

                def keep_v(p, b):
                    dve.wait_ge(v_made, p + 1)
                    wait(dve, pv_done, UP * (p - 1))
                    for s in range(2):
                        for m in range(KT):
                            out = v_pad[:, b, s, m * 256:(m + 1) * 256]
                            src = tiles(bank_a)[:, s, m * P:(m + 1) * P].rearrange("p (e i d) -> p e i d", e=2, i=UH)
                            add = bias.v[:, m * P:(m + 1) * P].rearrange("p (e i d) -> p e i d", e=2, i=UH)
                            for e in range(2):
                                half = out[:, e * P:(e + 1) * P].rearrange("p (i z) -> p i z", i=UH)
                                last = dve.tensor_tensor(half[:, :, e * D:(e + 1) * D], src[:, e], add[:, e], ALU.add)
                    last.then_inc(v_ready, 1)

                def row_max(p, u):
                    dve.wait_ge(scores_ready, UP * p + u + 1)
                    wait(dve, exp_done, UP * p + u - 1)
                    dve.memset(S.carrier[:, u % 2:u % 2 + 1], 0.0)
                    for i in range(UH):
                        last = dve.tensor_tensor_reduce(masked[:, u % 2, i, :], scores[u % 2][:, i, :], S.hidden[:], 1.0,
                                                        LARGEST, ALU.add, ALU.min, neg_max[:, u % 2, i:i + 1])
                    last.then_inc(max_ready, 1)

                def keep_p(p, u):
                    dve.wait_ge(pT_made, UP * p + u + 1)
                    wait(dve, pv_done, UP * p + u - 1)
                    if count is None:
                        last = dve.tensor_copy(probsT[:, u % 2], pT_ps[u % 2])
                    else:
                        seen = count[:, u % UNITS, :].unsqueeze(1).broadcast_to([P, UH, P])
                        last = dve.tensor_tensor(probsT[:, u % 2], pT_ps[u % 2], seen, ALU.mult)
                    last.then_inc(pT_ready[u % 2], 1)

                def invert(p, s, m):
                    dve.wait_ge(o_kept, 2 * p + s + 1)
                    dve.reciprocal(recip[:, m, :], sum_raw[:, m, :]).then_inc(recip_done, 1)

                def residual(p, s):
                    n = 2 * p + s
                    y = (bank_b, bank_a)[s][:, 0:C]
                    dve.wait_ge(y_made, n + 1)
                    dve.wait_ge(bo_added, p + 1)
                    dve.tensor_tensor(S.x[:, n, :], y, S.x[:, n, :], ALU.add).then_inc(x_done, 1)
                    dve.wait_ge(x_done, n + 1)

                def stats(p, s):
                    n = 2 * p + s
                    dve.bn_stats(S.stats[:, n, :], S.x[:, n, :]).then_inc(stats_done, 1)

                def step(p, b):
                    first = is_(p, 0)
                    more = not is_(p, NP - 1)
                    more2 = not (is_(p, NP - 1) or is_(p, NP - 2))
                    for k in range(UP):
                        row_max(p, k)
                        if k == 1 and not first:
                            residual(p - 1, 0)
                        if k == 2 and not first:
                            invert(p - 1, 1, 0)
                        if k == 5 and not first:
                            residual(p - 1, 1)
                        if k == 6:
                            invert(p, 0, 0)
                        if count is None and k % 2 == 0:
                            pass
                        elif k >= 1:
                            keep_p(p, k - 1)
                        elif not first:
                            keep_p(p - 1, UP - 1)
                        if k == 0 and not first:
                            keep_v(p, b)
                        if k == 1 and not first:
                            stats(p - 1, 0)
                        if k == 2 and not first:
                            invert(p - 1, 1, 1)
                        if k == 3 and more2:
                            norm(p + 2)
                        if k == 5 and not first:
                            stats(p - 1, 1)
                        if k == 6:
                            invert(p, 0, 1)

                norm(0)
                dve.memset(v_pad[:], 0.0).then_inc(v_cleared, 1)
                norm(1)
                dve.wait_ge(v_cleared, 1)
                keep_v(0, 0)
                pairs(dve, step)
                if count is not None:
                    keep_p(NP - 1, UP - 1)
                residual(NP - 1, 0)
                stats(NP - 1, 0)
                for m in range(KT):
                    invert(NP - 1, 1, m)
                residual(NP - 1, 1)
                stats(NP - 1, 1)

            @block.gpsimd
            def _(pool):
                def spread_q(p, s):
                    pool.wait_ge(q_ready, p + 1)
                    wait(pool, scores_ready, UP * (p - 1) + (s + 1) * UNITS)
                    for m in range(KT):
                        last = pool.tensor_tensor(
                            q_heads[:, s, m],
                            q_sb[:, m, s * P:(s + 1) * P].unsqueeze(1).broadcast_to([P, P // D, P]),
                            S.head_rows[:].unsqueeze(2).broadcast_to([P, P // D, P]), ALU.mult)
                    last.then_inc(q_heads_ready, 1)

                def add_bo(p):
                    pool.wait_ge(n_ready, p + 1)
                    for s in range(2):
                        n = 2 * p + s
                        last = pool.tensor_tensor(S.x[:, n, :], S.x[:, n, :], bias.o[:], ALU.add)
                    last.then_inc(bo_added, 1)

                def normalize(p, s):
                    n = 2 * p + s
                    pool.wait_ge(recip_done, KT * (n + 1))
                    wait(pool, y_made, n)
                    pool.tensor_tensor(o_sb[:], o_raw[:], recip[:], ALU.mult)
                    pool.tensor_tensor(oT[0][:], o_raw[:], recip[:], ALU.mult).then_inc(o_done, 1)
                    pool.wait_ge(o_done, n + 1)
                    pool.tensor_tensor(oT[1][:], o_sb[:], oT[0][:].bitcast(F32), ALU.subtract).then_inc(o_ready, 1)

                def rest_n(p):
                    pool.wait_ge(nhi_ready, p + 1)
                    pool.tensor_tensor(nT[1][:], n_raw[:], nT[0][:].bitcast(F32), ALU.subtract).then_inc(nlo_ready, 1)

                def rest_c(p):
                    pool.wait_ge(chi_ready, p + 1)
                    pool.tensor_tensor(cT[1][:], c_raw[:], cT[0][:].bitcast(F32), ALU.subtract).then_inc(clo_ready, 1)

                def step(p, b):
                    more = not is_(p, NP - 1)
                    add_bo(p)
                    if more:
                        rest_n(p + 1)
                    if not is_(p, 0):
                        normalize(p - 1, 1)
                    if more:
                        rest_c(p + 1)
                        spread_q(p + 1, 0)
                    normalize(p, 0)
                    if more:
                        spread_q(p + 1, 1)

                rest_n(0)
                rest_c(0)
                for s in range(2):
                    spread_q(0, s)
                pairs(pool, step)
                normalize(NP - 1, 1)
        clear(nc, own_sems)


def gate_weights(nc, S, name, G):
    step, squares, root = (S.sem(f"{name}_{n}") for n in ("step", "squares", "root"))
    with nc.sbuf_tensor(f"{name}_ones", [P, P], F32) as ones, nc.Block() as block:
        @block.vector
        def _(dve):
            n = [0]

            def then(ins):
                n[0] += 1
                ins.then_inc(step, 1)
                dve.wait_ge(step, n[0])

            dve.memset(ones[:], 1.0)
            then(dve.tensor_tensor(G.work[:], G.sim[:], G.sim[:], ALU.mult))
            dve.wait_ge(squares, 1)
            then(dve.tensor_copy(G.norm[:], S.bank[0][:, 0:E]))
            then(dve.tensor_tensor(G.norm[:], S.bank[0][:, E:2 * E], G.norm[:], ALU.add))
            dve.wait_ge(root, 1)
            then(dve.tensor_scalar(G.norm[:], G.norm[:], 1e-12, None, ALU.max))
            then(dve.reciprocal(G.norm[:], G.norm[:]))
            then(dve.tensor_tensor(G.sim[:], G.sim[:], G.norm[:].unsqueeze(1).broadcast_to([P, KT, E]), ALU.mult))
            hi, lo = G.split[:, :, 0:E], G.split[:, :, E:2 * E]
            then(dve.tensor_copy(hi, G.sim[:]))
            then(dve.tensor_tensor(lo, G.sim[:], hi.bitcast(F32), ALU.subtract))
            dve.wait_ge(root, 2)
            then(dve.tensor_scalar(G.gates[:], G.gates[:], 1.0, None, ALU.add))
            then(dve.reciprocal(G.gates[:], G.gates[:]))

        @block.tensor
        def _(pe):
            pe.wait_ge(step, 1)
            pe.matmul(S.bank[0][:, 0:KT * E], ones[:], G.work[:].rearrange("p k e -> p (k e)"),
                      start=True, stop=True).then_inc(squares, 1)

        @block.scalar
        def _(act):
            act.wait_ge(step, 3)
            act.activation(G.norm[:], G.norm[:], ACT.Sqrt).then_inc(root, 1)
            act.activation(G.gates[:], G.gates[:], ACT.Exp, scale=-1.0).then_inc(root, 1)


GATE_BEFORE, GATE_STEPS = 6, 11


def gate_tiles(sb, n):
    one = {f: sb(f"gate_{f}", [P, n]) for f in ("square_sum", "squared", "rnorm", "peak", "none", "total")}
    all_ = {f: sb(f"gate_{f}", [P, n, E]) for f in ("partial", "logit", "gated", "best", "tied", "above", "key", "order",
                                                    "active", "shifted", "exp")}
    return named(n=n, **one, **all_)


def gate_products(pe, out, left, columns):
    for k in range(KT):
        pe.matmul(out, left[0][k], columns[:, k, :], start=k == 0, stop=False)
        last = pe.matmul(out[:, 0:E], left[1][k], columns[:, k, 0:E], start=False, stop=k == KT - 1)
    return last


def gate_chain(dve, step, index, at):
    n = [at]

    def then(ins):
        n[0] += 1
        ins.then_inc(step, 1)
        dve.wait_ge(step, GATE_STEPS * index + n[0])
    return then


def gate_before(S, dve, T, G, dots, step, index):
    then = gate_chain(dve, step, index, 0)
    each = range(T.n)
    ts, stt = dve.tensor_scalar, dve.scalar_tensor_tensor
    for i in each:
        last = stt(T.partial[:, i, :], dots[:, i, E:2 * E], T.rnorm[:, i:i + 1], G.gates[:], ALU.mult, ALU.subtract)
    then(last)
    for i in each:
        last = stt(T.logit[:, i, :], dots[:, i, 0:E], T.rnorm[:, i:i + 1], T.partial[:, i, :], ALU.mult, ALU.add)
    then(last)
    ts(T.gated[:], T.logit[:], 0.0, None, ALU.max)
    for i in each:
        last = dve.max(T.best[:, i, :], T.logit[:, i, :])
    then(last)
    for i in each:
        second = T.best[:, i, 1:2]
        stt(T.tied[:, i, :], T.logit[:, i, :], second, S.rank[:, i, :], ALU.is_ge, ALU.mult)
        ts(T.above[:, i, :], T.logit[:, i, :], second, 2.0 * E, ALU.is_gt, ALU.mult)
    ts(T.peak[:], T.best[:, :, 0], 0.0, None, ALU.max)
    then(ts(T.none[:], T.best[:, :, 0], 0.0, None, ALU.is_le))
    then(dve.tensor_tensor(T.key[:], T.tied[:], T.above[:], ALU.add))
    for i in each:
        ts(T.shifted[:, i, :], T.gated[:, i, :], T.peak[:, i:i + 1], None, ALU.subtract)
    for i in each:
        last = dve.max(T.order[:, i, :], T.key[:, i, :])
    then(last)


def gate_after(dve, T, out, exp_done, step, index, ready):
    then = gate_chain(dve, step, index, GATE_BEFORE)
    each = range(T.n)
    ts = dve.tensor_scalar
    for i in each:
        last = ts(T.active[:, i, :], T.key[:, i, :], T.order[:, i, 1:2], T.none[:, i:i + 1], ALU.is_ge, ALU.mult)
    then(last)
    then(dve.scalar_tensor_tensor(T.active[:], T.logit[:], 0.0, T.active[:], ALU.is_gt, ALU.add))
    dve.wait_ge(exp_done, index + 1)
    then(dve.tensor_tensor(T.exp[:], T.exp[:], T.active[:], ALU.mult))
    then(dve.tensor_reduce(T.total[:], T.exp[:], AX.X, ALU.add))
    then(dve.reciprocal(T.total[:], T.total[:]))
    for i in each:
        last = ts(out[:, i, :], T.exp[:, i, :], T.total[:, i:i + 1], None, ALU.mult)
    last.then_inc(ready, 1)


def parities(eng, count, step, ahead=2, begin=0):
    for n in range(begin, ahead):
        step(n, n % 2)
    if count > ahead + 4:
        with eng.Fori(ahead // 2, count // 2 - 2) as i:
            for b in range(2):
                step(2 * i + b, b)
    for n in range(max(ahead, count - 4), count):
        step(n, n % 2)


def mixture_attention(nc, S, L, W, G, ln_w, ln_b, hs_dram, load_next):
    NS = S.n_seq
    Q3 = 3 * HID
    with ExitStack() as mem:
        def sb(name, shape, dt=F32):
            return mem.enter_context(nc.sbuf_tensor(f"{L}_{name}", shape, dt))

        own_sems = []

        def sem(name):
            own_sems.append(mem.enter_context(nc.semaphore(f"{L}_{name}")))
            return own_sems[-1]

        normed = sb("normed", [P, 2, C])
        square = sb("square", [P, C])
        nT = [sb("nT_hi", [P, 2, KT, P], F32R), sb("nT_lo", [P, 2, KT, P], F32R)]
        T = gate_tiles(sb, 1)
        rw = sb("rw", [P, 2, 1, E])
        rw_out = sb("rw_out", [P, 2, E])
        qkv = sb("qkv", [P, 2, Q3])
        qkv_odd = sb("qkv_odd", [P, 2, Q3])
        qkv_part = sb("qkv_part", [P, 3, Q3])
        qkT = sb("qkT", [P, 2, P])
        neg_max, row_sum, row_scale = sb("neg_max", [P, 1]), sb("row_sum", [P, 1]), sb("row_scale", [P, 1])
        masked, probs, probsT = sb("masked", [P, P]), sb("probs", [P, P]), sb("probsT", [P, P])
        attn = sb("attn", [P, HID])
        aT = [sb("aT_hi", [P, P], F32R), sb("aT_lo", [P, P], F32R)]
        y = sb("y", [P, C])
        hs_even, hs_odd, hs = sb("hs_even", [P, C]), sb("hs_odd", [P, C]), sb("hs", [P, 2, C])
        out_part = sb("out_part", [P, 3, C])
        seq_stats = sb("seq_stats", [P, 6])

        nT_ps = S.bank[0][:, 0:C].rearrange("p (k t) -> p k t", k=KT)
        dots_ps = S.bank[0][:, C:C + 2 * E]
        qkT_ps = S.bank[1][:, 0:2 * P].rearrange("p (k t) -> p k t", k=2)
        aT_ps = S.bank[1][:, 0:P]
        scores, attn_ps, pT_ps = S.bank[2][:, 0:P], S.bank[2][:, 0:HID], S.bank[3][:, 0:P]
        q_bank = [S.bank[4][:, 0:Q3], S.bank[5][:, 0:Q3]]
        o_bank = [S.bank[6].rearrange("p (e c) -> p e c", e=2), S.bank[7].rearrange("p (e c) -> p e c", e=2)]

        names = ("n_made scaled n_ready squared guarded rooted tn_ready nhi_ready nlo_ready dots_made "
                 "gate_step gate_exp gate_ready kept q_even_made q_odd_made even_added odd_read odd_added "
                 "qkv_ready turned qkT_ready scored max_ready exp_done recip_done pT_made pT_ready attn_made "
                 "attn_ready aT_made ahi_ready alo_ready o_even_made o_odd_made o_even_added o_odd_read "
                 "o_odd_added y_ready hs_ready x_added stats_done").split()
        M = named(**{n: sem(n) for n in names})
        hs_stored = [sem("hs_even_stored"), sem("hs_odd_stored")]
        has = lambda s, ahead: not any(is_(s, NS - 1 - d) for d in range(ahead))

        with nc.Block() as block:
            @block.sync
            def _(sp):
                next_loaded = load_next(sp)

                def step(s, b):
                    sp.wait_ge(M.hs_ready, s + 1)
                    sp.dma_start(hs_dram[bass.ds(s, 1)].rearrange("s t c -> (s t) c"), hs[:, b]
                                 ).then_inc(hs_stored[b], 16)
                parities(sp, NS, step)
                for b in range(2):
                    sp.wait_ge(hs_stored[b], 8 * NS)
                wait(sp, *next_loaded)

            @block.tensor
            def _(pe):
                def turn_n(s, b):
                    pe.wait_ge(M.n_ready, s + 1)
                    wait(pe, M.gate_step, GATE_STEPS * (s - 1) + 2)
                    for k in range(KT):
                        last = pe.transpose(nT_ps[:, k, :], normed[:, b, k * P:(k + 1) * P], S.ident[:])
                    last.then_inc(M.tn_ready, 1)

                def dot_gate(s, b):
                    pe.wait_ge(M.nlo_ready, s + 1)
                    gate_products(pe, dots_ps, [[t[:, b, k, :] for k in range(KT)] for t in nT], G.split
                                  ).then_inc(M.dots_made, 1)

                def project(s, b, e):
                    if e % 2 == 0:
                        wait(pe, M.even_added, 4 * s + e // 2)
                    else:
                        wait(pe, M.odd_read, 4 * s + e // 2)
                    for k in range(KT):
                        last = mm3(pe, q_bank[e % 2], [t[:, b, k, :] for t in nT],
                                   [w[:, e, k, :] for w in (W.hi, W.lo)], k == 0, k == KT - 1)
                    last.then_inc((M.q_even_made, M.q_odd_made)[e % 2], 1)

                def turn_qk(s, b):
                    pe.wait_ge(M.qkv_ready, s + 1)
                    wait(pe, M.alo_ready, s)
                    for n in range(2):
                        last = pe.transpose(qkT_ps[:, n, :], qkv[:, b, n * HID:(n + 1) * HID], S.ident[:])
                    last.then_inc(M.turned, 1)

                def score(s):
                    pe.wait_ge(M.qkT_ready, s + 1)
                    wait(pe, M.attn_ready, s)
                    pe.matmul(scores, qkT[:, 0, :], qkT[:, 1, :], start=True, stop=True).then_inc(M.scored, 1)

                def turn_p(s):
                    pe.wait_ge(M.exp_done, s + 1)
                    wait(pe, M.pT_ready, s)
                    pe.transpose(pT_ps, probs[:], S.ident[:]).then_inc(M.pT_made, 1)

                def times_v(s, b):
                    pe.wait_ge(M.pT_ready, s + 1)
                    pe.matmul(attn_ps, probsT[:], qkv[:, b, 2 * HID:Q3], start=True, stop=True).then_inc(M.attn_made, 1)

                def turn_a(s):
                    pe.wait_ge(M.attn_ready, s + 1)
                    pe.transpose(aT_ps, attn[:], S.ident[:]).then_inc(M.aT_made, 1)

                def project_out(s, n):
                    if n == 0:
                        pe.wait_ge(M.alo_ready, s + 1)
                    if n % 2 == 0:
                        wait(pe, M.o_even_added, 4 * s + n)
                    else:
                        wait(pe, M.o_odd_read, 4 * s + n - 1)
                    mm3(pe, S.bank[6 + n % 2], [t[:] for t in aT],
                        [w[:, 2 * n:2 * n + 2, :].rearrange("p e c -> p (e c)") for w in (W.o_hi, W.o_lo)],
                        True, True).then_inc((M.o_even_made, M.o_odd_made)[n % 2], 1)

                def step(s, b):
                    first, one, two = is_(s, 0), has(s, 1), has(s, 2)
                    for e in range(E):
                        if one:
                            project(s + 1, 1 - b, e)
                        if e == 0 and two:
                            turn_n(s + 2, b)
                        if e == 1:
                            turn_qk(s, b)
                        if e == 2:
                            score(s)
                        if e == 4:
                            turn_p(s)
                        if e == 5:
                            times_v(s, b)
                        if e == 6:
                            turn_a(s)
                        if e in (0, 2, 3, 5) and not first:
                            project_out(s - 1, (0, 2, 3, 5).index(e))
                        if e == 2 and two:
                            dot_gate(s + 2, b)

                for s in range(2):
                    turn_n(s, s)
                    dot_gate(s, s)
                for e in range(E):
                    project(0, 0, e)
                parities(pe, NS, step, 4)
                for n in range(E // 2):
                    project_out(NS - 1, n)

            @block.scalar
            def _(act):
                def squares(s, b):
                    act.wait_ge(M.n_ready, s + 1)
                    wait(act, M.guarded, s)
                    act.activation(square[:], normed[:, b, :], ACT.Square, accum_out=T.square_sum[:]).then_inc(M.squared, 1)

                def round_n(s, b):
                    act.wait_ge(M.tn_ready, s + 1)
                    wait(act, M.q_odd_made, 4 * (s - 1))
                    act.activation(nT[0][:, b], nT_ps, ACT.Copy).then_inc(M.nhi_ready, 1)

                def gate_exp(s):
                    act.wait_ge(M.gate_step, GATE_STEPS * s + GATE_BEFORE)
                    act.activation(T.exp[:], T.shifted[:], ACT.Exp).then_inc(M.gate_exp, 1)

                def weigh_odd(s, b, e):
                    act.wait_ge(M.q_odd_made, 4 * s + e // 2 + 1)
                    if e == 1:
                        act.wait_ge(M.gate_ready, s + 1)
                        wait(act, M.qkv_ready, s - 1)
                        out = qkv_odd[:, b, :]
                    else:
                        wait(act, M.odd_added, 3 * (s - 1) + e // 2)
                        out = qkv_part[:, e // 2 - 1, :]
                    act.activation(out, q_bank[1], ACT.Copy, scale=rw[:, b, 0, e:e + 1]).then_inc(M.odd_read, 1)

                def keep_qk(s):
                    act.wait_ge(M.turned, s + 1)
                    wait(act, M.scored, s)
                    act.activation(qkT[:, 0, :], qkT_ps[:, 0, :], ACT.Copy, scale=-float(HID) ** -0.5)
                    act.activation(qkT[:, 1, :], qkT_ps[:, 1, :], ACT.Copy).then_inc(M.qkT_ready, 1)

                def exps(s):
                    act.wait_ge(M.max_ready, s + 1)
                    wait(act, M.pT_made, s)
                    wait(act, M.recip_done, s)
                    act.activation(probs[:], masked[:], ACT.Exp, bias=neg_max[:], scale=-1.0, accum_out=row_sum[:]).then_inc(M.exp_done, 1)

                def keep_p(s):
                    act.wait_ge(M.pT_made, s + 1)
                    wait(act, M.attn_made, s)
                    act.activation(probsT[:], pT_ps, ACT.Copy).then_inc(M.pT_ready, 1)

                def round_a(s):
                    act.wait_ge(M.aT_made, s + 1)
                    wait(act, M.o_odd_made, 2 * s)
                    act.activation(aT[0][:], aT_ps, ACT.Copy).then_inc(M.ahi_ready, 1)

                def weigh_out(s, b, n):
                    act.wait_ge(M.o_odd_made, 2 * s + n // 2 + 1)
                    for i in range(2):
                        e = 2 * n + i
                        part = 2 * (n // 2) + i - 1
                        if part < 0:
                            act.wait_ge(M.kept, s + 1)
                            wait(act, M.hs_ready, s)
                            out = hs_odd[:]
                        else:
                            wait(act, M.o_odd_added, 3 * (s - 1) + part + 1)
                            out = out_part[:, part, :]
                        act.activation(out, o_bank[1][:, i, :], ACT.Copy, scale=rw_out[:, b, e:e + 1]).then_inc(M.o_odd_read, 1)

                def step(s, b):
                    first, one, two = is_(s, 0), has(s, 1), has(s, 2)
                    if two:
                        squares(s + 2, b)
                        round_n(s + 2, b)
                    if one:
                        weigh_odd(s + 1, 1 - b, 1)
                    keep_qk(s)
                    if not first:
                        weigh_out(s - 1, 1 - b, 1)
                    exps(s)
                    if one:
                        weigh_odd(s + 1, 1 - b, 3)
                    if two:
                        gate_exp(s + 2)
                    keep_p(s)
                    if one:
                        weigh_odd(s + 1, 1 - b, 5)
                    if not first:
                        weigh_out(s - 1, 1 - b, 3)
                    round_a(s)
                    if one:
                        weigh_odd(s + 1, 1 - b, 7)

                for s in range(2):
                    round_n(s, s)
                    squares(s, s)
                    gate_exp(s)
                for e in range(1, E, 2):
                    weigh_odd(0, 0, e)
                parities(act, NS, step, 4)
                weigh_out(NS - 1, 1, 1)
                weigh_out(NS - 1, 1, 3)

            @block.vector
            def _(dve):
                def norm(s, b):
                    wait(dve, M.tn_ready, s - 1)
                    wait(dve, M.squared, s - 1)
                    dve.tensor_scalar(normed[:, b, :], S.x[:, s, :], S.mean[:, bass.ds(s, 1)],
                                      S.rstd2[:, bass.ds(s, 1)], ALU.subtract, ALU.mult).then_inc(M.n_made, 1)

                def rest_n(s, b):
                    dve.wait_ge(M.nhi_ready, s + 1)
                    dve.tensor_tensor(nT[1][:, b], nT_ps, nT[0][:, b].bitcast(F32), ALU.subtract).then_inc(M.nlo_ready, 1)

                def guard(s):
                    dve.wait_ge(M.squared, s + 1)
                    wait(dve, M.rooted, s)
                    dve.tensor_scalar(T.squared[:], T.square_sum[:], 1e-24, None, ALU.max).then_inc(M.guarded, 1)

                def gate_first(s):
                    dve.wait_ge(M.dots_made, s + 1)
                    dve.wait_ge(M.rooted, s + 1)
                    gate_before(S, dve, T, G, dots_ps.unsqueeze(1), M.gate_step, s)

                def gate_last(s, b):
                    wait(dve, M.odd_read, 4 * (s - 1))
                    gate_after(dve, T, rw[:, b], M.gate_exp, M.gate_step, s, M.gate_ready)

                def keep_gate(s, b):
                    dve.wait_ge(M.gate_ready, s + 1)
                    wait(dve, M.o_odd_read, 4 * (s - 1))
                    dve.tensor_copy(rw_out[:, b, :], rw[:, b, 0, :]).then_inc(M.kept, 1)

                def weigh_even(s, b, e):
                    n = 4 * s + e // 2
                    dve.wait_ge(M.q_even_made, n + 1)
                    wait(dve, M.even_added, n)
                    scale = rw[:, b, 0, e:e + 1]
                    if e == 0:
                        dve.wait_ge(M.gate_ready, s + 1)
                        wait(dve, M.attn_made, s - 1)
                        last = dve.tensor_scalar(qkv[:, b, :], q_bank[0], scale, None, ALU.mult)
                    else:
                        last = dve.scalar_tensor_tensor(qkv[:, b, :], q_bank[0], scale, qkv[:, b, :], ALU.mult, ALU.add)
                    last.then_inc(M.even_added, 1)

                def add_qkv(s, b):
                    dve.wait_ge(M.even_added, 4 * (s + 1))
                    dve.wait_ge(M.odd_added, 3 * (s + 1))
                    dve.tensor_tensor(qkv[:, b, :], qkv[:, b, :], qkv_odd[:, b, :], ALU.add).then_inc(M.qkv_ready, 1)

                def row_max(s):
                    dve.wait_ge(M.scored, s + 1)
                    wait(dve, M.exp_done, s)
                    dve.memset(S.carrier[:, 0:1], 0.0)
                    dve.tensor_tensor_reduce(masked[:], scores, S.hidden[:], 1.0, LARGEST, ALU.add, ALU.min, neg_max[:]
                                             ).then_inc(M.max_ready, 1)

                def sum_scale(s):
                    dve.wait_ge(M.exp_done, s + 1)
                    dve.reciprocal(row_scale[:], row_sum[:]).then_inc(M.recip_done, 1)

                def normalize(s):
                    dve.wait_ge(M.attn_made, s + 1)
                    dve.wait_ge(M.recip_done, s + 1)
                    wait(dve, M.aT_made, s)
                    dve.tensor_scalar(attn[:], attn_ps, row_scale[:], None, ALU.mult).then_inc(M.attn_ready, 1)

                def rest_a(s):
                    dve.wait_ge(M.ahi_ready, s + 1)
                    dve.tensor_tensor(aT[1][:], aT_ps, aT[0][:].bitcast(F32), ALU.subtract).then_inc(M.alo_ready, 1)

                def first_ln(s):
                    wait(dve, M.o_even_added, 4 * (s - 1) + 1)
                    dve.tensor_scalar(y[:], S.x[:, s, :], S.mean[:, bass.ds(s, 1)], S.rstd[:, bass.ds(s, 1)],
                                      ALU.subtract, ALU.mult).then_inc(M.y_ready, 1)

                def weigh_out(s, b, n):
                    dve.wait_ge(M.o_even_made, 2 * s + n // 2 + 1)
                    for i in range(2):
                        at = 4 * s + n + i
                        if n == 0 and i == 0:
                            dve.wait_ge(M.y_ready, s + 1)
                            dve.wait_ge(M.kept, s + 1)
                            wait(dve, M.hs_ready, s)
                        wait(dve, M.o_even_added, at)
                        dve.scalar_tensor_tensor(hs_even[:], o_bank[0][:, i, :], rw_out[:, b, 2 * n + i:2 * n + i + 1],
                                                 (hs_even if n or i else y)[:], ALU.mult, ALU.add).then_inc(M.o_even_added, 1)

                def finish(s, b):
                    dve.wait_ge(M.o_even_added, 4 * (s + 1))
                    dve.wait_ge(M.o_odd_added, 3 * (s + 1))
                    wait(dve, M.x_added, s - 1)
                    wait(dve, hs_stored[b], 8 * (s - b))
                    dve.tensor_tensor(hs[:, b, :], hs_even[:], hs_odd[:], ALU.add).then_inc(M.hs_ready, 1)
                    dve.wait_ge(M.hs_ready, s + 1)
                    dve.bn_stats(seq_stats[:], hs[:, b, :]).then_inc(M.stats_done, 1)
                    dve.wait_ge(M.stats_done, s + 1)
                    dve.tensor_copy(S.stats[:, s, :], seq_stats[:])

                def step(s, b):
                    first, one, two, three = is_(s, 0), has(s, 1), has(s, 2), has(s, 3)
                    keep_gate(s, b)
                    if three:
                        norm(s + 3, 1 - b)
                    if one:
                        weigh_even(s + 1, 1 - b, 0)
                    add_qkv(s, b)
                    if not (first or is_(s, 1)):
                        finish(s - 2, b)
                    if two:
                        rest_n(s + 2, b)
                    if not first:
                        weigh_out(s - 1, 1 - b, 0)
                    if two:
                        guard(s + 2)
                    if one:
                        weigh_even(s + 1, 1 - b, 2)
                    row_max(s)
                    if two:
                        gate_first(s + 2)
                    if not first:
                        weigh_out(s - 1, 1 - b, 2)
                    first_ln(s)
                    sum_scale(s)
                    if one:
                        weigh_even(s + 1, 1 - b, 4)
                    normalize(s)
                    if two:
                        gate_last(s + 2, b)
                    if one:
                        weigh_even(s + 1, 1 - b, 6)
                    rest_a(s)

                norm(0, 0)
                norm(1, 1)
                for s in range(2):
                    rest_n(s, s)
                    guard(s)
                    gate_first(s)
                    gate_last(s, s)
                norm(2, 0)
                for e in range(0, E, 2):
                    weigh_even(0, 0, e)
                parities(dve, NS, step, 4)
                finish(NS - 2, 0)
                weigh_out(NS - 1, 1, 0)
                weigh_out(NS - 1, 1, 2)
                finish(NS - 1, 1)

            @block.gpsimd
            def _(pool):
                def root(s):
                    pool.wait_ge(M.guarded, s + 1)
                    wait(pool, M.gate_step, GATE_STEPS * (s - 1) + 2)
                    pool.tensor_tensor(T.rnorm[:], T.squared[:], S.minus_half[:, 0:T.n], ALU.pow).then_inc(M.rooted, 1)

                def affine(s, b):
                    pool.wait_ge(M.n_made, s + 1)
                    pool.tensor_tensor(normed[:, b, :], normed[:, b, :], ln_w[:], ALU.mult).then_inc(M.scaled, 1)
                    pool.wait_ge(M.scaled, s + 1)
                    pool.tensor_tensor(normed[:, b, :], normed[:, b, :], ln_b[:], ALU.add).then_inc(M.n_ready, 1)

                def add_odd(s, b, e):
                    n = e // 2 - 1
                    pool.wait_ge(M.odd_read, 4 * s + e // 2 + 1)
                    wait(pool, M.odd_added, 3 * s + n)
                    pool.tensor_tensor(qkv_odd[:, b, :], qkv_odd[:, b, :], qkv_part[:, n, :], ALU.add).then_inc(M.odd_added, 1)

                def add_out(s, part):
                    pool.wait_ge(M.o_odd_read, 4 * s + part + 2)
                    wait(pool, M.o_odd_added, 3 * s + part)
                    pool.tensor_tensor(hs_odd[:], hs_odd[:], out_part[:, part, :], ALU.add).then_inc(M.o_odd_added, 1)

                def add_hs(s, b):
                    pool.wait_ge(M.hs_ready, s + 1)
                    pool.tensor_tensor(S.x[:, s, :], S.x[:, s, :], hs[:, b, :], ALU.add).then_inc(M.x_added, 1)

                def step(s, b):
                    first, one, two, three = is_(s, 0), has(s, 1), has(s, 2), has(s, 3)
                    if three:
                        affine(s + 3, 1 - b)
                    if not (first or is_(s, 1)):
                        add_hs(s - 2, b)
                    if two:
                        root(s + 2)
                    if one:
                        add_odd(s + 1, 1 - b, 3)
                    if not first:
                        add_out(s - 1, 0)
                    if one:
                        add_odd(s + 1, 1 - b, 5)
                    if not first:
                        add_out(s - 1, 1)
                        add_out(s - 1, 2)
                    if one:
                        add_odd(s + 1, 1 - b, 7)

                for s in range(2):
                    affine(s, s)
                    root(s)
                affine(2, 0)
                for e in range(3, E, 2):
                    add_odd(0, 0, e)
                parities(pool, NS, step, 4)
                add_hs(NS - 2, 0)
                for part in range(3):
                    add_out(NS - 1, part)
                add_hs(NS - 1, 1)
        clear(nc, own_sems)


def mixture_mlp(nc, S, L, W, G, ln_w, ln_b, hs_dram, load_next):
    NS = S.n_seq
    NP = NS // 2
    with ExitStack() as mem:
        def sb(name, shape, dt=F32):
            return mem.enter_context(nc.sbuf_tensor(f"{L}_{name}", shape, dt))

        own_sems = []

        def sem(name):
            own_sems.append(mem.enter_context(nc.semaphore(f"{L}_{name}")))
            return own_sems[-1]

        normed = sb("normed", [P, 2, C])
        square = S.bank[7].rearrange("p (s c) -> p s c", s=2)
        nT = [sb("nT_hi", [P, 2, KT, 2 * P], F32R), sb("nT_lo", [P, 2, KT, 2 * P], F32R)]
        T = gate_tiles(sb, 2)
        rw = sb("rw", [P, 2, 2, E])
        inter = sb("inter", [P, 2, 512])
        iT = [sb("inter_hi", [P, 2, KT, 2 * P], F32R), sb("inter_lo", [P, 2, KT, 2 * P], F32R)]
        hs = sb("hs", [P, 2, 2, C])
        total = sb("total", [P, 2, 2, C])
        seq_stats = sb("seq_stats", [P, 2, 6])

        nT_ps = S.bank[0].rearrange("p (k t) -> p k t", k=KT)
        dots_ps = S.bank[1][:, 0:4 * E].rearrange("p (s e) -> p s e", s=2)
        up_bank = [S.bank[2], S.bank[3], S.bank[6]]
        down_bank = [S.bank[4], S.bank[5]]

        names = ("n_made scaled n_ready squared guarded rooted tn_ready nhi_ready nlo_ready dots_made gate_step gate_exp "
                 "gate_ready up_made inter_ready ihi_ready ilo_ready down_made added stats_done").split()
        M = named(**{n: sem(n) for n in names})
        hs_loaded = [sem("hs_even_loaded"), sem("hs_odd_loaded")]
        has = lambda p, ahead: not any(is_(p, NP - 1 - d) for d in range(ahead))

        with nc.Block() as block:
            @block.sync
            def _(sp):
                def step(p, b):
                    wait(sp, M.n_made, p - 1)
                    sp.dma_start(hs[:, b], hs_dram[bass.ds(2 * p, 2)].rearrange("s t c -> t s c")
                                 ).then_inc(hs_loaded[b], 16)
                for p in range(2):
                    step(p, p)
                next_loaded = load_next(sp)
                parities(sp, NP, step, begin=2)
                wait(sp, *next_loaded)

            @block.tensor
            def _(pe):
                def turn_n(p):
                    pe.wait_ge(M.n_ready, p + 1)
                    wait(pe, M.nlo_ready, p)
                    for k in range(KT):
                        for s in range(2):
                            last = pe.transpose(nT_ps[:, k, s * P:(s + 1) * P], normed[:, s, k * P:(k + 1) * P], S.ident[:])
                    last.then_inc(M.tn_ready, 1)

                def dot_gate(p, b):
                    pe.wait_ge(M.nlo_ready, p + 1)
                    wait(pe, M.gate_step, GATE_STEPS * (p - 1) + 2)
                    for s in range(2):
                        last = gate_products(pe, dots_ps[:, s, :], [[t[:, b, k, s * P:(s + 1) * P] for k in range(KT)]
                                                                    for t in nT], G.split)
                    last.then_inc(M.dots_made, 1)

                def up(p, b, e):
                    wait(pe, M.ihi_ready, E * p + e - 1)
                    if e == 0:
                        pe.wait_ge(M.nlo_ready, p + 1)
                    out = up_bank[e % 2].rearrange("p (m t) -> p m t", m=KT)
                    for m in range(KT):
                        for k in range(KT):
                            last = mm3(pe, out[:, m, :], [w[:, 0, e, k, m * P:(m + 1) * P] for w in (W.hi, W.lo)],
                                       [t[:, b, k, :] for t in nT], k == 0, k == KT - 1)
                    last.then_inc(M.up_made, 1)

                def down(p, e):
                    pe.wait_ge(M.ilo_ready, E * p + e + 1)
                    wait(pe, M.added, 2 * (E * p + e - 1))
                    out = down_bank[e % 2].rearrange("p (s c) -> p s c", s=2)
                    for s in range(2):
                        for k in range(KT):
                            last = mm3(pe, out[:, s, :], [t[:, e % 2, k, s * P:(s + 1) * P] for t in iT],
                                       [w[:, 1, e, k, :] for w in (W.hi, W.lo)], k == 0, k == KT - 1)
                    last.then_inc(M.down_made, 1)

                def step(p, b):
                    for e in range(E):
                        up(p, b, e)
                        if e >= 1:
                            down(p, e - 1)
                        elif not is_(p, 0):
                            down(p - 1, E - 1)
                        if e == 1 and has(p, 1):
                            turn_n(p + 1)
                        if e == 4 and has(p, 1):
                            dot_gate(p + 1, 1 - b)

                turn_n(0)
                dot_gate(0, 0)
                parities(pe, NP, step)
                down(NP - 1, E - 1)

            @block.scalar
            def _(act):
                def round_n(p, b):
                    act.wait_ge(M.tn_ready, p + 1)
                    wait(act, M.up_made, E * (p - 1))
                    act.activation(nT[0][:, b], nT_ps, ACT.Copy).then_inc(M.nhi_ready, 1)

                def squares(p):
                    act.wait_ge(M.n_ready, p + 1)
                    wait(act, M.guarded, p)
                    for s in range(2):
                        last = act.activation(square[:, s], normed[:, s, :], ACT.Square, accum_out=T.square_sum[:, s:s + 1])
                    last.then_inc(M.squared, 1)

                def gelu(p, e):
                    n = E * p + e
                    act.wait_ge(M.up_made, n + 1)
                    wait(act, M.ilo_ready, n - 1)
                    wait(act, M.down_made, n - 1)
                    act.activation(inter[:, e % 2], up_bank[e % 2], ACT.Gelu).then_inc(M.inter_ready, 1)
                    act.activation(iT[0][:, e % 2].rearrange("p k t -> p (k t)"), up_bank[e % 2], ACT.Gelu).then_inc(M.ihi_ready, 1)

                def step(p, b):
                    for e in range(E):
                        gelu(p, e)
                        if has(p, 1):
                            if e == 1:
                                round_n(p + 1, 1 - b)
                            if e == 2:
                                squares(p + 1)

                round_n(0, 0)
                squares(0)
                parities(act, NP, step)

            @block.vector
            def _(dve):
                def norm(p, b):
                    dve.wait_ge(hs_loaded[b], 8 * (p - b) + 16)
                    wait(dve, M.tn_ready, p)
                    wait(dve, M.squared, p)
                    for s in range(2):
                        n = 2 * p + s
                        last = dve.tensor_scalar(normed[:, s, :], hs[:, b, s, :], S.mean[:, bass.ds(n, 1)],
                                                 S.rstd[:, bass.ds(n, 1)], ALU.subtract, ALU.mult)
                    last.then_inc(M.n_made, 1)

                def rest_n(p, b):
                    dve.wait_ge(M.nhi_ready, p + 1)
                    dve.tensor_tensor(nT[1][:, b], nT_ps, nT[0][:, b].bitcast(F32), ALU.subtract).then_inc(M.nlo_ready, 1)

                def guard(p):
                    dve.wait_ge(M.squared, p + 1)
                    wait(dve, M.rooted, p)
                    dve.tensor_scalar(T.squared[:], T.square_sum[:], 1e-24, None, ALU.max).then_inc(M.guarded, 1)

                def gate_first(p):
                    dve.wait_ge(M.dots_made, p + 1)
                    dve.wait_ge(M.rooted, p + 1)
                    gate_before(S, dve, T, G, dots_ps, M.gate_step, p)

                def gate_last(p, b):
                    gate_after(dve, T, rw[:, b], M.gate_exp, M.gate_step, p, M.gate_ready)

                def rest_i(p, e):
                    n = E * p + e
                    dve.wait_ge(M.ihi_ready, n + 1)
                    dve.tensor_tensor(iT[1][:, e % 2].rearrange("p k t -> p (k t)"), inter[:, e % 2],
                                      iT[0][:, e % 2].rearrange("p k t -> p (k t)").bitcast(F32), ALU.subtract
                                      ).then_inc(M.ilo_ready, 1)

                def add(p, b, e):
                    n = E * p + e
                    dve.wait_ge(M.down_made, n + 1)
                    if e == 0:
                        dve.wait_ge(M.gate_ready, p + 1)
                    wait(dve, M.added, 2 * n)
                    out = down_bank[e % 2].rearrange("p (s c) -> p s c", s=2)
                    for s in range(2):
                        dve.scalar_tensor_tensor(total[:, b, s, :], out[:, s, :], rw[:, b, s, e:e + 1],
                                                 total[:, b, s, :] if e else S.x[:, 2 * p + s, :],
                                                 ALU.mult, ALU.add).then_inc(M.added, 1)

                def finish(p, b):
                    dve.wait_ge(M.added, 2 * E * (p + 1))
                    for s in range(2):
                        dve.bn_stats(seq_stats[:, s, :], total[:, b, s, :]).then_inc(M.stats_done, 1)
                    dve.tensor_copy(S.x[:, bass.ds(2 * p, 2), :], total[:, b])
                    dve.wait_ge(M.stats_done, 2 * p + 2)
                    dve.tensor_copy(S.stats[:, bass.ds(2 * p, 2), :], seq_stats[:])

                def step(p, b):
                    for e in range(E):
                        rest_i(p, e)
                        if e >= 1:
                            add(p, b, e - 1)
                        elif not is_(p, 0):
                            add(p - 1, 1 - b, E - 1)
                        if e == 1:
                            if not is_(p, 0):
                                finish(p - 1, 1 - b)
                            if has(p, 1):
                                rest_n(p + 1, 1 - b)
                        if e == 3 and has(p, 1):
                            guard(p + 1)
                        if e == 3 and has(p, 2):
                            norm(p + 2, b)
                        if e == 4 and has(p, 1):
                            gate_first(p + 1)
                        if e == 7:
                            if has(p, 1):
                                gate_last(p + 1, 1 - b)

                norm(0, 0)
                rest_n(0, 0)
                guard(0)
                gate_first(0)
                gate_last(0, 0)
                norm(1, 1)
                parities(dve, NP, step)
                add(NP - 1, 1, E - 1)
                finish(NP - 1, 1)

            @block.gpsimd
            def _(pool):
                def root(p):
                    pool.wait_ge(M.guarded, p + 1)
                    wait(pool, M.gate_step, GATE_STEPS * (p - 1) + 2)
                    pool.tensor_tensor(T.rnorm[:], T.squared[:], S.minus_half[:, 0:T.n], ALU.pow).then_inc(M.rooted, 1)

                def gate_exp(p):
                    pool.wait_ge(M.gate_step, GATE_STEPS * p + GATE_BEFORE)
                    pool.tensor_tensor(T.exp[:], S.euler[:], T.shifted[:], ALU.pow).then_inc(M.gate_exp, 1)

                def affine(p):
                    pool.wait_ge(M.n_made, p + 1)
                    wide = lambda t: t[:].unsqueeze(1).broadcast_to([P, 2, C])
                    pool.tensor_tensor(normed[:], normed[:], wide(ln_w), ALU.mult).then_inc(M.scaled, 1)
                    pool.wait_ge(M.scaled, p + 1)
                    pool.tensor_tensor(normed[:], normed[:], wide(ln_b), ALU.add).then_inc(M.n_ready, 1)

                def step(p, b):
                    if has(p, 1):
                        root(p + 1)
                        gate_exp(p + 1)
                    if has(p, 2):
                        affine(p + 2)

                affine(0)
                root(0)
                gate_exp(0)
                affine(1)
                parities(pool, NP, step)
        clear(nc, own_sems)


def routed_experts(nc, S, L, W, R, out_dram):
    NP = S.n_seq // 2
    SLOTS = E
    with ExitStack() as mem:
        def sb(name, shape, dt=F32):
            return mem.enter_context(nc.sbuf_tensor(f"{L}_{name}", shape, dt))

        own_sems = []

        def sem(name):
            own_sems.append(mem.enter_context(nc.semaphore(f"{L}_{name}")))
            return own_sems[-1]

        normed = sb("normed", [P, 2, C])
        nT = [sb("nT_hi", [P, 2, KT, 2 * P], F32R), sb("nT_lo", [P, 2, KT, 2 * P], F32R)]
        partial, logit, tied, first, exp = (sb(n, [P, 2, E]) for n in ("partial", "logit", "tied", "first", "exp"))
        top, order, weight = (sb(n, [P, 2]) for n in ("top", "order", "weight"))
        gate = sb("gate", [P, 2, 2, P])
        gateT = sb("gateT", [P, 2, 2, P])
        even, odd, base, both = (sb(n, [P, 2, C]) for n in ("even", "odd", "base", "both"))
        part = sb("part", [P, 2, 3, C])
        result = sb("result", [P, 2, 2, C])

        nT_ps = S.bank[0].rearrange("p (k t) -> p k t", k=KT)
        dots_ps = S.bank[1][:, 0:4 * E].rearrange("p (s e) -> p s e", s=2)
        gateT_ps = S.bank[2][:, 0:2 * P].rearrange("p (s t) -> p s t", s=2)
        bias_ps = S.bank[3].rearrange("p (s c) -> p s c", s=2)
        y_bank = [S.bank[4 + n].rearrange("p (e c) -> p e c", e=2) for n in range(4)]

        names = ("n_ready tn_ready nhi_ready nlo_ready dots_made dots_read step exp_done gate_cleared gate_ready gT_made gT_ready "
                 "bias_made base_ready even_made odd_made even_added odd_read odd_added both_done result_ready").split()
        M = named(**{n: sem(n) for n in names})
        stored = [sem("even_stored"), sem("odd_stored")]
        has = lambda p, ahead: not any(is_(p, NP - 1 - d) for d in range(ahead))
        STEPS = 9

        with nc.Block() as block:
            @block.sync
            def _(sp):
                def step(p, b):
                    sp.wait_ge(M.result_ready, 2 * p + 2)
                    sp.dma_start(out_dram[bass.ds(2 * p, 2)].rearrange("s t c -> t s c"), result[:, b]
                                 ).then_inc(stored[b], 16)
                parities(sp, NP, step)
                for b in range(2):
                    sp.wait_ge(stored[b], 8 * NP)

            @block.tensor
            def _(pe):
                def turn_n(p):
                    pe.wait_ge(M.n_ready, p + 1)
                    wait(pe, M.nlo_ready, p)
                    for k in range(KT):
                        for s in range(2):
                            last = pe.transpose(nT_ps[:, k, s * P:(s + 1) * P], normed[:, s, k * P:(k + 1) * P], S.ident[:])
                    last.then_inc(M.tn_ready, 1)

                def dot_router(p, b):
                    pe.wait_ge(M.nlo_ready, p + 1)
                    wait(pe, M.dots_read, 2 * p)
                    for s in range(2):
                        last = gate_products(pe, dots_ps[:, s, :], [[t[:, b, k, s * P:(s + 1) * P] for k in range(KT)]
                                                                    for t in nT], R.split)
                    last.then_inc(M.dots_made, 1)

                def turn_gate(p, b):
                    pe.wait_ge(M.gate_ready, p + 1)
                    wait(pe, M.gT_ready, p)
                    for s in range(2):
                        last = pe.transpose(gateT_ps[:, s, :], gate[:, b, s, :], S.ident[:])
                    last.then_inc(M.gT_made, 1)

                def bias(p, b):
                    pe.wait_ge(M.gT_ready, p + 1)
                    wait(pe, M.base_ready, p)
                    for s in range(2):
                        last = pe.matmul(bias_ps[:, s, :], gateT[:, b, s, :], R.expert_b[:], start=True, stop=True)
                    last.then_inc(M.bias_made, 1)

                def expert(p, b, t):
                    s, n = divmod(t, 4)
                    if n % 2 == 0:
                        wait(pe, M.even_added, 8 * p + 4 * s - 4 + n + 2)
                    else:
                        wait(pe, M.odd_read, 8 * p + 4 * s - 4 + n + 1)
                    for k in range(KT):
                        last = mm3(pe, S.bank[4 + n], [t_[:, b, k, s * P:(s + 1) * P] for t_ in nT],
                                   [w[:, k, 2 * n:2 * n + 2, :].rearrange("p e c -> p (e c)") for w in (W.hi, W.lo)],
                                   k == 0, k == KT - 1)
                    last.then_inc((M.even_made, M.odd_made)[n % 2], 1)

                def step(p, b):
                    for t in range(SLOTS):
                        expert(p, b, t)
                        if t == 1:
                            turn_gate(p, b)
                        if t == 3:
                            bias(p, b)
                        if has(p, 1):
                            if t == 0:
                                turn_n(p + 1)
                            if t == 2:
                                dot_router(p + 1, 1 - b)

                turn_n(0)
                dot_router(0, 0)
                parities(pe, NP, step)

            @block.scalar
            def _(act):
                def round_n(p, b):
                    act.wait_ge(M.tn_ready, p + 1)
                    wait(act, M.odd_made, 4 * (p - 1))
                    act.activation(nT[0][:, b], nT_ps, ACT.Copy).then_inc(M.nhi_ready, 1)

                def gate_exp(p):
                    act.wait_ge(M.step, STEPS * p + 4)
                    act.activation(exp[:], logit[:], ACT.Exp).then_inc(M.exp_done, 1)

                def keep_gate(p, b):
                    act.wait_ge(M.gT_made, p + 1)
                    wait(act, M.bias_made, p - 1)
                    act.activation(gateT[:, b], gateT_ps, ACT.Copy).then_inc(M.gT_ready, 1)

                def weigh(p, b, t):
                    s, n = divmod(t, 4)
                    q = 2 * p + s
                    act.wait_ge(M.odd_made, 2 * q + n // 2 + 1)
                    for i in range(2):
                        k = 2 * (n // 2) + i - 1
                        if k < 0:
                            act.wait_ge(M.gate_ready, p + 1)
                            wait(act, M.both_done, q - 1)
                            out = odd[:, s, :]
                        else:
                            wait(act, M.odd_added, 3 * (q - 2) + k + 1)
                            out = part[:, s, k, :]
                        act.activation(out, y_bank[n][:, i, :], ACT.Copy, scale=gate[:, b, s, 2 * n + i:2 * n + i + 1]
                                       ).then_inc(M.odd_read, 1)

                def step(p, b):
                    for t in range(SLOTS):
                        if t % 2:
                            weigh(p, b, t)
                        if t == 1:
                            keep_gate(p, b)
                        if has(p, 1):
                            if t == 0:
                                round_n(p + 1, 1 - b)
                            if t == 5:
                                gate_exp(p + 1)

                round_n(0, 0)
                gate_exp(0)
                parities(act, NP, step)

            @block.vector
            def _(dve):
                def norm(p):
                    wait(dve, M.tn_ready, p)
                    for s in range(2):
                        n = 2 * p + s
                        last = dve.tensor_scalar(normed[:, s, :], S.x[:, n, :], S.mean[:, bass.ds(n, 1)],
                                                 S.rstd[:, bass.ds(n, 1)], ALU.subtract, ALU.mult)
                    last.then_inc(M.n_ready, 1)

                def rest_n(p, b):
                    dve.wait_ge(M.nhi_ready, p + 1)
                    dve.tensor_tensor(nT[1][:, b], nT_ps, nT[0][:, b].bitcast(F32), ALU.subtract).then_inc(M.nlo_ready, 1)

                wide = lambda t: t[:].unsqueeze(2).broadcast_to([P, 2, E])

                def chain(p, at):
                    n = [at]

                    def then(ins):
                        n[0] += 1
                        ins.then_inc(M.step, 1)
                        dve.wait_ge(M.step, STEPS * p + n[0])
                    return then

                def gate_first(p):
                    then = chain(p, 0)
                    tt = dve.tensor_tensor
                    dve.wait_ge(M.dots_made, p + 1)
                    tt(partial[:], dots_ps[:, :, E:2 * E], R.bias[:].unsqueeze(1).broadcast_to([P, 2, E]), ALU.add
                       ).then_inc(M.dots_read, 1)
                    dve.wait_ge(M.dots_read, 2 * p + 1)
                    tt(logit[:], dots_ps[:, :, 0:E], partial[:], ALU.add).then_inc(M.dots_read, 1)
                    dve.wait_ge(M.dots_read, 2 * p + 2)
                    then(dve.tensor_reduce(top[:], logit[:], AX.X, ALU.max))
                    then(tt(tied[:], logit[:], wide(top), ALU.is_ge))
                    then(tt(tied[:], tied[:], S.rank[:], ALU.mult))
                    then(tt(logit[:], logit[:], wide(top), ALU.subtract))
                    then(dve.tensor_reduce(order[:], tied[:], AX.X, ALU.max))
                    then(tt(first[:], S.rank[:], wide(order), ALU.is_equal))

                def gate_last(p, b):
                    then = chain(p, 6)
                    dve.wait_ge(M.exp_done, p + 1)
                    then(dve.tensor_reduce(weight[:], exp[:], AX.X, ALU.add))
                    then(dve.reciprocal(weight[:], weight[:]))
                    wait(dve, M.gT_made, p - 1)
                    wait(dve, M.odd_read, 8 * (p - 1))
                    then(dve.tensor_tensor(first[:], first[:], wide(weight), ALU.mult))
                    dve.tensor_copy(gate[:, b, :, 0:E], first[:]).then_inc(M.gate_ready, 1)

                def add_bias(p):
                    dve.wait_ge(M.bias_made, p + 1)
                    dve.tensor_tensor(base[:], bias_ps, S.x[:, bass.ds(2 * p, 2), :], ALU.add).then_inc(M.base_ready, 1)

                def weigh(p, b, t):
                    s, n = divmod(t, 4)
                    q = 2 * p + s
                    dve.wait_ge(M.even_made, 2 * q + n // 2 + 1)
                    for i in range(2):
                        y, scale = y_bank[n][:, i, :], gate[:, b, s, 2 * n + i:2 * n + i + 1]
                        if n + i == 0:
                            dve.wait_ge(M.gate_ready, p + 1)
                            wait(dve, M.both_done, q - 1)
                            last = dve.tensor_scalar(even[:, s, :], y, scale, None, ALU.mult)
                        else:
                            dve.wait_ge(M.even_added, 4 * q + n + i)
                            last = dve.scalar_tensor_tensor(even[:, s, :], y, scale, even[:, s, :], ALU.mult, ALU.add)
                        last.then_inc(M.even_added, 1)

                def finish(p, b, s):
                    q = 2 * p + s
                    dve.wait_ge(M.even_added, 4 * q + 4)
                    dve.wait_ge(M.odd_added, 3 * q + 3)
                    dve.tensor_tensor(both[:, s, :], even[:, s, :], odd[:, s, :], ALU.add).then_inc(M.both_done, 1)
                    dve.wait_ge(M.both_done, q + 1)
                    dve.wait_ge(M.base_ready, p + 1)
                    wait(dve, stored[b], 8 * (p - b))
                    dve.tensor_tensor(result[:, b, s, :], both[:, s, :], base[:, s, :], ALU.add).then_inc(M.result_ready, 1)

                def step(p, b):
                    for t in range(SLOTS):
                        if t % 2 == 0:
                            weigh(p, b, t)
                        if t == 1:
                            if not is_(p, 0):
                                finish(p - 1, 1 - b, 1)
                            if has(p, 1):
                                rest_n(p + 1, 1 - b)
                        if t == 3 and has(p, 1):
                            gate_first(p + 1)
                        if t == 4:
                            add_bias(p)
                        if t == 5:
                            finish(p, b, 0)
                            if has(p, 2):
                                norm(p + 2)
                        if t == 6 and has(p, 1):
                            gate_last(p + 1, 1 - b)

                dve.memset(gate[:], 0.0).then_inc(M.gate_cleared, 1)
                norm(0)
                rest_n(0, 0)
                gate_first(0)
                dve.wait_ge(M.gate_cleared, 1)
                gate_last(0, 0)
                norm(1)
                parities(dve, NP, step)
                finish(NP - 1, 1, 1)

            @block.gpsimd
            def _(pool):
                def step(p, b):
                    for s in range(2):
                        q = 2 * p + s
                        for k in range(3):
                            pool.wait_ge(M.odd_read, 4 * q + k + 2)
                            wait(pool, M.odd_added, 3 * q + k)
                            pool.tensor_tensor(odd[:, s, :], odd[:, s, :], part[:, s, k, :], ALU.add).then_inc(M.odd_added, 1)
                parities(pool, NP, step)
        clear(nc, own_sems)


def setup(nc, S, a):
    loaded = S.sem("setup_loaded")
    S.x_loaded = [S.sem(f"x{n}_loaded") for n in range(S.n_seq // CHUNK)]
    with nc.Block() as block:
        @block.sync
        def _(sp):
            sp.dma_start(S.raw[:, 0:4 * KT * C], a["weights0"]).then_inc(loaded, 16)
            sp.dma_start(S.columns[:], a["columns"]).then_inc(loaded, 16)
            sp.dma_start(S.rows[:], a["rows"].partition_broadcast(P)).then_inc(loaded, 16)
            sp.dma_start(S.constants[:], a["constants"]).then_inc(loaded, 16)
            sp.dma_start(S.expert_b[:], a["expert_b"]).then_inc(loaded, 16)
            for n, chunk_loaded in enumerate(S.x_loaded):
                at = slice(n * CHUNK, (n + 1) * CHUNK)
                sp.dma_start(S.x[:, at, :], a["x"][at].rearrange("s t c -> t s c")).then_inc(chunk_loaded, 16)
            sp.wait_ge(loaded, 5 * 16)


def first_stats(nc, S):
    stats_done = S.sem("first_stats_done")
    with nc.Block() as block:
        @block.vector
        def _(dve):
            for n, loaded in enumerate(S.x_loaded):
                dve.wait_ge(loaded, 16)
                for s in range(n * CHUNK, (n + 1) * CHUNK):
                    last = dve.bn_stats(S.stats[:, s, :], S.x[:, s, :])
                last.then_inc(stats_done, 1)
            dve.wait_ge(stats_done, len(S.x_loaded))


def program(nc, a, out, phases=5):
    with ExitStack() as mem:
        def sb(name, shape, dt=F32):
            return mem.enter_context(nc.sbuf_tensor(name, shape, dt))

        S = Named()
        S.n_seq = a["x"].shape[0]
        S.sem = lambda name: mem.enter_context(nc.semaphore(name))
        S.bank = [mem.enter_context(nc.psum_tensor(f"bank{n}", [P, 512], F32))[:] for n in range(8)]
        S.x = sb("x_all", [P, S.n_seq, C])
        S.stats = sb("stats", [P, S.n_seq, 6])
        S.mean, S.var, S.root = (sb(n, [P, S.n_seq]) for n in ("mean", "var", "root"))
        S.rstd, S.rstd2 = sb("rstd", [P, S.n_seq]), sb("rstd2", [P, S.n_seq])
        S.raw = sb("raw_weights", [P, 2 * E * KT * C])
        S.carrier = sb("carrier", [P, 2])
        S.expert_b = sb("expert_bias", [P, C])

        def parts(tile, widths):
            ends = np.cumsum(widths)
            return [tile[:, int(e) - w:int(e)] for e, w in zip(ends, widths)]

        shapes = {n: c.shape[1:] for n, c in constants().items()}
        widths = [int(np.prod(s)) for s in shapes.values()]
        S.constants = sb("constants", [P, sum(widths)])
        c = dict(zip(shapes, parts(S.constants, widths)))
        S.ident, S.hidden, S.head_rows, S.minus_half = c["ident"], c["hidden"], c["head_rows"], c["minus_half"]
        S.count = c["count"].rearrange("p (j q) -> p j q", j=UNITS)
        S.ones_half = c["ones_half"].rearrange("p (e m) -> p e m", e=2)
        S.rank, S.euler = (c[n].rearrange("p (s e) -> p s e", e=E) for n in ("rank", "euler"))

        S.rows = sb("rows", [P, sum(w for _, w in ROWS)])
        row = dict(zip([n for n, _ in ROWS], parts(S.rows, [w for _, w in ROWS])))
        S.columns = sb("columns", [P, KT * sum(w for _, w in COLUMNS)])
        column = dict(zip([n for n, _ in COLUMNS], parts(S.columns, [KT * w for _, w in COLUMNS])))
        by_expert = lambda name: column[name].rearrange("p (k e) -> p k e", k=KT)

        def gate(name):
            return named(sim=by_expert(f"{name}_sim"), work=sb(f"{name}_work", [P, KT, E]), norm=sb(f"{name}_norm", [P, E]),
                         split=sb(f"{name}_split", [P, KT, 2 * E], F32R)[:], gates=row[f"{name}_gates"])

        B = {L: named(q=column[f"{L}_bq"], k=column[f"{L}_bk"], v=row[f"{L}_bv"], o=row[f"{L}_bo"])
             for L in ("L0_xattn", "L1_xattn")}
        ln1, ln2 = ((row[f"L0_ffn_{n}_w"], row[f"L0_ffn_{n}_b"]) for n in ("ln1", "ln2"))
        attention_gate, mlp_gate = gate("L0_ffn_smha"), gate("L0_ffn_moe")
        R = named(raw=by_expert("L1_ffn_router_w"), split=sb("router_split", [P, KT, 2 * E], F32R)[:],
                  bias=row["L1_ffn_router_b"], expert_b=S.expert_b)
        hs_dram = nc.dram_tensor("hs", a["x"].shape, F32).ap()

        def weights(own, name, shape):
            return [own.enter_context(nc.sbuf_tensor(f"{name}_{part}", shape, F32R)) for part in ("hi", "lo")]

        weights_loaded = [S.sem(f"weights{n}_loaded") for n in range(5)]

        def load(n):
            def start(dma):
                source = a[f"weights{n}"]
                dma.dma_start(S.raw[:, 0:source.shape[1]], source).then_inc(weights_loaded[n], 16)
                return weights_loaded[n], 16
            return start

        setup(nc, S, a)

        with ExitStack() as own:
            W = Named()
            W.hi, W.lo = weights(own, "W0", [P, 4, KT, C])
            prepare(nc, S, "W0", attention_pieces(S, W) + [(R.split[:, :, 0:E], R.split[:, :, E:2 * E], R.raw)])
            gate_weights(nc, S, "gate1", attention_gate)
            gate_weights(nc, S, "gate2", mlp_gate)
            first_stats(nc, S)
            prepare(nc, S, "ln0", norms=1)
            attention(nc, S, "L0", a["ctx"], W, B["L0_xattn"], S.count, load(1))

        if phases >= 2:
            with ExitStack() as own:
                W = Named()
                W.hi, W.lo = weights(own, "W1", [P, E, KT, 3 * HID])
                W.o_hi, W.o_lo = weights(own, "W1_o", [P, E, C])
                raw = S.raw[:, 0:E * KT * 3 * HID].rearrange("p (e k w) -> p e k w", e=E, k=KT)
                raw_o = S.raw[:, E * KT * 3 * HID:].rearrange("p (e c) -> p e c", e=E)
                prepare(nc, S, "W1", [(W.hi[:, e], W.lo[:, e], raw[:, e]) for e in range(E)]
                        + [(W.o_hi[:, e:e + 4], W.o_lo[:, e:e + 4], raw_o[:, e:e + 4]) for e in (0, 4)], norms=2)
                mixture_attention(nc, S, "M1", W, attention_gate, *ln1, hs_dram, load(2))

        if phases >= 3:
            with ExitStack() as own:
                W = Named()
                W.hi, W.lo = weights(own, "W2", [P, 2, E, KT, C])
                raw = S.raw[:].rearrange("p (w e k c) -> p w e k c", w=2, e=E, k=KT)
                prepare(nc, S, "W2", [(W.hi[:, w, e:e + 2], W.lo[:, w, e:e + 2], raw[:, w, e:e + 2])
                                      for w in range(2) for e in range(0, E, 2)], norms=1)
                mixture_mlp(nc, S, "M2", W, mlp_gate, *ln2, hs_dram, load(3))

        if phases >= 4:
            with ExitStack() as own:
                W = Named()
                W.hi, W.lo = weights(own, "W3", [P, 4, KT, C])
                prepare(nc, S, "W3", attention_pieces(S, W), norms=1)
                attention(nc, S, "L1", a["ctx"], W, B["L1_xattn"], None, load(4))

        if phases >= 5:
            with ExitStack() as own:
                W = Named()
                W.hi, W.lo = weights(own, "W4", [P, KT, E, C])
                raw = S.raw[:, 0:E * KT * C].rearrange("p (e k c) -> p e k c", e=E, k=KT)
                prepare(nc, S, "W4", [(W.hi[:, :, e, :], W.lo[:, :, e, :], raw[:, e]) for e in range(E)], norms=1)
                routed_experts(nc, S, "M4", W, R, out)
        else:
            store(nc, S, out)


def store(nc, S, out):
    stored = S.sem("out_stored")
    with nc.Block() as block:
        @block.sync
        def _(sp):
            sp.dma_start(out.rearrange("s t c -> t s c"), S.x[:]).then_inc(stored, 16)
            sp.wait_ge(stored, 16)


def kernel(**inputs):
    import concourse.bacc as bacc
    from concourse.bass_utils import run_bass_kernel_spmd
    nc = bacc.Bacc("TRN2", target_bir_lowering=False, num_devices=1)
    arrays, a = {}, {}
    for name, value in layouts({n: np.asarray(v) for n, v in inputs.items()}).items():
        value = np.ascontiguousarray(value)
        arrays[f"in_{name}"] = value
        a[name] = nc.dram_tensor(f"in_{name}", value.shape, mybir.dt.from_np(value.dtype), kind="ExternalInput").ap()
    out = nc.dram_tensor("out", a["x"].shape, F32, kind="ExternalOutput").ap()
    program(nc, a, out)
    return run_bass_kernel_spmd(nc, [arrays], core_ids=[0]).results[0]["out"]
```
